# Optimizing a Trainium2 kernel written in Bass

```python
import numpy as np
import jax
import jax.numpy as jnp

def _softmax(x, axis=-1):
    return jax.nn.softmax(x, axis=axis)

def _gelu(x):
    return jax.nn.gelu(x, approximate=True)

def _silu(x):
    return jax.nn.silu(x)

def _sigmoid(x):
    return jax.nn.sigmoid(x)

def _layernorm(x, axis=-1, eps=1e-05):
    m = jnp.mean(x, axis=axis, keepdims=True)
    v = jnp.var(x, axis=axis, keepdims=True)
    return (x - m) / jnp.sqrt(v + eps)

def _scatter_add(tgt, idx, src, axis=0):
    return tgt.at[idx].add(src)

def _segment_sum(src, seg, n):
    return jax.ops.segment_sum(src, seg, n)
kernel_name = 'mk_flamingo_gated_d4_seqx_r8_f4e1b5'

def setup_inputs(seed: int=0):
    np.random.seed(seed)
    _w = jnp.asarray

    def _rec_inputs():
        import jax
        import jax.numpy as jnp
        _rk = jax.random.key(seed)
        x = -0.000125 + 0.9999 * jax.random.normal(jax.random.fold_in(_rk, 1), (128, 64, 128), jnp.float32)
        _lenS = 64 - jax.random.randint(jax.random.fold_in(_rk, 7), (128,), 0, max(1, 64 // 4) + 1, jnp.int32)
        _lenS2 = 64 - jax.random.randint(jax.random.fold_in(_rk, 8), (128,), 0, max(1, 64 // 4) + 1, jnp.int32)
        _ctx_1024P = jax.random.normal(jax.random.fold_in(_rk, 11), (128, 16, 128), jnp.float32)
        _ctx_1024c = jax.random.dirichlet(jax.random.fold_in(_rk, 511), 0.3 * jnp.ones((16,), jnp.float32), (128, 64))
        _ctx_1024t = jnp.einsum('bsk,bkd->bsd', _ctx_1024c, _ctx_1024P)
        _ctx_1024t = _ctx_1024t * jax.lax.rsqrt(jnp.mean(jnp.square(_ctx_1024t)) + 1e-12) * 0.953939
        ctx_1024 = -1.52775e-05 + 0.999936 * (_ctx_1024t + 0.3 * jax.random.normal(jax.random.fold_in(_rk, 611), (128, 64, 128), jnp.float32))
        _validS = jnp.arange(64)[None, :] < _lenS[:, None]
        _validS2 = jnp.arange(64)[None, :] < _lenS2[:, None]
        _causal = jnp.tril(jnp.ones((64, 64), dtype=bool))
        mask_1x1xSxS2_ik0 = jnp.where(jnp.broadcast_to(_validS2[0:1, None, None, :], (1, 1, 64, 64)), 0, 1).astype(jnp.int32)
        mask_BxS2_bf0 = jnp.logical_not(jnp.ones((128, 64), dtype=bool))
        _g = jax.random.normal(jax.random.fold_in(_rk, 9001), (2, 4), jnp.float32)
        _g = jnp.sign(_g) * jnp.maximum(jnp.abs(_g), 1.0) + (_g == 0) * 1.0
        g_xattn = _g[0]
        g_ffn = _g[1]
        return (x, ctx_1024, mask_1x1xSxS2_ik0, mask_BxS2_bf0, g_xattn, g_ffn)
    x, ctx_1024, mask_1x1xSxS2_ik0, mask_BxS2_bf0, g_xattn, g_ffn = _rec_inputs()

    def _L0_xattn_setup():
        import jax, jax.numpy as jnp
        import numpy as np
        DECAY = 0.9
        key = jax.random.key(seed)
        k1, k2, k3 = jax.random.split(key, 3)
        B, S, D = (8, 512, 128)
        q = jax.random.normal(k1, (B, S, D), dtype=jnp.float32)
        k = jax.random.normal(k2, (B, S, D), dtype=jnp.float32)
        v = jax.random.normal(k3, (B, S, D), dtype=jnp.float32)
        return {'q': q, 'k': k, 'v': v}
    _L0_xattn_all = _L0_xattn_setup()
    _L0_xattn_in = {k: v for k, v in _L0_xattn_all.items() if k in ()}
    del _L0_xattn_all

    def _L0_ffn_setup():
        import jax, jax.numpy as jnp
        import numpy as np
        D = 128
        H = 4
        HD = D // H
        E = 8
        FF = 512
        CAP_FACTOR = 1.0

        def _ln(x, g, b, eps=1e-05):
            mu = jnp.mean(x, -1, keepdims=True)
            v = jnp.mean((x - mu) ** 2, -1, keepdims=True)
            return (x - mu) * jax.lax.rsqrt(v + eps) * g + b

        def _mha(x, w, b, ow, ob):
            L, N, _ = x.shape
            qkv = x @ w.T + b
            q, k, v = jnp.split(qkv, 3, axis=-1)
            rh = lambda t: t.reshape(L, N, H, HD).transpose(1, 2, 0, 3)
            q, k, v = (rh(q), rh(k), rh(v))
            scores = jnp.einsum('nhld,nhmd->nhlm', q, k) / np.float32(np.sqrt(HD))
            attn = jax.nn.softmax(scores, axis=-1)
            o = jnp.einsum('nhlm,nhmd->nhld', attn, v).transpose(2, 0, 1, 3).reshape(L, N, D)
            return o @ ow.T + ob

        def _moe(x, wg, w1, b1, w2, b2):
            L, N, _ = x.shape
            S = L * N
            cap = int(CAP_FACTOR * S) // E
            xf = x.reshape(S, D)
            gates = jax.nn.softmax(xf @ wg, axis=-1)
            idx = jnp.argmax(gates, axis=-1)
            mask1 = jax.nn.one_hot(idx, E, dtype=x.dtype)
            loc = jnp.sum((jnp.cumsum(mask1, 0) - 1.0) * mask1, -1).astype(jnp.int32)
            keep = loc < cap
            gate_val = jnp.take_along_axis(gates, idx[:, None], -1)[:, 0]
            slot = jnp.where(keep, idx.astype(jnp.int32) * cap + loc, E * cap)
            disp = jnp.zeros((E * cap, D), x.dtype).at[slot].set(xf, mode='drop')
            disp = disp.reshape(E, cap, D)
            h = jnp.einsum('ecd,edf->ecf', disp, w1) + b1[:, None, :]
            y = (jnp.einsum('ecf,efd->ecd', h, w2) + b2[:, None, :]).reshape(E * cap, D)
            out = jnp.where(keep[:, None], gate_val[:, None] * y[jnp.minimum(slot, E * cap - 1)], 0.0)
            return out.reshape(L, N, D)
        key = jax.random.key(seed)
        ks = jax.random.split(key, 8)
        L, N = (128, 16)
        s = 0.02
        return {'x': jax.random.normal(ks[0], (L, N, D), jnp.float32), 'in_proj_w': jax.random.normal(ks[1], (3 * D, D), jnp.float32) * s, 'in_proj_b': jnp.zeros((3 * D,), jnp.float32), 'out_proj_w': jax.random.normal(ks[2], (D, D), jnp.float32) * s, 'out_proj_b': jnp.zeros((D,), jnp.float32), 'ln1_g': jnp.ones((D,), jnp.float32), 'ln1_b': jnp.zeros((D,), jnp.float32), 'ln2_g': jnp.ones((D,), jnp.float32), 'ln2_b': jnp.zeros((D,), jnp.float32), 'wg': jax.random.normal(ks[3], (D, E), jnp.float32) * s, 'w1': jax.random.normal(ks[4], (E, D, FF), jnp.float32) * s, 'b1': jnp.zeros((E, FF), jnp.float32), 'w2': jax.random.normal(ks[5], (E, FF, D), jnp.float32) * s, 'b2': jnp.zeros((E, D), jnp.float32)}
    _L0_ffn_all = _L0_ffn_setup()
    _L0_ffn_in = {k: v for k, v in _L0_ffn_all.items() if k in ('in_proj_w', 'in_proj_b', 'out_proj_w', 'out_proj_b', 'ln1_g', 'ln1_b', 'ln2_g', 'ln2_b', 'wg', 'w1', 'b1', 'w2', 'b2')}
    del _L0_ffn_all

    def _L1_xattn_setup():
        import jax, jax.numpy as jnp
        import numpy as np
        B, L_ENC, L_DEC, D = (16, 64, 128, 128)
        key = jax.random.key(seed)
        k1, k2, k3, k4, k5, k6 = jax.random.split(key, 6)
        encoder_hc = jax.random.normal(k1, (B, L_ENC, D), dtype=jnp.float32)
        decoder_hq = jax.random.normal(k2, (B, L_DEC, D), dtype=jnp.float32)
        w_sim = jax.random.normal(k3, (3 * D,), dtype=jnp.float32) * 0.02
        b_sim = jax.random.normal(k4, (1,), dtype=jnp.float32) * 0.02
        W_qv = jax.random.normal(k5, (4 * D, D), dtype=jnp.float32) * 0.02
        b_qv = jax.random.normal(k6, (D,), dtype=jnp.float32) * 0.02
        return {'encoder_hc': encoder_hc, 'decoder_hq': decoder_hq, 'w_sim': w_sim, 'b_sim': b_sim, 'W_qv': W_qv, 'b_qv': b_qv}
    _L1_xattn_all = _L1_xattn_setup()
    _L1_xattn_in = {k: v for k, v in _L1_xattn_all.items() if k in ('w_sim', 'b_sim', 'W_qv', 'b_qv')}
    del _L1_xattn_all

    def _L1_ffn_setup():
        import jax, jax.numpy as jnp
        import numpy as np
        TOPK = 4
        N_GROUPS = 4
        TOPK_GROUPS = 2
        ROUTE_SCALE = 2.5

        def _gate(x2, Wg):
            T = x2.shape[0]
            E = Wg.shape[0]
            scores = x2 @ Wg.T
            s = jax.nn.sigmoid(scores)
            g = s.reshape(T, N_GROUPS, E // N_GROUPS)
            group_scores = g.max(axis=-1)
            _, gidx = jax.lax.top_k(group_scores, TOPK_GROUPS)
            group_mask = jnp.any(jax.nn.one_hot(gidx, N_GROUPS, dtype=jnp.bool_), axis=1)
            masked = jnp.where(group_mask[:, :, None], g, -jnp.inf).reshape(T, E)
            _, idx = jax.lax.top_k(masked, TOPK)
            w = jnp.take_along_axis(s, idx, axis=1)
            w = w / jnp.sum(w, axis=-1, keepdims=True)
            w = w * ROUTE_SCALE
            return (w.astype(x2.dtype), idx)
        key = jax.random.key(seed)
        ks = jax.random.split(key, 6)
        B, S, D, I, E = (2, 256, 128, 128, 16)
        scale = 0.02
        return {'x': jax.random.normal(ks[0], (B, S, D), dtype=jnp.float32), 'Wg': jax.random.normal(ks[1], (E, D), dtype=jnp.float32) * scale, 'W1': jax.random.normal(ks[2], (E, I, D), dtype=jnp.float32) * scale, 'b1': jnp.zeros((E, I), dtype=jnp.float32), 'W2': jax.random.normal(ks[3], (E, D, I), dtype=jnp.float32) * scale, 'b2': jnp.zeros((E, D), dtype=jnp.float32), 'W3': jax.random.normal(ks[4], (E, I, D), dtype=jnp.float32) * scale, 'b3': jnp.zeros((E, I), dtype=jnp.float32)}
    _L1_ffn_all = _L1_ffn_setup()
    _L1_ffn_in = {k: v for k, v in _L1_ffn_all.items() if k in ('Wg', 'W1', 'b1', 'W2', 'b2', 'W3', 'b3')}
    del _L1_ffn_all

    def _L2_xattn_setup():
        import jax, jax.numpy as jnp
        import numpy as np
        D_MODEL = 128
        N_HEAD = 16
        BATCH = 4
        SEQ = 256
        key = jax.random.key(seed)
        ks = jax.random.split(key, 12)
        s = 1.0 / np.sqrt(D_MODEL)
        inp = {'q': jax.random.normal(ks[0], (BATCH, SEQ, D_MODEL), jnp.float32), 'k': jax.random.normal(ks[1], (BATCH, SEQ, D_MODEL), jnp.float32), 'v': jax.random.normal(ks[2], (BATCH, SEQ, D_MODEL), jnp.float32), 'mask': jnp.tril(jnp.ones((SEQ, SEQ), jnp.int32))[None, None, :, :], 'w_q': jax.random.normal(ks[3], (D_MODEL, D_MODEL), jnp.float32) * s, 'b_q': jax.random.normal(ks[4], (D_MODEL,), jnp.float32) * s, 'w_k': jax.random.normal(ks[5], (D_MODEL, D_MODEL), jnp.float32) * s, 'b_k': jax.random.normal(ks[6], (D_MODEL,), jnp.float32) * s, 'w_v': jax.random.normal(ks[7], (D_MODEL, D_MODEL), jnp.float32) * s, 'b_v': jax.random.normal(ks[8], (D_MODEL,), jnp.float32) * s, 'w_o': jax.random.normal(ks[9], (D_MODEL, D_MODEL), jnp.float32) * s, 'b_o': jax.random.normal(ks[10], (D_MODEL,), jnp.float32) * s}
        return inp
    _L2_xattn_all = _L2_xattn_setup()
    _L2_xattn_in = {k: v for k, v in _L2_xattn_all.items() if k in ('w_q', 'b_q', 'w_k', 'b_k', 'w_v', 'b_v', 'w_o', 'b_o')}
    del _L2_xattn_all

    def _L2_ffn_setup():
        import jax, jax.numpy as jnp
        import numpy as np
        E = 8
        K = 2
        D = 128
        H = 4 * D
        EPS = 1e-05
        TEMP = 1.5
        key = jax.random.key(seed)
        ks = jax.random.split(key, 6)
        B, T = (2, 256)
        x = jax.random.normal(ks[0], (B, T, D), dtype=jnp.float32)
        gamma = jnp.ones((D,), dtype=jnp.float32)
        beta = jnp.zeros((D,), dtype=jnp.float32)
        router_w = jax.random.normal(ks[1], (E, D), dtype=jnp.float32) * 0.02
        W1 = jax.random.normal(ks[2], (E, D, H), dtype=jnp.float32) * 0.02
        W2 = jax.random.normal(ks[3], (E, H, D), dtype=jnp.float32) * 0.02
        return {'x': x, 'gamma': gamma, 'beta': beta, 'router_w': router_w, 'W1': W1, 'W2': W2}
    _L2_ffn_all = _L2_ffn_setup()
    _L2_ffn_in = {k: v for k, v in _L2_ffn_all.items() if k in ('gamma', 'beta', 'router_w', 'W1', 'W2')}
    del _L2_ffn_all

    def _L3_xattn_setup():
        import jax, jax.numpy as jnp
        import numpy as np
        D = 128
        H = 16
        HD = D // H
        DFF = 4 * D
        EPS = 1e-05

        def _layernorm(x, g, b):
            mu = jnp.mean(x, axis=-1, keepdims=True)
            var = jnp.var(x, axis=-1, keepdims=True)
            return (x - mu) * jax.lax.rsqrt(var + EPS) * g + b
        key = jax.random.key(seed)
        ks = jax.random.split(key, 16)
        B, SQ, SK = (4, 128, 256)
        s = 1.0 / np.sqrt(D)
        inp = {'query': jax.random.normal(ks[0], (B, SQ, D), jnp.float32), 'key_value': jax.random.normal(ks[1], (B, SK, D), jnp.float32), 'key_padding_mask': jnp.zeros((B, SK), jnp.bool_), 'Wq': jax.random.normal(ks[2], (D, D), jnp.float32) * s, 'bq': jnp.zeros((D,), jnp.float32), 'Wk': jax.random.normal(ks[3], (D, D), jnp.float32) * s, 'bk': jnp.zeros((D,), jnp.float32), 'Wv': jax.random.normal(ks[4], (D, D), jnp.float32) * s, 'bv': jnp.zeros((D,), jnp.float32), 'Wo': jax.random.normal(ks[5], (D, D), jnp.float32) * s, 'bo': jnp.zeros((D,), jnp.float32), 'ln1_g': jnp.ones((D,), jnp.float32), 'ln1_b': jnp.zeros((D,), jnp.float32), 'W1': jax.random.normal(ks[6], (D, DFF), jnp.float32) * s, 'b1': jnp.zeros((DFF,), jnp.float32), 'W2': jax.random.normal(ks[7], (DFF, D), jnp.float32) * (1.0 / np.sqrt(DFF)), 'b2': jnp.zeros((D,), jnp.float32), 'ln2_g': jnp.ones((D,), jnp.float32), 'ln2_b': jnp.zeros((D,), jnp.float32)}
        return inp
    _L3_xattn_all = _L3_xattn_setup()
    _L3_xattn_in = {k: v for k, v in _L3_xattn_all.items() if k in ('Wq', 'bq', 'Wk', 'bk', 'Wv', 'bv', 'Wo', 'bo', 'ln1_g', 'ln1_b', 'W1', 'b1', 'W2', 'b2', 'ln2_g', 'ln2_b')}
    del _L3_xattn_all

    def _L3_ffn_setup():
        import jax, jax.numpy as jnp
        import numpy as np
        D_MODEL = 128
        DEPTH = 8
        M = 2 ** DEPTH
        N_INTERNAL = M - 1
        B, T = (8, 512)

        def _leaf_probs(gate):
            BT = gate.shape[0]
            lp = jnp.ones((BT, M), dtype=gate.dtype)
            for level in range(DEPTH):
                n = 2 ** level
                half = M // (2 * n)
                g = gate[:, n - 1:2 * n - 1]
                f = jnp.stack([1.0 - g, g], axis=-1)
                f = jnp.broadcast_to(f[..., None], (BT, n, 2, half))
                lp = lp * f.reshape(BT, M)
            return lp
        key = jax.random.key(seed)
        ks = jax.random.split(key, 7)
        x = jax.random.normal(ks[0], (B, T, D_MODEL), dtype=jnp.float32)
        Wq = jax.random.normal(ks[1], (D_MODEL, D_MODEL), dtype=jnp.float32) * 0.02
        routers = jax.random.normal(ks[2], (N_INTERNAL, D_MODEL), dtype=jnp.float32) * 0.02
        leaf_keys = jax.random.normal(ks[3], (M, D_MODEL), dtype=jnp.float32) * 0.02
        leaf_values = jax.random.normal(ks[4], (M, D_MODEL), dtype=jnp.float32) * 0.02
        Wout_w = jax.random.normal(ks[5], (D_MODEL, D_MODEL), dtype=jnp.float32) * 0.02
        Wout_b = jax.random.normal(ks[6], (D_MODEL,), dtype=jnp.float32) * 0.02
        return {'x': x, 'Wq': Wq, 'routers': routers, 'leaf_keys': leaf_keys, 'leaf_values': leaf_values, 'Wout_w': Wout_w, 'Wout_b': Wout_b}
    _L3_ffn_all = _L3_ffn_setup()
    _L3_ffn_in = {k: v for k, v in _L3_ffn_all.items() if k in ('Wq', 'routers', 'leaf_keys', 'leaf_values', 'Wout_w', 'Wout_b')}
    del _L3_ffn_all
    return {'x': x, 'ctx_1024': ctx_1024, 'mask_1x1xSxS2_ik0': mask_1x1xSxS2_ik0, 'mask_BxS2_bf0': mask_BxS2_bf0, 'g_xattn': g_xattn, 'g_ffn': g_ffn, 'L0_ffn_in_proj_w': _L0_ffn_in['in_proj_w'], 'L0_ffn_in_proj_b': _L0_ffn_in['in_proj_b'], 'L0_ffn_out_proj_w': _L0_ffn_in['out_proj_w'], 'L0_ffn_out_proj_b': _L0_ffn_in['out_proj_b'], 'L0_ffn_ln1_g': _L0_ffn_in['ln1_g'], 'L0_ffn_ln1_b': _L0_ffn_in['ln1_b'], 'L0_ffn_ln2_g': _L0_ffn_in['ln2_g'], 'L0_ffn_ln2_b': _L0_ffn_in['ln2_b'], 'L0_ffn_wg': _L0_ffn_in['wg'], 'L0_ffn_w1': _L0_ffn_in['w1'], 'L0_ffn_b1': _L0_ffn_in['b1'], 'L0_ffn_w2': _L0_ffn_in['w2'], 'L0_ffn_b2': _L0_ffn_in['b2'], 'L1_xattn_w_sim': _L1_xattn_in['w_sim'], 'L1_xattn_b_sim': _L1_xattn_in['b_sim'], 'L1_xattn_W_qv': _L1_xattn_in['W_qv'], 'L1_xattn_b_qv': _L1_xattn_in['b_qv'], 'L1_ffn_Wg': _L1_ffn_in['Wg'], 'L1_ffn_W1': _L1_ffn_in['W1'], 'L1_ffn_b1': _L1_ffn_in['b1'], 'L1_ffn_W2': _L1_ffn_in['W2'], 'L1_ffn_b2': _L1_ffn_in['b2'], 'L1_ffn_W3': _L1_ffn_in['W3'], 'L1_ffn_b3': _L1_ffn_in['b3'], 'L2_xattn_w_q': _L2_xattn_in['w_q'], 'L2_xattn_b_q': _L2_xattn_in['b_q'], 'L2_xattn_w_k': _L2_xattn_in['w_k'], 'L2_xattn_b_k': _L2_xattn_in['b_k'], 'L2_xattn_w_v': _L2_xattn_in['w_v'], 'L2_xattn_b_v': _L2_xattn_in['b_v'], 'L2_xattn_w_o': _L2_xattn_in['w_o'], 'L2_xattn_b_o': _L2_xattn_in['b_o'], 'L2_ffn_gamma': _L2_ffn_in['gamma'], 'L2_ffn_beta': _L2_ffn_in['beta'], 'L2_ffn_router_w': _L2_ffn_in['router_w'], 'L2_ffn_W1': _L2_ffn_in['W1'], 'L2_ffn_W2': _L2_ffn_in['W2'], 'L3_xattn_Wq': _L3_xattn_in['Wq'], 'L3_xattn_bq': _L3_xattn_in['bq'], 'L3_xattn_Wk': _L3_xattn_in['Wk'], 'L3_xattn_bk': _L3_xattn_in['bk'], 'L3_xattn_Wv': _L3_xattn_in['Wv'], 'L3_xattn_bv': _L3_xattn_in['bv'], 'L3_xattn_Wo': _L3_xattn_in['Wo'], 'L3_xattn_bo': _L3_xattn_in['bo'], 'L3_xattn_ln1_g': _L3_xattn_in['ln1_g'], 'L3_xattn_ln1_b': _L3_xattn_in['ln1_b'], 'L3_xattn_W1': _L3_xattn_in['W1'], 'L3_xattn_b1': _L3_xattn_in['b1'], 'L3_xattn_W2': _L3_xattn_in['W2'], 'L3_xattn_b2': _L3_xattn_in['b2'], 'L3_xattn_ln2_g': _L3_xattn_in['ln2_g'], 'L3_xattn_ln2_b': _L3_xattn_in['ln2_b'], 'L3_ffn_Wq': _L3_ffn_in['Wq'], 'L3_ffn_routers': _L3_ffn_in['routers'], 'L3_ffn_leaf_keys': _L3_ffn_in['leaf_keys'], 'L3_ffn_leaf_values': _L3_ffn_in['leaf_values'], 'L3_ffn_Wout_w': _L3_ffn_in['Wout_w'], 'L3_ffn_Wout_b': _L3_ffn_in['Wout_b']}

def reference(x, ctx_1024, mask_1x1xSxS2_ik0, mask_BxS2_bf0, g_xattn, g_ffn, L0_ffn_in_proj_w, L0_ffn_in_proj_b, L0_ffn_out_proj_w, L0_ffn_out_proj_b, L0_ffn_ln1_g, L0_ffn_ln1_b, L0_ffn_ln2_g, L0_ffn_ln2_b, L0_ffn_wg, L0_ffn_w1, L0_ffn_b1, L0_ffn_w2, L0_ffn_b2, L1_xattn_w_sim, L1_xattn_b_sim, L1_xattn_W_qv, L1_xattn_b_qv, L1_ffn_Wg, L1_ffn_W1, L1_ffn_b1, L1_ffn_W2, L1_ffn_b2, L1_ffn_W3, L1_ffn_b3, L2_xattn_w_q, L2_xattn_b_q, L2_xattn_w_k, L2_xattn_b_k, L2_xattn_w_v, L2_xattn_b_v, L2_xattn_w_o, L2_xattn_b_o, L2_ffn_gamma, L2_ffn_beta, L2_ffn_router_w, L2_ffn_W1, L2_ffn_W2, L3_xattn_Wq, L3_xattn_bq, L3_xattn_Wk, L3_xattn_bk, L3_xattn_Wv, L3_xattn_bv, L3_xattn_Wo, L3_xattn_bo, L3_xattn_ln1_g, L3_xattn_ln1_b, L3_xattn_W1, L3_xattn_b1, L3_xattn_W2, L3_xattn_b2, L3_xattn_ln2_g, L3_xattn_ln2_b, L3_ffn_Wq, L3_ffn_routers, L3_ffn_leaf_keys, L3_ffn_leaf_values, L3_ffn_Wout_w, L3_ffn_Wout_b):
    import jax
    import jax.numpy as jnp

    def _L0_xattn_ref(q, k, v):
        import jax, jax.numpy as jnp
        import numpy as np
        DECAY = 0.9
        kv = jnp.swapaxes(k * v, 0, 1)

        def step(r, kv_t):
            r = DECAY * r + kv_t
            return (r, r)
        r0 = jnp.zeros(q.shape[:1] + q.shape[2:], dtype=q.dtype)
        _, rs = jax.lax.scan(step, r0, kv)
        return q * jnp.swapaxes(rs, 0, 1)

    def _L0_ffn_ref(x, in_proj_w, in_proj_b, out_proj_w, out_proj_b, ln1_g, ln1_b, ln2_g, ln2_b, wg, w1, b1, w2, b2):
        import jax, jax.numpy as jnp
        import numpy as np
        D = 128
        H = 4
        HD = D // H
        E = 8
        FF = 512
        CAP_FACTOR = 1.0

        def _ln(x, g, b, eps=1e-05):
            mu = jnp.mean(x, -1, keepdims=True)
            v = jnp.mean((x - mu) ** 2, -1, keepdims=True)
            return (x - mu) * jax.lax.rsqrt(v + eps) * g + b

        def _mha(x, w, b, ow, ob):
            L, N, _ = x.shape
            qkv = x @ w.T + b
            q, k, v = jnp.split(qkv, 3, axis=-1)
            rh = lambda t: t.reshape(L, N, H, HD).transpose(1, 2, 0, 3)
            q, k, v = (rh(q), rh(k), rh(v))
            scores = jnp.einsum('nhld,nhmd->nhlm', q, k) / np.float32(np.sqrt(HD))
            attn = jax.nn.softmax(scores, axis=-1)
            o = jnp.einsum('nhlm,nhmd->nhld', attn, v).transpose(2, 0, 1, 3).reshape(L, N, D)
            return o @ ow.T + ob

        def _moe(x, wg, w1, b1, w2, b2):
            L, N, _ = x.shape
            S = L * N
            cap = int(CAP_FACTOR * S) // E
            xf = x.reshape(S, D)
            gates = jax.nn.softmax(xf @ wg, axis=-1)
            idx = jnp.argmax(gates, axis=-1)
            mask1 = jax.nn.one_hot(idx, E, dtype=x.dtype)
            loc = jnp.sum((jnp.cumsum(mask1, 0) - 1.0) * mask1, -1).astype(jnp.int32)
            keep = loc < cap
            gate_val = jnp.take_along_axis(gates, idx[:, None], -1)[:, 0]
            slot = jnp.where(keep, idx.astype(jnp.int32) * cap + loc, E * cap)
            disp = jnp.zeros((E * cap, D), x.dtype).at[slot].set(xf, mode='drop')
            disp = disp.reshape(E, cap, D)
            h = jnp.einsum('ecd,edf->ecf', disp, w1) + b1[:, None, :]
            y = (jnp.einsum('ecf,efd->ecd', h, w2) + b2[:, None, :]).reshape(E * cap, D)
            out = jnp.where(keep[:, None], gate_val[:, None] * y[jnp.minimum(slot, E * cap - 1)], 0.0)
            return out.reshape(L, N, D)
        y1 = _ln(x + _mha(x, in_proj_w, in_proj_b, out_proj_w, out_proj_b), ln1_g, ln1_b)
        y2 = _ln(y1 + _moe(y1, wg, w1, b1, w2, b2), ln2_g, ln2_b)
        return y2

    def _L1_xattn_ref(encoder_hc, decoder_hq, w_sim, b_sim, W_qv, b_qv):
        import jax, jax.numpy as jnp
        import numpy as np
        B, L_ENC, L_DEC, D = (16, 64, 128, 128)
        d = encoder_hc.shape[-1]
        w1, w2, w3 = (w_sim[:d], w_sim[d:2 * d], w_sim[2 * d:])
        Sim = (encoder_hc @ w1)[:, :, None] + (decoder_hq @ w2)[:, None, :] + jnp.einsum('bid,bjd->bij', encoder_hc * w3, decoder_hq) + b_sim[0]
        A = jax.nn.softmax(Sim, axis=2)
        hq_hat = jnp.einsum('bij,bjd->bid', A, decoder_hq)
        Batt = jax.nn.softmax(jnp.max(Sim, axis=2), axis=1)
        hc_bar = jnp.einsum('bi,bid->bd', Batt, encoder_hc)[:, None, :]
        hc_hat = jnp.broadcast_to(hc_bar, encoder_hc.shape)
        feats = jnp.concatenate([encoder_hc, hq_hat, encoder_hc * hq_hat, encoder_hc * hc_hat], axis=-1)
        hcq = feats @ W_qv + b_qv
        return hcq

    def _L1_ffn_ref(x, Wg, W1, b1, W2, b2, W3, b3):
        import jax, jax.numpy as jnp
        import numpy as np
        TOPK = 4
        N_GROUPS = 4
        TOPK_GROUPS = 2
        ROUTE_SCALE = 2.5

        def _gate(x2, Wg):
            T = x2.shape[0]
            E = Wg.shape[0]
            scores = x2 @ Wg.T
            s = jax.nn.sigmoid(scores)
            g = s.reshape(T, N_GROUPS, E // N_GROUPS)
            group_scores = g.max(axis=-1)
            _, gidx = jax.lax.top_k(group_scores, TOPK_GROUPS)
            group_mask = jnp.any(jax.nn.one_hot(gidx, N_GROUPS, dtype=jnp.bool_), axis=1)
            masked = jnp.where(group_mask[:, :, None], g, -jnp.inf).reshape(T, E)
            _, idx = jax.lax.top_k(masked, TOPK)
            w = jnp.take_along_axis(s, idx, axis=1)
            w = w / jnp.sum(w, axis=-1, keepdims=True)
            w = w * ROUTE_SCALE
            return (w.astype(x2.dtype), idx)
        shape = x.shape
        D = shape[-1]
        x2 = x.reshape(-1, D)
        weights, indices = _gate(x2, Wg)
        E = Wg.shape[0]
        y = jnp.zeros_like(x2)
        for e in range(E):
            we = jnp.sum(weights * (indices == e), axis=-1)
            h = jax.nn.silu(x2 @ W1[e].T + b1[e]) * (x2 @ W3[e].T + b3[e])
            y = y + (h @ W2[e].T + b2[e]) * we[:, None]
        return y.reshape(shape)

    def _L2_xattn_ref(q, k, v, mask, w_q, b_q, w_k, b_k, w_v, b_v, w_o, b_o):
        import jax, jax.numpy as jnp
        import numpy as np
        D_MODEL = 128
        N_HEAD = 16
        BATCH = 4
        SEQ = 256
        batch, q_len, d_model = q.shape
        k_len = k.shape[1]
        n_d = d_model // N_HEAD
        qh = (q @ w_q.T + b_q).reshape(batch, q_len, N_HEAD, n_d).transpose(0, 2, 1, 3)
        kh = (k @ w_k.T + b_k).reshape(batch, k_len, N_HEAD, n_d).transpose(0, 2, 1, 3)
        vh = (v @ w_v.T + b_v).reshape(batch, k_len, N_HEAD, n_d).transpose(0, 2, 1, 3)
        score = jnp.einsum('bhqd,bhkd->bhqk', qh, kh) / jnp.sqrt(jnp.float32(n_d))
        score = jnp.where(mask == 0, jnp.float32(-1000000000.0), score)
        attn = jax.nn.softmax(score, axis=-1)
        out = jnp.einsum('bhqk,bhkd->bhqd', attn, vh)
        out = out.transpose(0, 2, 1, 3).reshape(batch, q_len, d_model)
        return out @ w_o.T + b_o

    def _L2_ffn_ref(x, gamma, beta, router_w, W1, W2):
        import jax, jax.numpy as jnp
        import numpy as np
        E = 8
        K = 2
        D = 128
        H = 4 * D
        EPS = 1e-05
        TEMP = 1.5
        res = x
        mu = jnp.mean(x, axis=-1, keepdims=True)
        var = jnp.mean(jnp.square(x - mu), axis=-1, keepdims=True)
        xn = (x - mu) * jax.lax.rsqrt(var + EPS) * gamma + beta
        logits = jnp.einsum('btd,ed->bte', xn, router_w)
        probs = jax.nn.softmax(logits / TEMP, axis=-1)
        w, idx = jax.lax.top_k(probs, K)
        wdense = jnp.sum(jax.nn.one_hot(idx, E, dtype=w.dtype) * w[..., None], axis=-2)
        h = jax.nn.silu(jnp.einsum('btd,edf->betf', xn, W1))
        y = jnp.einsum('betf,efd->betd', h, W2)
        out = jnp.einsum('bte,betd->btd', wdense, y)
        return out + res

    def _L3_xattn_ref(query, key_value, key_padding_mask, Wq, bq, Wk, bk, Wv, bv, Wo, bo, ln1_g, ln1_b, W1, b1, W2, b2, ln2_g, ln2_b):
        import jax, jax.numpy as jnp
        import numpy as np
        D = 128
        H = 16
        HD = D // H
        DFF = 4 * D
        EPS = 1e-05

        def _layernorm(x, g, b):
            mu = jnp.mean(x, axis=-1, keepdims=True)
            var = jnp.var(x, axis=-1, keepdims=True)
            return (x - mu) * jax.lax.rsqrt(var + EPS) * g + b
        B, SQ, _ = query.shape
        SK = key_value.shape[1]
        scale = HD ** (-0.5)
        q = (query @ Wq + bq).reshape(B, SQ, H, HD).transpose(0, 2, 1, 3)
        k = (key_value @ Wk + bk).reshape(B, SK, H, HD).transpose(0, 2, 1, 3)
        v = (key_value @ Wv + bv).reshape(B, SK, H, HD).transpose(0, 2, 1, 3)
        scores = jnp.einsum('bhqd,bhkd->bhqk', q, k) * scale
        scores = jnp.where(key_padding_mask[:, None, None, :], -jnp.inf, scores)
        attn = jax.nn.softmax(scores, axis=-1)
        attn_out = jnp.einsum('bhqk,bhkd->bhqd', attn, v)
        attn_out = attn_out.transpose(0, 2, 1, 3).reshape(B, SQ, D)
        attn_out = attn_out @ Wo + bo
        x = _layernorm(query + attn_out, ln1_g, ln1_b)
        ffn = jax.nn.gelu(x @ W1 + b1, approximate=False) @ W2 + b2
        return _layernorm(x + ffn, ln2_g, ln2_b)

    def _L3_ffn_ref(x, Wq, routers, leaf_keys, leaf_values, Wout_w, Wout_b):
        import jax, jax.numpy as jnp
        import numpy as np
        D_MODEL = 128
        DEPTH = 8
        M = 2 ** DEPTH
        N_INTERNAL = M - 1
        B, T = (8, 512)

        def _leaf_probs(gate):
            BT = gate.shape[0]
            lp = jnp.ones((BT, M), dtype=gate.dtype)
            for level in range(DEPTH):
                n = 2 ** level
                half = M // (2 * n)
                g = gate[:, n - 1:2 * n - 1]
                f = jnp.stack([1.0 - g, g], axis=-1)
                f = jnp.broadcast_to(f[..., None], (BT, n, 2, half))
                lp = lp * f.reshape(BT, M)
            return lp
        Bv, Tv, d = x.shape
        q = jnp.einsum('btd,ed->bte', x, Wq)
        q_flat = q.reshape(Bv * Tv, d)
        gate = jax.nn.sigmoid(q_flat @ routers.T)
        leaf_prob = _leaf_probs(gate)
        ret = (leaf_prob @ leaf_values).reshape(Bv, Tv, d)
        return jnp.einsum('btd,ed->bte', ret, Wout_w) + Wout_b
    x = x + jnp.tanh(g_xattn[0]) * _L0_xattn_ref(_layernorm(x, axis=-1), ctx_1024, ctx_1024)
    x = x + jnp.tanh(g_ffn[0]) * _L0_ffn_ref(_layernorm(x, axis=-1), L0_ffn_in_proj_w, L0_ffn_in_proj_b, L0_ffn_out_proj_w, L0_ffn_out_proj_b, L0_ffn_ln1_g, L0_ffn_ln1_b, L0_ffn_ln2_g, L0_ffn_ln2_b, L0_ffn_wg, L0_ffn_w1, L0_ffn_b1, L0_ffn_w2, L0_ffn_b2)
    x = x + jnp.tanh(g_xattn[1]) * _L1_xattn_ref(_layernorm(x, axis=-1), ctx_1024, L1_xattn_w_sim, L1_xattn_b_sim, L1_xattn_W_qv, L1_xattn_b_qv)
    x = x + jnp.tanh(g_ffn[1]) * _L1_ffn_ref(_layernorm(x, axis=-1), L1_ffn_Wg, L1_ffn_W1, L1_ffn_b1, L1_ffn_W2, L1_ffn_b2, L1_ffn_W3, L1_ffn_b3)
    x = x + jnp.tanh(g_xattn[2]) * _L2_xattn_ref(_layernorm(x, axis=-1), ctx_1024, ctx_1024, mask_1x1xSxS2_ik0, L2_xattn_w_q, L2_xattn_b_q, L2_xattn_w_k, L2_xattn_b_k, L2_xattn_w_v, L2_xattn_b_v, L2_xattn_w_o, L2_xattn_b_o)
    x = x + jnp.tanh(g_ffn[2]) * _L2_ffn_ref(_layernorm(x, axis=-1), L2_ffn_gamma, L2_ffn_beta, L2_ffn_router_w, L2_ffn_W1, L2_ffn_W2)
    x = x + jnp.tanh(g_xattn[3]) * _L3_xattn_ref(_layernorm(x, axis=-1), ctx_1024, mask_BxS2_bf0, L3_xattn_Wq, L3_xattn_bq, L3_xattn_Wk, L3_xattn_bk, L3_xattn_Wv, L3_xattn_bv, L3_xattn_Wo, L3_xattn_bo, L3_xattn_ln1_g, L3_xattn_ln1_b, L3_xattn_W1, L3_xattn_b1, L3_xattn_W2, L3_xattn_b2, L3_xattn_ln2_g, L3_xattn_ln2_b)
    x = x + jnp.tanh(g_ffn[3]) * _L3_ffn_ref(_layernorm(x, axis=-1), L3_ffn_Wq, L3_ffn_routers, L3_ffn_leaf_keys, L3_ffn_leaf_values, L3_ffn_Wout_w, L3_ffn_Wout_b)
    return x

_drawn_inputs = setup_inputs


def setup_inputs(seed=0):
    import zlib

    import numpy as np

    out = dict(_drawn_inputs(seed))
    spreads = {'L0_ffn_in_proj_b': (0.0, 0.8),
     'L0_ffn_out_proj_b': (0.0, 0.776),
     'L0_ffn_ln1_g': (1.0, 0.6),
     'L0_ffn_ln1_b': (0.0, 0.8),
     'L0_ffn_ln2_g': (1.0, 0.6),
     'L0_ffn_ln2_b': (0.0, 0.8),
     'L0_ffn_b1': (0.0, 0.8),
     'L0_ffn_b2': (0.0, 0.8),
     'L1_ffn_b1': (0.0, 0.8),
     'L1_ffn_b2': (0.0, 0.581),
     'L1_ffn_b3': (0.0, 0.8),
     'L2_ffn_gamma': (1.0, 0.6),
     'L2_ffn_beta': (0.0, 0.8),
     'L3_xattn_bq': (0.0, 2.0),
     'L3_xattn_bk': (0.0, 2.0),
     'L3_xattn_bv': (0.0, 2.0),
     'L3_xattn_bo': (0.0, 0.767),
     'L3_xattn_ln1_g': (1.0, 0.6),
     'L3_xattn_ln1_b': (0.0, 0.779),
     'L3_xattn_b1': (0.0, 2.0),
     'L3_xattn_b2': (0.0, 2.0),
     'L3_xattn_ln2_g': (1.0, 0.6),
     'L3_xattn_ln2_b': (0.0, 0.62)}
    factors = {'g_ffn': 8.0,
     'L0_ffn_in_proj_w': 8.0,
     'L0_ffn_out_proj_w': 8.0,
     'L0_ffn_wg': 8.0,
     'L0_ffn_w1': 8.0,
     'L0_ffn_w2': 8.0,
     'L1_xattn_w_sim': 8.0,
     'L1_xattn_b_qv': 8.0,
     'L1_ffn_Wg': 4.665,
     'L1_ffn_W1': 8.0,
     'L1_ffn_W2': 8.0,
     'L1_ffn_W3': 8.0,
     'L2_xattn_b_q': 8.0,
     'L2_xattn_b_k': 64.0,
     'L2_xattn_b_v': 6.02,
     'L2_xattn_b_o': 6.075,
     'L2_ffn_router_w': 8.0,
     'L2_ffn_W1': 8.0,
     'L2_ffn_W2': 8.0,
     'L3_ffn_Wq': 43.636,
     'L3_ffn_routers': 43.952,
     'L3_ffn_leaf_values': 42.514,
     'L3_ffn_Wout_w': 42.22,
     'L3_ffn_Wout_b': 27.941,
     'L3_xattn_Wq': 5.619,
     'L3_xattn_Wk': 4.458}
    for name, (base, spread) in spreads.items():
        noise = np.random.default_rng([zlib.crc32(name.encode()), seed]).standard_normal(out[name].shape)
        drawn = base * np.exp(spread * noise) if base else spread * noise
        out[name] = jnp.asarray(drawn.astype(out[name].dtype))
    for name, factor in factors.items():
        out[name] = (out[name] * factor).astype(out[name].dtype)
    return out
```

```python
from contextlib import ExitStack

import numpy as np

import concourse.bass as bass
from concourse import mybir

F32 = mybir.dt.float32
U8 = mybir.dt.uint8
I32 = mybir.dt.int32
ALU = mybir.AluOpType
ACT = mybir.ActivationFunctionType
AX = mybir.AxisListType

P = 128
B, S, D = 128, 64, 128
TOKENS = B * S
TILES = TOKENS // P
G = 4
GROUPS = TILES // G
N = G * P
BG = N // S
LN_EPS = 1e-5
DMA = 16

DECAY = 0.9
L0_HEADS, L0_HD = 4, 32
L0_E, L0_FF = 8, 512
L0_CAP = TOKENS // L0_E
L1_E, L1_GROUPS, L1_TOPK, L1_TOPG, ROUTE_SCALE = 16, 4, 4, 2, 2.5
HEADS, HD = 16, 8
L2_E, L2_H, L2_TEMP = 8, 512, 1.5
FFN = 512
LEAVES = 256
BIG = 3.4028234e38


def reuse(eng, sem, value):
    if not (isinstance(value, int) and value <= 0):
        eng.wait_ge(sem, value)


def wait_apart(eng, sem, value, passed):
    eng.wait_ge(sem, value)
    eng.sem_inc(passed, 1)


def over_groups(front, main, eng):
    front(0, 0)
    main(0, 0, lambda *parts: front(1, 1, *parts))
    main(1, 1, lambda *parts: front(2, 0, *parts))
    with eng.Fori(1, GROUPS // 2 - 1) as pair:
        main(pair * 2, 0, lambda *parts: front(pair * 2 + 1, 1, *parts))
        main(pair * 2 + 1, 1, lambda *parts: front(pair * 2 + 2, 0, *parts))
    main(GROUPS - 2, 0, lambda *parts: front(GROUPS - 1, 1, *parts))
    main(GROUPS - 1, 1, lambda *parts: None)


def loads(i, h, count=1):
    return (i - h) * (count * DMA // 2) + count * DMA


def each_group(step, eng):
    step(0, 0)
    step(1, 1)
    with eng.Fori(1, GROUPS // 2) as pair:
        step(pair * 2, 0)
        step(pair * 2 + 1, 1)


class Chip:

    def __init__(self, nc, ctx, dram):
        self.nc, self.dram = nc, dram
        self.x_all = ctx.enter_context(nc.sbuf_tensor("x_all", [P, TILES, D], F32))
        self.ident = ctx.enter_context(nc.sbuf_tensor("ident", [P, P], F32))
        self.tanh_g = ctx.enter_context(nc.sbuf_tensor("tanh_g", [P, 8], F32))
        self.neg_half = ctx.enter_context(nc.sbuf_tensor("neg_half", [P, G], F32))
        self.passed = {e: ctx.enter_context(nc.semaphore(f"passed_{e}")) for e in ("v", "pool", "act", "pe")}
        self.bank = [ctx.enter_context(nc.psum_tensor(f"bank{k}", [P, 512], F32)) for k in range(8)]


class Phase:

    def __init__(self, chip, name):
        self.chip, self.nc, self.name = chip, chip.nc, name
        self.ctx, self.sems = ExitStack(), []

    def __enter__(self):
        return self

    def __exit__(self, *failure):
        self.ctx.close()
        if failure[0] is None:
            self.nc.clear_and_free_semaphores(self.sems)
            self.nc.all_engine_barrier()

    def sem(self, what):
        self.sems.append(self.nc.alloc_semaphore(f"{self.name}_{what}"))
        return self.sems[-1]

    def sb(self, what, shape, dt=F32):
        return self.ctx.enter_context(self.nc.sbuf_tensor(f"{self.name}_{what}", shape, dt))


class LayerNorm:

    def __init__(self, ph, what):
        self.chip = ph.chip
        self.stats = ph.sb(f"{what}_stats", [P, G, 6])
        self.mv = ph.sb(f"{what}_mv", [P, G, 2])
        self.var_eps = ph.sb(f"{what}_var_eps", [P, G])
        self.rstd = ph.sb(f"{what}_rstd", [P, G])
        self.stats_done = ph.sem(f"{what}_stats")
        self.var_done = ph.sem(f"{what}_var")
        self.eps_added = ph.sem(f"{what}_eps")
        self.rstd_done = ph.sem(f"{what}_rstd")

    def vector_stats(self, v, i, tile):
        for t in range(G):
            v.bn_stats(self.stats[:, t, :], tile(t)).then_inc(self.stats_done, 1)
        wait_apart(v, self.stats_done, i * G + G, self.chip.passed["v"])
        for t in range(G):
            v.bn_aggr(self.mv[:, t, :], self.stats[:, t, :]).then_inc(self.var_done, 1)

    def pool_rstd(self, pool, i):
        wait_apart(pool, self.var_done, i * G + G, self.chip.passed["pool"])
        pool.tensor_scalar(self.var_eps[:, :], self.mv[:, :, 1], LN_EPS, None, ALU.add).then_inc(self.eps_added, 1)
        pool.wait_ge(self.eps_added, i + 1)
        pool.tensor_tensor(self.rstd[:, :], self.var_eps[:, :], self.chip.neg_half[:, :], ALU.pow)\
            .then_inc(self.rstd_done, 1)

    def vector_apply(self, v, i, tile, out, done):
        v.wait_ge(self.rstd_done, i + 1)
        for t in range(G):
            v.tensor_scalar(out[:, t, :], tile(t), self.mv[:, t, 0:1], self.rstd[:, t:t + 1],
                            ALU.subtract, ALU.mult).then_inc(done, 1)


def group_of(tensor, i):
    return tensor[:, bass.ds(i * G, G), :]


def tile_of(tensor, i, t):
    return tensor[:, bass.ds(i * G + t, 1), :].rearrange("p a d -> p (a d)")


def transposes(pe, bank, tiles, ident):
    for t, src in enumerate(tiles):
        done = pe.transpose(bank[:, t * P:(t + 1) * P], src, ident[:, :])
    return done


def constants(chip):
    nc, dram = chip.nc, chip.dram
    with Phase(chip, "const") as ph:
        loaded, gates, filled = ph.sem("loaded"), ph.sem("gates"), ph.sem("filled")
        g_raw = ph.sb("g_raw", [P, 8])
        with nc.Block() as block:
            @block.sync
            def _(sp):
                sp.dma_start(chip.ident[:, :], dram["ident"]).then_inc(loaded, DMA)
                sp.dma_start(g_raw[:, 0:4], dram["g_xattn"]).then_inc(loaded, DMA)
                sp.dma_start(g_raw[:, 4:8], dram["g_ffn"]).then_inc(loaded, DMA)
                sp.wait_ge(loaded, 3 * DMA)

            @block.gpsimd
            def _(pool):
                pool.memset(chip.neg_half[:, :], -0.5).then_inc(filled, 1)

            @block.scalar
            def _(act):
                act.wait_ge(loaded, 3 * DMA)
                act.activation(chip.tanh_g[:, :], g_raw[:, :], ACT.Tanh).then_inc(gates, 1)


def l0_mix(chip):
    nc, dram, x_all, bank = chip.nc, chip.dram, chip.x_all, chip.bank
    with Phase(chip, "l0mix") as ph:
        ln = LayerNorm(ph, "ln")
        powers = ph.sb("powers", [P, P])
        ctx = ph.sb("ctx", [P, 2, G, D])
        kv = ph.sb("kv", [P, 2, N])
        xn = ph.sb("xn", [P, 2, G, D])
        scaled = ph.sb("scaled", [P, N])
        x_out = ph.sb("x_out", [P, 2, G, D])
        w_in, kv_done = ph.sem("w_in"), ph.sem("kv")
        loaded, stored = [ph.sem("loaded0"), ph.sem("loaded1")], [ph.sem("stored0"), ph.sem("stored1")]
        xn_done, r_done, scaled_done = ph.sem("xn"), ph.sem("r"), ph.sem("scaled")
        out_done = ph.sem("out")
        x_dram = dram["x"].rearrange("(n p) d -> p n d", p=P)
        ctx_dram = dram["ctx"].rearrange("(n p) d -> p n d", p=P)
        x1_dram = dram["x1"].rearrange("(n p) d -> p n d", p=P)
        tanh_g = chip.tanh_g[:, 0:1]

        with nc.Block() as block:
            @block.sync
            def _(sp):
                sp.dma_start(powers[:, :], dram["powers"]).then_inc(w_in, DMA)

                def step(i, h):
                    reuse(sp, kv_done, i - 1)
                    sp.dma_start(group_of(x_all, i), group_of(x_dram, i)).then_inc(loaded[h], DMA)
                    sp.dma_start(ctx[:, h], group_of(ctx_dram, i)).then_inc(loaded[h], DMA)
                each_group(step, sp)

            @block.scalar
            def _(act):
                def step(i, h):
                    act.wait_ge(loaded[h], loads(i, h, 2))
                    reuse(act, r_done, i - 1)
                    act.activation(kv[:, h], ctx[:, h].rearrange("p t d -> p (t d)"), ACT.Square)\
                        .then_inc(kv_done, 1)
                    act.wait_ge(out_done, i + 1)
                    act.dma_start(group_of(x1_dram, i), x_out[:, h]).then_inc(stored[h], DMA)
                each_group(step, act)
                for h in range(2):
                    act.wait_ge(stored[h], loads(GROUPS - 2 + h, h))

            @block.gpsimd
            def _(pool):
                each_group(lambda i, h: ln.pool_rstd(pool, i), pool)

            @block.tensor
            def _(pe):
                pe.wait_ge(w_in, DMA)

                def step(i, h):
                    pe.wait_ge(kv_done, i + 1)
                    reuse(pe, scaled_done, i - 1)
                    pe.matmul(bank[h][:, :], powers[:, :], kv[:, h], start=True, stop=True).then_inc(r_done, 1)
                each_group(step, pe)

            @block.vector
            def _(v):
                def front(i, h):
                    wait_apart(v, loaded[h], loads(i, h, 2), chip.passed["v"])
                    ln.vector_stats(v, i, lambda t: tile_of(x_all, i, t))

                def main(i, h, nxt):
                    ln.vector_apply(v, i, lambda t: tile_of(x_all, i, t), xn[:, h], xn_done)
                    nxt()
                    v.wait_ge(r_done, i + 1)
                    v.wait_ge(xn_done, i * G + G)
                    v.tensor_tensor(scaled[:, :], xn[:, h].rearrange("p t d -> p (t d)"), bank[h][:, :], ALU.mult)\
                        .then_inc(scaled_done, 1)
                    reuse(v, stored[h], loads(i - 2, h))
                    v.wait_ge(scaled_done, i + 1)
                    v.scalar_tensor_tensor(out=x_out[:, h], in0=scaled[:, :].rearrange("p (t d) -> p t d", t=G),
                                           scalar=tanh_g, in1=group_of(x_all, i), op0=ALU.mult, op1=ALU.add)\
                        .then_inc(out_done, 1)
                over_groups(front, main, v)


def l0_attention(chip, y1_all, logits):
    nc, dram, x_all, bank, ident = chip.nc, chip.dram, chip.x_all, chip.bank, chip.ident
    H, W = L0_HEADS, L0_HD + 1
    scale = L0_HD ** -0.5
    with Phase(chip, "l0att") as ph:
        ln0, ln1 = LayerNorm(ph, "ln0"), LayerNorm(ph, "ln1")
        wqkv, wo = ph.sb("wqkv", [P, 3 * D]), ph.sb("wo", [P, D])
        b_cols, bq_scaled = ph.sb("b_cols", [P, 3]), ph.sb("bq_scaled", [P, 1])
        bv, bo = ph.sb("bv", [P, D]), ph.sb("bo", [P, D])
        ln_g, ln_b, wg = ph.sb("ln_g", [P, D]), ph.sb("ln_b", [P, D]), ph.sb("wg", [P, L0_E])
        z, z_t = ph.sb("z", [P, 2, G, D]), ph.sb("z_t", [P, 2, N])
        q_t, k_t = ph.sb("q_t", [P, 2, N]), ph.sb("k_t", [P, 2, N])
        v_ones = ph.sb("v_ones", [P, 2, G, H, W])
        top = ph.sb("top", [P, H, G])
        probs, probs_t = ph.sb("probs", [P, H, N]), ph.sb("probs_t", [P, H, N])
        rsum = ph.sb("rsum", [P, G, H])
        o, o_t = ph.sb("o", [P, G, D]), ph.sb("o_t", [P, N])
        res, normed = ph.sb("res", [P, G, D]), ph.sb("normed", [P, G, D])
        y1, y1_t = ph.sb("y1", [P, G, D]), ph.sb("y1_t", [P, 2, N])

        w_in, ones_set, bq_done = ph.sem("w_in"), ph.sem("ones_set"), ph.sem("bq")
        x_in = [ph.sem("x_in0"), ph.sem("x_in1")]
        stored = [ph.sem("stored0"), ph.sem("stored1")]
        z_done, z_turned, z_t_done = ph.sem("z"), ph.sem("z_turned"), ph.sem("z_t")
        qkv_done, qk_out, v_out = ph.sem("qkv"), ph.sem("qk_out"), ph.sem("v_out")
        scored, topped, shifted = ph.sem("scored"), ph.sem("topped"), ph.sem("shifted")
        exped, p_turned, p_t_done = ph.sem("exped"), ph.sem("p_turned"), ph.sem("p_t")
        pv_done, rsum_done, o_done = ph.sem("pv"), ph.sem("rsum"), ph.sem("o")
        o_turned, o_t_done, proj_done = ph.sem("o_turned"), ph.sem("o_t"), ph.sem("proj")
        res_done, normed_done, gained, y1_done = ph.sem("res"), ph.sem("normed"), ph.sem("gained"), ph.sem("y1")
        y1_turned, y1_t_done, gated, logits_out = (ph.sem("y1_turned"), ph.sem("y1_t"), ph.sem("gated"),
                                                   ph.sem("logits_out"))
        x1_dram = dram["x1"].rearrange("(l n) d -> l n d", n=S)
        y1_t_dram = dram["y1_t"].rearrange("p (g n) -> p g n", g=GROUPS)
        row = lambda ap: ap[:, :].unsqueeze(1).to_broadcast([P, G, D])
        side = lambda ap: ap.rearrange("p t d -> p (t d)")

        with nc.Block() as block:
            @block.sync
            def _(sp):
                for dst, name in ((wqkv, "l0_wqkv"), (wo, "l0_wo"), (b_cols, "l0_b_cols"), (bv, "l0_bv"),
                                  (bo, "l0_bo"), (ln_g, "l0_ln1_g"), (ln_b, "l0_ln1_b"), (wg, "l0_wg")):
                    sp.dma_start(dst[:, :], dram[name]).then_inc(w_in, DMA)

                def step(i, h):
                    reuse(sp, z_done, (i - 1) * G)
                    sp.dma_start(group_of(x_all, i), group_of(x1_dram, i)).then_inc(x_in[h], DMA)
                each_group(step, sp)

            @block.gpsimd
            def _(pool):
                pool.memset(v_ones[:, :, :, :, :], 1.0).then_inc(ones_set, 1)

                def front(i, h):
                    ln0.pool_rstd(pool, i)

                def main(i, h, nxt):
                    nxt()
                    ln1.pool_rstd(pool, i)
                    pool.wait_ge(y1_t_done, i + 1)
                    pool.dma_start(y1_t_dram[:, bass.ds(i, 1), :].rearrange("p a n -> p (a n)"), y1_t[:, h])\
                        .then_inc(stored[h], DMA)
                over_groups(front, main, pool)
                for h in range(2):
                    pool.wait_ge(stored[h], loads(GROUPS - 2 + h, h))

            @block.tensor
            def _(pe):
                pe.wait_ge(w_in, 8 * DMA)

                def front(i, h):
                    pe.wait_ge(z_done, i * G + G)
                    transposes(pe, bank[0], [z[:, h, t, :] for t in range(G)], ident).then_inc(z_turned, 1)
                    reuse(pe, qk_out, i * 2)
                    reuse(pe, v_out, i)
                    pe.wait_ge(z_t_done, i + 1)
                    pe.matmul(bank[1][:, :], wqkv[:, 0:D], z_t[:, h], start=True, stop=True).then_inc(qkv_done, 1)
                    pe.matmul(bank[2][:, :], wqkv[:, D:2 * D], z_t[:, h], start=True, stop=True)\
                        .then_inc(qkv_done, 1)
                    for t in range(G):
                        mm = pe.matmul(bank[3][:, t * D:(t + 1) * D], z_t[:, h, t * P:(t + 1) * P], wqkv[:, 2 * D:],
                                       start=True, stop=True)
                    mm.then_inc(qkv_done, 1)

                def main(i, h, nxt):
                    pe.wait_ge(qk_out, i * 2 + 2)
                    reuse(pe, logits_out, i)
                    for t in range(G):
                        for n in range(H):
                            r = slice(n * L0_HD, (n + 1) * L0_HD)
                            mm = pe.matmul(bank[4 + n][:, t * P:(t + 1) * P], q_t[r, h, t * P:(t + 1) * P],
                                           k_t[r, h, t * P:(t + 1) * P], start=True, stop=True)
                            if t == G - 1:
                                mm.then_inc(scored, 1)
                    for n in range(H):
                        pe.wait_ge(exped, i * H + n + 1)
                        transposes(pe, bank[4 + n], [probs[:, n, t * P:(t + 1) * P] for t in range(G)], ident)\
                            .then_inc(p_turned, 1)
                    pe.wait_ge(v_out, i + 1)
                    pe.wait_ge(p_t_done, i * H + H)
                    for t in range(G):
                        for n in range(H):
                            mm = pe.matmul(bank[4 + t // 2][:, ((t % 2) * H + n) * W:((t % 2) * H + n + 1) * W],
                                           probs_t[:, n, t * P:(t + 1) * P], v_ones[:, h, t, n, :],
                                           start=True, stop=True)
                        if t % 2:
                            mm.then_inc(pv_done, 1)
                    nxt()
                    pe.wait_ge(o_done, i * 2 + 2)
                    transposes(pe, bank[6], [o[:, t, :] for t in range(G)], ident).then_inc(o_turned, 1)
                    pe.wait_ge(o_t_done, i + 1)
                    for t in range(G):
                        mm = pe.matmul(bank[7][:, t * D:(t + 1) * D], o_t[:, t * P:(t + 1) * P], wo[:, :],
                                       start=True, stop=True)
                    mm.then_inc(proj_done, 1)
                    pe.wait_ge(y1_done, i + 1)
                    transposes(pe, bank[5], [y1[:, t, :] for t in range(G)], ident).then_inc(y1_turned, 1)
                    pe.wait_ge(y1_t_done, i + 1)
                    for t in range(G):
                        mm = pe.matmul(bank[6][:, t * L0_E:(t + 1) * L0_E], y1_t[:, h, t * P:(t + 1) * P], wg[:, :],
                                       start=True, stop=True)
                    mm.then_inc(gated, 1)
                over_groups(front, main, pe)

            @block.scalar
            def _(act):
                act.wait_ge(w_in, 8 * DMA)
                act.mul(bq_scaled[:, :], b_cols[:, 0:1], scale).then_inc(bq_done, 1)
                act.wait_ge(bq_done, 1)

                def front(i, h):
                    act.wait_ge(z_turned, i + 1)
                    act.activation(z_t[:, h], bank[0][:, :], ACT.Identity).then_inc(z_t_done, 1)
                    act.wait_ge(qkv_done, i * 3 + 1)
                    act.activation(q_t[:, h], bank[1][:, :], ACT.Identity, bias=bq_scaled[:, 0:1], scale=scale)\
                        .then_inc(qk_out, 1)
                    act.wait_ge(qkv_done, i * 3 + 2)
                    act.activation(k_t[:, h], bank[2][:, :], ACT.Identity, bias=b_cols[:, 1:2]).then_inc(qk_out, 1)

                def main(i, h, nxt):
                    for n in range(H):
                        act.wait_ge(shifted, i * H + n + 1)
                        act.activation(probs[:, n], probs[:, n], ACT.Exp).then_inc(exped, 1)
                    for n in range(H):
                        act.wait_ge(p_turned, i * H + n + 1)
                        act.activation(probs_t[:, n], bank[4 + n][:, :], ACT.Identity).then_inc(p_t_done, 1)
                    nxt()
                    act.wait_ge(o_turned, i + 1)
                    act.activation(o_t[:, :], bank[6][:, :], ACT.Identity).then_inc(o_t_done, 1)
                    act.wait_ge(y1_turned, i + 1)
                    reuse(act, stored[h], loads(i - 2, h))
                    act.activation(y1_t[:, h], bank[5][:, :], ACT.Identity).then_inc(y1_t_done, 1)
                over_groups(front, main, act)

            @block.vector
            def _(v):
                v.wait_ge(w_in, 8 * DMA)
                v.wait_ge(ones_set, 1)

                def front(i, h):
                    wait_apart(v, x_in[h], loads(i, h), chip.passed["v"])
                    ln0.vector_stats(v, i, lambda t: tile_of(x_all, i, t))
                    ln0.vector_apply(v, i, lambda t: tile_of(x_all, i, t), z[:, h], z_done)

                def value_rows(i, h):
                    v.wait_ge(qkv_done, i * 3 + 3)
                    v.tensor_tensor(v_ones[:, h, :, :, 0:L0_HD],
                                    bank[3][:, :].rearrange("p (t n d) -> p t n d", t=G, n=H),
                                    bv[:, :].rearrange("p (n d) -> p n d", n=H).unsqueeze(1)
                                    .to_broadcast([P, G, H, L0_HD]), ALU.add).then_inc(v_out, 1)

                def main(i, h, nxt):
                    value_rows(i, h)
                    for n in range(H):
                        by_tile = bank[4 + n][:, :].rearrange("p (t m) -> p t m", t=G)
                        v.wait_ge(scored, i * H + n + 1)
                        v.tensor_reduce(top[:, n, :], by_tile, AX.X, ALU.max).then_inc(topped, 1)
                        v.wait_ge(topped, i * H + n + 1)
                        v.tensor_tensor(probs[:, n].rearrange("p (t m) -> p t m", t=G), by_tile,
                                        top[:, n, :].unsqueeze(2).to_broadcast([P, G, P]), ALU.subtract)\
                            .then_inc(shifted, 1)
                    nxt()
                    for b in range(2):
                        pv = bank[4 + b][:, 0:2 * H * W].rearrange("p (t n w) -> p t n w", t=2, n=H)
                        v.wait_ge(pv_done, i * 2 + b + 1)
                        v.reciprocal(rsum[:, 2 * b:2 * b + 2, :], pv[:, :, :, L0_HD]).then_inc(rsum_done, 1)
                        v.wait_ge(rsum_done, i * 2 + b + 1)
                        v.tensor_tensor(o[:, 2 * b:2 * b + 2, :].rearrange("p t (n d) -> p t n d", n=H),
                                        pv[:, :, :, 0:L0_HD],
                                        rsum[:, 2 * b:2 * b + 2, :].unsqueeze(3).to_broadcast([P, 2, H, L0_HD]),
                                        ALU.mult).then_inc(o_done, 1)
                    v.wait_ge(proj_done, i + 1)
                    v.tensor_tensor(side(res[:, :, :]), bank[7][:, :], side(z[:, h]), ALU.add).then_inc(res_done, 1)
                    v.wait_ge(res_done, i * 2 + 1)
                    v.tensor_tensor(res[:, :, :], res[:, :, :], row(bo), ALU.add).then_inc(res_done, 1)
                    wait_apart(v, res_done, i * 2 + 2, chip.passed["v"])
                    ln1.vector_stats(v, i, lambda t: res[:, t, :])
                    ln1.vector_apply(v, i, lambda t: res[:, t, :], normed, normed_done)
                    v.wait_ge(normed_done, i * G + G)
                    v.tensor_tensor(normed[:, :, :], normed[:, :, :], row(ln_g), ALU.mult).then_inc(gained, 1)
                    v.wait_ge(gained, i + 1)
                    v.tensor_tensor(y1[:, :, :], normed[:, :, :], row(ln_b), ALU.add).then_inc(y1_done, 1)
                    v.wait_ge(y1_done, i + 1)
                    v.tensor_scalar(group_of(y1_all, i), y1[:, :, :], 1.0, None, ALU.mult)
                    v.wait_ge(gated, i + 1)
                    v.tensor_scalar(logits[:, bass.ds(i * G, G), :],
                                    bank[6][:, 0:G * L0_E].rearrange("p (t e) -> p t e", t=G), 1.0, None, ALU.mult)\
                        .then_inc(logits_out, 1)
                over_groups(front, main, v)


def l0_route(chip, logits, weight):
    nc, dram, bank = chip.nc, chip.dram, chip.bank
    E = L0_E
    with Phase(chip, "l0route") as ph:
        first, later = ph.sb("first", [P, E]), ph.sb("later", [P, P])
        best, total = ph.sb("best", [P, TILES]), ph.sb("total", [P, TILES])
        shifted, exps = ph.sb("shifted", [P, TILES, E]), ph.sb("exps", [P, TILES, E])
        hot, place = ph.sb("hot", [P, TILES, E]), ph.sb("place", [P, TILES, E])
        count, base = ph.sb("count", [P, E]), ph.sb("base", [P, E])
        ones = ph.sb("ones", [P, TILES])
        loaded, ones_set, done, exped, based = (ph.sem("loaded"), ph.sem("ones"), ph.sem("vector_steps"),
                                                ph.sem("exped"), ph.sem("based"))
        wide = lambda ap: ap[:, :].unsqueeze(2).to_broadcast([P, TILES, E])
        with nc.Block() as block:
            @block.sync
            def _(sp):
                sp.dma_start(first[:, :], dram["l0_first"]).then_inc(loaded, DMA)
                sp.dma_start(later[:, :], dram["later"]).then_inc(loaded, DMA)

            @block.gpsimd
            def _(pool):
                pool.memset(ones[:, :], 1.0).then_inc(ones_set, 1)

            @block.scalar
            def _(act):
                act.wait_ge(done, 2)
                act.activation(exps[:, :, :], shifted[:, :, :], ACT.Exp).then_inc(exped, 1)

            @block.tensor
            def _(pe):
                pe.wait_ge(loaded, 2 * DMA)
                pe.wait_ge(done, 7)
                pe.matmul(bank[0][:, 0:E], later[:, :], count[:, :], start=True, stop=True).then_inc(based, 1)

            @block.vector
            def _(v):
                v.wait_ge(loaded, 2 * DMA)
                v.tensor_reduce(best[:, :], logits[:, :, :], AX.X, ALU.max).then_inc(done, 1)
                v.wait_ge(done, 1)
                v.tensor_tensor(shifted[:, :, :], logits[:, :, :], wide(best), ALU.subtract).then_inc(done, 1)
                v.wait_ge(done, 2)
                v.tensor_scalar(hot[:, :, :], shifted[:, :, :], 0.0, None, ALU.is_equal).then_inc(done, 1)
                v.wait_ge(done, 3)
                v.tensor_tensor(place[:, :, :], hot[:, :, :], first[:, :].unsqueeze(1).to_broadcast([P, TILES, E]),
                                ALU.mult).then_inc(done, 1)
                v.wait_ge(done, 4)
                v.tensor_reduce(best[:, :], place[:, :, :], AX.X, ALU.max).then_inc(done, 1)
                v.wait_ge(done, 5)
                v.tensor_tensor(hot[:, :, :], place[:, :, :], wide(best), ALU.is_equal).then_inc(done, 1)
                v.wait_ge(done, 6)
                v.tensor_reduce(count[:, :], hot[:, :, :].rearrange("p n e -> p e n"), AX.X, ALU.add).then_inc(done, 1)
                v.wait_ge(based, 1)
                v.tensor_copy(base[:, :], bank[0][:, 0:E]).then_inc(done, 1)
                v.wait_ge(done, 8)
                v.wait_ge(ones_set, 1)
                for e in range(E):
                    v.tensor_tensor_scan(place[:, :, e], ones[:, :], hot[:, :, e], base[:, e:e + 1], ALU.mult, ALU.add)\
                        .then_inc(done, 1)
                v.wait_ge(exped, 1)
                v.tensor_reduce(total[:, :], exps[:, :, :], AX.X, ALU.add).then_inc(done, 1)
                v.wait_ge(done, 9 + E)
                v.reciprocal(best[:, :], total[:, :]).then_inc(done, 1)
                v.scalar_tensor_tensor(out=weight[:, :, :], in0=place[:, :, :], scalar=float(L0_CAP),
                                       in1=hot[:, :, :], op0=ALU.is_le, op1=ALU.mult).then_inc(done, 1)
                v.wait_ge(done, 11 + E)
                v.tensor_tensor(weight[:, :, :], weight[:, :, :], wide(best), ALU.mult).then_inc(done, 1)


def l0_experts(chip, y1_all, weight):
    nc, dram, x_all, bank, ident = chip.nc, chip.dram, chip.x_all, chip.bank, chip.ident
    E, C = L0_E, L0_FF // P
    with Phase(chip, "l0moe") as ph:
        ln = LayerNorm(ph, "ln")
        w1_t, w2 = ph.sb("w1_t", [P, E, C, D]), ph.sb("w2", [P, E, C, D])
        b1, b1_wide, b2 = ph.sb("b1", [P, E, C]), ph.sb("b1_wide", [P, E * C * E + 8]), ph.sb("b2", [E, D])
        w12, b12 = ph.sb("w12", [P, E, D]), ph.sb("b12", [E, D])
        ln_g, ln_b = ph.sb("ln_g", [P, D]), ph.sb("ln_b", [P, D])
        y1_t = ph.sb("y1_t", [P, 2, N])
        w_now, w_t = ph.sb("w_now", [P, 2, G, E]), ph.sb("w_t", [E, 2, N])
        acc, normed = ph.sb("acc", [P, 2, G, D]), ph.sb("normed", [P, G, D])
        w_in, b1_zero, b1_spread = ph.sem("w_in"), ph.sem("b1_zero"), ph.sem("b1_spread")
        merged, merged_out, affine = ph.sem("merged"), ph.sem("merged_out"), ph.sem("affine")
        y_in, stored = [ph.sem("y_in0"), ph.sem("y_in1")], [ph.sem("stored0"), ph.sem("stored1")]
        w_now_done, w_turned, w_t_done, biased = (ph.sem("w_now"), ph.sem("w_turned"), ph.sem("w_t"), ph.sem("biased"))
        made, used, acc_done = ph.sem("made"), ph.sem("used"), ph.sem("acc")
        normed_done, gained, moved, x2_done = ph.sem("normed"), ph.sem("gained"), ph.sem("moved"), ph.sem("x2")
        y1_t_dram = dram["y1_t"].rearrange("p (g n) -> p g n", g=GROUPS)
        x2_dram = dram["x2"].rearrange("(l n) d -> l n d", n=S)
        tanh_g = chip.tanh_g[:, 4:5]
        row = lambda ap: ap[:, :].unsqueeze(1).to_broadcast([P, G, D])

        with nc.Block() as block:
            @block.sync
            def _(sp):
                for dst, name in ((w1_t, "l0_w1_t"), (w2, "l0_w2"), (b1, "l0_b1")):
                    sp.dma_start(dst[:, :, :], dram[name]).then_inc(w_in, DMA)
                for dst, name in ((b2, "l0_b2"), (ln_g, "l0_ln2_g"), (ln_b, "l0_ln2_b")):
                    sp.dma_start(dst[:, :], dram[name]).then_inc(w_in, DMA)

                def step(i, h):
                    reuse(sp, made, (i - 1) * G)
                    sp.dma_start(y1_t[:, h], y1_t_dram[:, bass.ds(i, 1), :].rearrange("p a n -> p (a n)"))\
                        .then_inc(y_in[h], DMA)
                each_group(step, sp)

            @block.gpsimd
            def _(pool):
                pool.memset(b1_wide[:, :], 0.0).then_inc(b1_zero, 1)

                def step(i, h):
                    ln.pool_rstd(pool, i)
                    pool.wait_ge(x2_done, i + 1)
                    pool.dma_start(group_of(x2_dram, i), group_of(x_all, i)).then_inc(stored[h], DMA)
                each_group(step, pool)
                for h in range(2):
                    pool.wait_ge(stored[h], loads(GROUPS - 2 + h, h))

            @block.tensor
            def _(pe):
                pe.wait_ge(w_in, 6 * DMA)
                pe.wait_ge(b1_spread, 1)
                for e in range(E):
                    for c in range(C):
                        pe.matmul(bank[e // 4][:, (e % 4) * D:(e % 4 + 1) * D], w1_t[:, e, c, :], w2[:, e, c, :],
                                  start=(c == 0), stop=(c == C - 1))
                for k in range(E * C):
                    mm = pe.matmul(bank[2][0:E, 0:D], b1_wide[:, k * E:(k + 1) * E], w2[:, k // C, k % C, :],
                                   start=(k == 0), stop=(k == E * C - 1))
                mm.then_inc(merged, 1)
                pe.wait_ge(merged_out, 3)

                def step(i, h):
                    pe.wait_ge(w_now_done, i + 1)
                    reuse(pe, acc_done, i)
                    for t in range(G):
                        mm = pe.transpose(bank[6][0:E, t * P:(t + 1) * P], w_now[:, h, t, :], ident[:, :])
                    mm.then_inc(w_turned, 1)
                    pe.wait_ge(w_t_done, i + 1)
                    for t in range(G):
                        mm = pe.matmul(bank[7][:, t * D:(t + 1) * D], w_t[:, h, t * P:(t + 1) * P], b12[:, :],
                                       start=True, stop=True)
                    mm.then_inc(biased, 1)
                    pe.wait_ge(y_in[h], loads(i, h))
                    for t in range(G):
                        reuse(pe, used, (i * G + t - 1) * E)
                        for half in range(2):
                            mm = pe.matmul(bank[2 * (t % 2) + half][:, :], y1_t[:, h, t * P:(t + 1) * P],
                                           w12[:, half * 4:half * 4 + 4, :].rearrange("p e d -> p (e d)"),
                                           start=True, stop=True)
                        mm.then_inc(made, 1)
                each_group(step, pe)

            @block.scalar
            def _(act):
                def step(i, h):
                    act.wait_ge(w_turned, i + 1)
                    act.activation(w_t[:, h], bank[6][0:E, :], ACT.Identity).then_inc(w_t_done, 1)
                each_group(step, act)

            @block.vector
            def _(v):
                v.wait_ge(w_in, 6 * DMA)
                v.wait_ge(b1_zero, 1)
                v.tensor_copy(b1_wide[:, 0:E * (C * E + 1)].rearrange("p (e r) -> p e r", e=E)[:, :, 0:C * E]
                              .rearrange("p e (c k) -> p e c k", c=C)[:, :, :, 0], b1[:, :, :]).then_inc(b1_spread, 1)
                v.tensor_scalar(ln_g[:, :], ln_g[:, :], tanh_g, None, ALU.mult).then_inc(affine, 1)
                v.tensor_scalar(ln_b[:, :], ln_b[:, :], tanh_g, None, ALU.mult).then_inc(affine, 1)
                v.wait_ge(merged, 1)
                for half in range(2):
                    v.tensor_copy(w12[:, half * 4:half * 4 + 4, :].rearrange("p e d -> p (e d)"), bank[half][:, :])\
                        .then_inc(merged_out, 1)
                v.tensor_tensor(b12[:, :], bank[2][0:E, 0:D], b2[:, :], ALU.add).then_inc(merged_out, 1)

                def front(i, h):
                    v.tensor_scalar(w_now[:, h], weight[:, bass.ds(i * G, G), :], 1.0, None, ALU.mult)\
                        .then_inc(w_now_done, 1)

                def main(i, h, nxt):
                    nxt()
                    for t in range(G):
                        v.wait_ge(made, i * G + t + 1)
                        for e in range(E):
                            if e:
                                v.wait_ge(used, i * G * E + t * E + e)
                            mm = v.scalar_tensor_tensor(
                                out=acc[:, h, t, :], in0=bank[2 * (t % 2) + e // 4][:, (e % 4) * D:(e % 4 + 1) * D],
                                scalar=w_now[:, h, t, e:e + 1],
                                in1=acc[:, h, t, :] if e else tile_of(y1_all, i, t), op0=ALU.mult, op1=ALU.add)
                            mm.then_inc(used, 1)
                    v.wait_ge(used, (i + 1) * G * E)
                    v.wait_ge(biased, i + 1)
                    v.tensor_tensor(acc[:, h].rearrange("p t d -> p (t d)"), acc[:, h].rearrange("p t d -> p (t d)"),
                                    bank[7][:, :], ALU.add).then_inc(acc_done, 1)
                    wait_apart(v, acc_done, i + 1, chip.passed["v"])
                    ln.vector_stats(v, i, lambda t: acc[:, h, t, :])
                    ln.vector_apply(v, i, lambda t: acc[:, h, t, :], normed, normed_done)
                    v.wait_ge(normed_done, i * G + G)
                    v.tensor_tensor(normed[:, :, :], normed[:, :, :], row(ln_g), ALU.mult).then_inc(gained, 1)
                    v.wait_ge(gained, i + 1)
                    v.tensor_tensor(normed[:, :, :], normed[:, :, :], row(ln_b), ALU.add).then_inc(moved, 1)
                    v.wait_ge(moved, i + 1)
                    v.tensor_tensor(group_of(x_all, i), normed[:, :, :], group_of(x_all, i), ALU.add)\
                        .then_inc(x2_done, 1)
                over_groups(front, main, v)


def l1_mix(chip):
    nc, dram, x_all, bank, ident = chip.nc, chip.dram, chip.x_all, chip.bank, chip.ident
    with Phase(chip, "l1mix") as ph:
        ln = LayerNorm(ph, "ln")
        w_sim, b_sim = ph.sb("w_sim", [P, 3]), ph.sb("b_sim", [P, 1])
        wqv, bqv, block_of = ph.sb("wqv", [P, 4, D]), ph.sb("bqv", [P, D]), ph.sb("block_of", [P, 2])
        ctx, ctx_t = ph.sb("ctx", [P, 2, G, D]), ph.sb("ctx_t", [P, 2, N])
        e, e_t = ph.sb("e", [P, 2, G, D]), ph.sb("e_t", [P, 2, N])
        key_t = ph.sb("key_t", [P, 2, N])
        top, own = ph.sb("top", [P, G]), ph.sb("own", [P, G])
        sim, rsum = ph.sb("sim", [P, G, S]), ph.sb("rsum", [P, G])
        attn, attn_t = ph.sb("attn", [P, G, 2, S]), ph.sb("attn_t", [P, N])
        peak, peak_sum = ph.sb("peak", [G, 2]), ph.sb("peak_sum", [G, 2])
        pick = ph.sb("pick", [G, 2, S])
        pick_two, hc = ph.sb("pick_two", [P, G, 2]), ph.sb("hc", [P, BG])
        hq_t, ehq_t, ehc_t = ph.sb("hq_t", [P, N]), ph.sb("ehq_t", [P, N]), ph.sb("ehc_t", [P, N])
        out = ph.sb("out", [P, N])

        w_in, zeroed = ph.sem("w_in"), ph.sem("zeroed")
        ctx_in = [ph.sem("ctx_in0"), ph.sem("ctx_in1")]
        e_done, e_turned, e_t_done, key_done = ph.sem("e"), ph.sem("e_turned"), ph.sem("e_t"), ph.sem("key")
        scored, topped, shifted, exped = ph.sem("scored"), ph.sem("topped"), ph.sem("shifted"), ph.sem("exped")
        summed, inverted, attn_done = ph.sem("summed"), ph.sem("inverted"), ph.sem("attn")
        attn_turned, attn_t_done, hq_done, hq_out = (ph.sem("attn_turned"), ph.sem("attn_t"), ph.sem("hq"),
                                                     ph.sem("hq_out"))
        own_done, own_turned, peaked, pick_shifted = (ph.sem("own"), ph.sem("own_turned"), ph.sem("peaked"),
                                                      ph.sem("pick_shifted"))
        pick_exped, pick_summed, pick_done, pick_turned = (ph.sem("pick_exped"), ph.sem("pick_summed"),
                                                           ph.sem("pick"), ph.sem("pick_turned"))
        pick_two_done, hc_made, hc_done = ph.sem("pick_two"), ph.sem("hc_made"), ph.sem("hc")
        feats_done, mixed, biased, x_done = ph.sem("feats"), ph.sem("mixed"), ph.sem("biased"), ph.sem("x")
        ctx_dram = dram["ctx"].rearrange("(n p) d -> p n d", p=P)
        ctx_t_dram = dram["ctx_t"].rearrange("p (g n) -> p g n", g=GROUPS)
        tanh_g = chip.tanh_g[:, 1:2]
        tiles = lambda ap: ap.rearrange("p (t d) -> p t d", t=G)

        with nc.Block() as block:
            @block.sync
            def _(sp):
                for dst, name in ((w_sim[:, :], "l1_w_sim"), (b_sim[:, :], "l1_b_sim"), (wqv[:, :, :], "l1_wqv"),
                                  (bqv[:, :], "l1_bqv"), (block_of[:, :], "block_of")):
                    sp.dma_start(dst, dram[name]).then_inc(w_in, DMA)

                def step(i, h):
                    reuse(sp, hq_done, i - 1)
                    sp.dma_start(ctx[:, h], group_of(ctx_dram, i)).then_inc(ctx_in[h], DMA)
                    sp.dma_start(ctx_t[:, h], ctx_t_dram[:, bass.ds(i, 1), :].rearrange("p a n -> p (a n)"))\
                        .then_inc(ctx_in[h], DMA)
                each_group(step, sp)

            @block.gpsimd
            def _(pool):
                pool.memset(attn[:, :, :, :], 0.0).then_inc(zeroed, 1)
                each_group(lambda i, h: ln.pool_rstd(pool, i), pool)

            @block.tensor
            def _(pe):
                pe.wait_ge(w_in, 5 * DMA)

                def front(i, h):
                    pe.wait_ge(e_done, i * G + G)
                    reuse(pe, e_t_done, i)
                    transposes(pe, bank[0], [e[:, h, t, :] for t in range(G)], ident).then_inc(e_turned, 1)

                def main(i, h, nxt):
                    pe.wait_ge(key_done, i + 1)
                    pe.wait_ge(ctx_in[h], loads(i, h, 2))
                    reuse(pe, own_done, i * 2)
                    reuse(pe, shifted, i)
                    for t in range(G):
                        for b in range(2):
                            c = slice(t * P + b * S, t * P + (b + 1) * S)
                            pe.matmul(bank[1][b * S:(b + 1) * S, t * S:(t + 1) * S], key_t[:, h, c], ctx_t[:, h, c],
                                      start=True, stop=True)
                    for t in range(G):
                        mm = pe.matmul(bank[1][:, G * S + t:G * S + t + 1], e_t[:, h, t * P:(t + 1) * P], w_sim[:, 0:1],
                                       start=True, stop=True)
                    mm.then_inc(scored, 1)
                    pe.wait_ge(own_done, i * 2 + 2)
                    pe.transpose(bank[2][0:G, 0:P], own[:, :], ident[:, :]).then_inc(own_turned, 1)
                    pe.wait_ge(attn_done, i * 2 + 2)
                    transposes(pe, bank[3], [attn[:, t].rearrange("p b s -> p (b s)") for t in range(G)], ident)\
                        .then_inc(attn_turned, 1)
                    pe.wait_ge(attn_t_done, i + 1)
                    for t in range(G):
                        mm = pe.matmul(bank[4][:, t * P:(t + 1) * P], ctx[:, h, t, :], attn_t[:, t * P:(t + 1) * P],
                                       start=True, stop=True)
                    mm.then_inc(hq_done, 1)
                    wait_apart(pe, pick_done, i + 1, chip.passed["pe"])
                    pe.transpose(bank[5][:, 0:G], pick[:, :, :].rearrange("p b s -> p (b s)"), ident[0:G, 0:G])\
                        .then_inc(pick_turned, 1)
                    pe.wait_ge(pick_two_done, i + 1)
                    for t in range(G):
                        mm = pe.matmul(bank[6][:, 2 * t:2 * t + 2], e[:, h, t, :], pick_two[:, t, :],
                                       start=True, stop=True)
                    mm.then_inc(hc_made, 1)
                    nxt()
                    pe.wait_ge(hq_out, i + 1)
                    pe.wait_ge(feats_done, i * 2 + 2)
                    for t in range(G):
                        c = slice(t * P, (t + 1) * P)
                        for k, feat in enumerate((e_t[:, h, c], hq_t[:, c], ehq_t[:, c], ehc_t[:, c])):
                            mm = pe.matmul(bank[7][:, c], feat, wqv[:, k, :], start=(k == 0), stop=(k == 3))
                    mm.then_inc(mixed, 1)
                over_groups(front, main, pe)

            @block.scalar
            def _(act):
                def front(i, h):
                    act.wait_ge(e_turned, i + 1)
                    act.activation(e_t[:, h], bank[0][:, :], ACT.Identity).then_inc(e_t_done, 1)

                def main(i, h, nxt):
                    act.wait_ge(shifted, i + 1)
                    act.activation(sim[:, :, :], sim[:, :, :], ACT.Exp).then_inc(exped, 1)
                    act.wait_ge(pick_shifted, i + 1)
                    act.activation(pick[:, :, :], pick[:, :, :], ACT.Exp).then_inc(pick_exped, 1)
                    act.wait_ge(attn_turned, i + 1)
                    act.activation(attn_t[:, :], bank[3][:, :], ACT.Identity).then_inc(attn_t_done, 1)
                    act.wait_ge(hq_done, i + 1)
                    act.activation(hq_t[:, :], bank[4][:, :], ACT.Identity).then_inc(hq_out, 1)
                    nxt()
                over_groups(front, main, act)

            @block.vector
            def _(v):
                v.wait_ge(w_in, 5 * DMA)
                v.wait_ge(zeroed, 1)

                def front(i, h):
                    ln.vector_stats(v, i, lambda t: tile_of(x_all, i, t))
                    ln.vector_apply(v, i, lambda t: tile_of(x_all, i, t), e[:, h], e_done)

                def make_key(i, h):
                    v.wait_ge(e_t_done, i + 1)
                    v.tensor_scalar(key_t[:, h], e_t[:, h], w_sim[:, 2:3], w_sim[:, 1:2], ALU.mult, ALU.add)\
                        .then_inc(key_done, 1)

                def main(i, h, nxt):
                    make_key(i, h)
                    scores = bank[1][:, 0:G * S].rearrange("p (t s) -> p t s", t=G)
                    wide = lambda ap: ap[:, :].unsqueeze(2).to_broadcast([P, G, S])
                    v.wait_ge(scored, i + 1)
                    v.tensor_reduce(top[:, :], scores, AX.X, ALU.max).then_inc(topped, 1)
                    v.wait_ge(topped, i + 1)
                    v.tensor_tensor(sim[:, :, :], scores, wide(top), ALU.subtract).then_inc(shifted, 1)
                    v.tensor_tensor(own[:, :], bank[1][:, G * S:G * S + G], top[:, :], ALU.add).then_inc(own_done, 1)
                    v.wait_ge(own_done, i * 2 + 1)
                    v.tensor_scalar(own[:, :], own[:, :], b_sim[:, 0:1], None, ALU.add).then_inc(own_done, 1)
                    v.wait_ge(exped, i + 1)
                    v.tensor_reduce(rsum[:, :], sim[:, :, :], AX.X, ALU.add).then_inc(summed, 1)
                    v.wait_ge(summed, i + 1)
                    v.reciprocal(rsum[:, :], rsum[:, :]).then_inc(inverted, 1)
                    v.wait_ge(inverted, i + 1)
                    for b in range(2):
                        r = slice(b * S, (b + 1) * S)
                        v.tensor_tensor(attn[r, :, b, :], sim[r, :, :], rsum[r, :].unsqueeze(2).to_broadcast([S, G, S]),
                                        ALU.mult).then_inc(attn_done, 1)
                    maxima = bank[2][0:G, 0:P].rearrange("p (b s) -> p b s", b=2)
                    over = lambda ap: ap[:, :].unsqueeze(2).to_broadcast([G, 2, S])
                    v.wait_ge(own_turned, i + 1)
                    v.tensor_reduce(peak[:, :], maxima, AX.X, ALU.max).then_inc(peaked, 1)
                    v.wait_ge(peaked, i + 1)
                    v.tensor_tensor(pick[:, :, :], maxima, over(peak), ALU.subtract).then_inc(pick_shifted, 1)
                    nxt()
                    v.wait_ge(pick_exped, i + 1)
                    v.tensor_reduce(peak_sum[:, :], pick[:, :, :], AX.X, ALU.add).then_inc(pick_summed, 1)
                    v.wait_ge(pick_summed, i * 2 + 1)
                    v.reciprocal(peak_sum[:, :], peak_sum[:, :]).then_inc(pick_summed, 1)
                    v.wait_ge(pick_summed, i * 2 + 2)
                    v.tensor_tensor(pick[:, :, :], pick[:, :, :], over(peak_sum), ALU.mult).then_inc(pick_done, 1)
                    v.wait_ge(pick_turned, i + 1)
                    v.tensor_tensor(pick_two[:, :, :], bank[5][:, 0:G].unsqueeze(2).to_broadcast([P, G, 2]),
                                    block_of[:, :].unsqueeze(1).to_broadcast([P, G, 2]), ALU.mult)\
                        .then_inc(pick_two_done, 1)
                    v.wait_ge(hq_out, i + 1)
                    v.tensor_tensor(ehq_t[:, :], e_t[:, h], hq_t[:, :], ALU.mult).then_inc(feats_done, 1)
                    v.wait_ge(hc_made, i + 1)
                    v.tensor_tensor(ehc_t[:, :].rearrange("p (b s) -> p b s", b=BG),
                                    e_t[:, h].rearrange("p (b s) -> p b s", b=BG),
                                    bank[6][:, 0:BG].unsqueeze(2).to_broadcast([P, BG, S]), ALU.mult)\
                        .then_inc(feats_done, 1)
                    v.wait_ge(mixed, i + 1)
                    v.tensor_tensor(tiles(out[:, :]), tiles(bank[7][:, :]),
                                    bqv[:, :].unsqueeze(1).to_broadcast([P, G, D]), ALU.add).then_inc(biased, 1)
                    v.wait_ge(biased, i + 1)
                    v.scalar_tensor_tensor(out=group_of(x_all, i), in0=tiles(out[:, :]), scalar=tanh_g,
                                           in1=group_of(x_all, i), op0=ALU.mult, op1=ALU.add).then_inc(x_done, 1)
                over_groups(front, main, v)


def l1_ffn(chip):
    nc, dram, x_all, bank, ident = chip.nc, chip.dram, chip.x_all, chip.bank, chip.ident
    E, EG, PER = L1_E, L1_GROUPS, L1_E // L1_GROUPS
    with Phase(chip, "l1ffn") as ph:
        ln = LayerNorm(ph, "ln")
        w1, w3, w2 = ph.sb("w1", [P, E, P]), ph.sb("w3", [P, E, P]), ph.sb("w2", [P, E, D])
        wg, b1, b3, b2 = ph.sb("wg", [P, E]), ph.sb("b1", [P, E]), ph.sb("b3", [P, E]), ph.sb("b2", [E, D])
        earlier = ph.sb("earlier", [P, EG, EG])
        z, z_t = ph.sb("z", [P, G, D]), ph.sb("z_t", [P, 2, N])
        gate, kept = ph.sb("gate", [P, G, E]), ph.sb("kept", [P, G, E])
        gtop, above, tied = ph.sb("gtop", [P, G, EG]), ph.sb("above", [P, G * EG, EG]), ph.sb("tied", [P, G * EG, EG])
        rank, gsel = ph.sb("rank", [P, G * EG]), ph.sb("gsel", [P, G * EG])
        best8, sel, tie = ph.sb("best8", [P, G, 8]), ph.sb("sel", [P, G, E]), ph.sb("tie", [P, G, E])
        n_above, tie_no = ph.sb("n_above", [P, G]), ph.sb("tie_no", [P, G, E])
        ones = ph.sb("ones", [P, E])
        wsum, w = ph.sb("wsum", [P, G]), ph.sb("w", [P, 2, G, E])
        w_t = ph.sb("w_t", [E, 2, N])
        act1, hid = ph.sb("act1", [P, 2, N]), ph.sb("hid", [P, 2, N])
        acc = ph.sb("acc", [P, G, D])

        w_in, ones_set = ph.sem("w_in"), ph.sem("ones_set")
        z_done, z_turned, z_t_done = ph.sem("z"), ph.sem("z_turned"), ph.sem("z_t")
        gated, gate_done, route = ph.sem("gated"), ph.sem("gate"), ph.sem("route_steps")
        w_turned, w_t_done = ph.sem("w_turned"), ph.sem("w_t")
        made1, made3, act1_done, hid_done = ph.sem("made1"), ph.sem("made3"), ph.sem("act1"), ph.sem("hid")
        made_y, used, x_done = ph.sem("made_y"), ph.sem("used"), ph.sem("x")
        tanh_g = chip.tanh_g[:, 5:6]
        PARTS = (5 + 2 * G, 6 + 2 * G, 7)
        STEPS = sum(PARTS)

        with nc.Block() as block:
            @block.sync
            def _(sp):
                for dst, name in ((wg[:, :], "l1_wg"), (b1[:, :], "l1_b1"), (b3[:, :], "l1_b3"), (b2[:, :], "l1_b2"),
                                  (earlier[:, :, :], "earlier4"), (w1[:, :, :], "l1_w1"), (w3[:, :, :], "l1_w3"),
                                  (w2[:, :, :], "l1_w2")):
                    sp.dma_start(dst, dram[name]).then_inc(w_in, DMA)

            @block.gpsimd
            def _(pool):
                pool.memset(ones[:, :], 1.0).then_inc(ones_set, 1)
                each_group(lambda i, h: ln.pool_rstd(pool, i), pool)

            @block.tensor
            def _(pe):
                pe.wait_ge(w_in, 8 * DMA)

                def turn(i, h):
                    pe.wait_ge(z_done, i * G + G)
                    reuse(pe, w_t_done, i)
                    transposes(pe, bank[0], [z[:, t, :] for t in range(G)], ident).then_inc(z_turned, 1)

                def router(i, h):
                    pe.wait_ge(z_t_done, i + 1)
                    for t in range(G):
                        mm = pe.matmul(bank[7][:, t * E:(t + 1) * E], z_t[:, h, t * P:(t + 1) * P], wg[:, :],
                                       start=True, stop=True)
                    mm.then_inc(gated, 1)

                def weights(i, h):
                    pe.wait_ge(route, (i + 1) * STEPS)
                    for t in range(G):
                        mm = pe.transpose(bank[0][0:E, t * P:(t + 1) * P], w[:, h, t, :], ident[:, :])
                    mm.then_inc(w_turned, 1)

                def front(i, h, *parts):
                    for part in parts or (turn, router, weights):
                        part(i, h)

                def hidden(i, h, e):
                    k = e % 2
                    reuse(pe, act1_done, i * E + e - 1)
                    pe.matmul(bank[1 + k][:, :], w1[:, e, :], z_t[:, h], start=True, stop=True).then_inc(made1, 1)
                    reuse(pe, hid_done, i * E + e - 1)
                    pe.matmul(bank[3 + k][:, :], w3[:, e, :], z_t[:, h], start=True, stop=True).then_inc(made3, 1)

                def outputs(i, h, e):
                    k = e % 2
                    pe.wait_ge(hid_done, i * E + e + 1)
                    reuse(pe, used, i * (E + 1) + e - 1)
                    for t in range(G):
                        mm = pe.matmul(bank[5 + k][:, t * D:(t + 1) * D], hid[:, k, t * P:(t + 1) * P], w2[:, e, :],
                                       start=True, stop=True)
                    mm.then_inc(made_y, 1)

                def main(i, h, nxt):
                    hidden(i, h, 0)
                    for e in range(E):
                        if e + 1 < E:
                            hidden(i, h, e + 1)
                        outputs(i, h, e)
                        for at, part in ((5, turn), (7, router), (E - 1, weights)):
                            if e == at:
                                nxt(part)
                    pe.wait_ge(w_t_done, i + 1)
                    reuse(pe, used, i * (E + 1) + E - 1)
                    for t in range(G):
                        mm = pe.matmul(bank[5][:, t * D:(t + 1) * D], w_t[:, h, t * P:(t + 1) * P], b2[:, :],
                                       start=True, stop=True)
                    mm.then_inc(made_y, 1)
                over_groups(front, main, pe)

            @block.scalar
            def _(act):
                act.wait_ge(w_in, 8 * DMA)

                def z_out(i, h):
                    act.wait_ge(z_turned, i + 1)
                    act.activation(z_t[:, h], bank[0][:, :], ACT.Identity).then_inc(z_t_done, 1)

                def gates(i, h):
                    act.wait_ge(gated, i + 1)
                    act.activation(gate[:, :, :].rearrange("p t e -> p (t e)"), bank[7][:, 0:G * E], ACT.Sigmoid)\
                        .then_inc(gate_done, 1)

                def weights_out(i, h):
                    act.wait_ge(w_turned, i + 1)
                    act.activation(w_t[:, h], bank[0][0:E, :], ACT.Identity).then_inc(w_t_done, 1)

                def front(i, h, *parts):
                    for part in parts or (z_out, gates, weights_out):
                        part(i, h)

                def main(i, h, nxt):
                    for e in range(E):
                        act.wait_ge(made1, i * E + e + 1)
                        reuse(act, hid_done, i * E + e - 1)
                        act.activation(act1[:, e % 2], bank[1 + e % 2][:, :], ACT.Silu, bias=b1[:, e:e + 1])\
                            .then_inc(act1_done, 1)
                        for at, part in ((6, z_out), (8, gates), (E - 1, weights_out)):
                            if e == at:
                                nxt(part)
                over_groups(front, main, act)

            @block.vector
            def _(v):
                v.wait_ge(w_in, 8 * DMA)
                v.wait_ge(ones_set, 1)

                def norm(i, h):
                    ln.vector_stats(v, i, lambda t: tile_of(x_all, i, t))
                    ln.vector_apply(v, i, lambda t: tile_of(x_all, i, t), z, z_done)

                at = steps = 0

                def step(instruction):
                    nonlocal steps
                    steps += 1
                    instruction.then_inc(route, 1)

                def settled():
                    v.wait_ge(route, at + steps)

                def choose_groups(i, h):
                    nonlocal at, steps
                    at, steps = i * STEPS, 0
                    by_group = gate[:, :, :].rearrange("p t (g e) -> p t g e", g=EG)
                    v.wait_ge(gate_done, i + 1)
                    step(v.tensor_reduce(gtop[:, :, :], by_group, AX.X, ALU.max))
                    settled()
                    for t in range(G):
                        others = gtop[:, t, :].unsqueeze(1).to_broadcast([P, EG, EG])
                        own = gtop[:, t, :].unsqueeze(2).to_broadcast([P, EG, EG])
                        step(v.tensor_tensor(above[:, t * EG:(t + 1) * EG, :], others, own, ALU.is_gt))
                        step(v.tensor_tensor(tied[:, t * EG:(t + 1) * EG, :], others, own, ALU.is_equal))
                    settled()
                    step(v.tensor_tensor(tied[:, :, :].rearrange("p (t a) b -> p t a b", t=G),
                                         tied[:, :, :].rearrange("p (t a) b -> p t a b", t=G),
                                         earlier[:, :, :].unsqueeze(1).to_broadcast([P, G, EG, EG]), ALU.mult))
                    settled()
                    step(v.tensor_tensor(above[:, :, :], above[:, :, :], tied[:, :, :], ALU.add))
                    settled()
                    step(v.tensor_reduce(rank[:, :], above[:, :, :], AX.X, ALU.add))
                    settled()
                    step(v.tensor_scalar(gsel[:, :], rank[:, :], float(L1_TOPG), None, ALU.is_lt))
                    settled()
                    assert steps == PARTS[0]

                def choose_experts(i, h):
                    nonlocal at, steps
                    at, steps = i * STEPS, PARTS[0]
                    by_group = gate[:, :, :].rearrange("p t (g e) -> p t g e", g=EG)
                    wide = gsel[:, :].rearrange("p (t g) -> p t g", g=EG).unsqueeze(3).to_broadcast([P, G, EG, PER])
                    kept4 = kept[:, :, :].rearrange("p t (g e) -> p t g e", g=EG)
                    settled()
                    step(v.tensor_tensor(kept4, by_group, wide, ALU.mult))
                    settled()
                    step(v.tensor_tensor(kept4, kept4, wide, ALU.add))
                    settled()
                    step(v.tensor_scalar(kept[:, :, :], kept[:, :, :], -1.0, None, ALU.add))
                    wait_apart(v, route, at + steps, chip.passed["v"])
                    for t in range(G):
                        v.max(best8[:, t, :], kept[:, t, :]).then_inc(route, 1)
                    steps += G
                    settled()
                    fourth = best8[:, :, L1_TOPK - 1].unsqueeze(2).to_broadcast([P, G, E])
                    step(v.tensor_tensor(sel[:, :, :], kept[:, :, :], fourth, ALU.is_gt))
                    step(v.tensor_tensor(tie[:, :, :], kept[:, :, :], fourth, ALU.is_equal))
                    settled()
                    step(v.tensor_reduce(n_above[:, :], sel[:, :, :], AX.X, ALU.add))
                    for t in range(G):
                        v.tensor_tensor_scan(tie_no[:, t, :], ones[:, :], tie[:, t, :], 0.0, ALU.mult, ALU.add)\
                            .then_inc(route, 1)
                    steps += G
                    assert steps == PARTS[0] + PARTS[1]

                def weigh(i, h):
                    nonlocal at, steps
                    at, steps = i * STEPS, PARTS[0] + PARTS[1]
                    settled()
                    step(v.tensor_tensor(tie_no[:, :, :], tie_no[:, :, :], n_above[:, :].unsqueeze(2)
                                         .to_broadcast([P, G, E]), ALU.add))
                    settled()
                    step(v.scalar_tensor_tensor(out=tie[:, :, :], in0=tie_no[:, :, :], scalar=float(L1_TOPK),
                                                in1=tie[:, :, :], op0=ALU.is_le, op1=ALU.mult))
                    settled()
                    step(v.tensor_tensor(sel[:, :, :], sel[:, :, :], tie[:, :, :], ALU.add))
                    settled()
                    step(v.tensor_tensor(sel[:, :, :], sel[:, :, :], gate[:, :, :], ALU.mult))
                    settled()
                    step(v.tensor_reduce(wsum[:, :], sel[:, :, :], AX.X, ALU.add))
                    settled()
                    step(v.reciprocal(wsum[:, :], wsum[:, :]))
                    settled()
                    step(v.scalar_tensor_tensor(out=w[:, h], in0=sel[:, :, :], scalar=ROUTE_SCALE,
                                                in1=wsum[:, :].unsqueeze(2).to_broadcast([P, G, E]),
                                                op0=ALU.mult, op1=ALU.mult))
                    assert steps == STEPS

                def front(i, h, *parts):
                    for part in parts or (norm, choose_groups, choose_experts, weigh):
                        part(i, h)

                def gate_hidden(i, h, e):
                    k = e % 2
                    v.wait_ge(made3, i * E + e + 1)
                    v.wait_ge(act1_done, i * E + e + 1)
                    v.scalar_tensor_tensor(out=hid[:, k], in0=bank[3 + k][:, :], scalar=b3[:, e:e + 1],
                                           in1=act1[:, k], op0=ALU.add, op1=ALU.mult).then_inc(hid_done, 1)

                def add_output(i, h, e):
                    v.wait_ge(made_y, i * (E + 1) + e + 1)
                    reuse(v, used, i * (E + 1) + e)
                    for t in range(G):
                        y = bank[5 + e % 2][:, t * D:(t + 1) * D]
                        if e:
                            mm = v.scalar_tensor_tensor(out=acc[:, t, :], in0=y, scalar=w[:, h, t, e:e + 1],
                                                        in1=acc[:, t, :], op0=ALU.mult, op1=ALU.add)
                        else:
                            mm = v.tensor_scalar(acc[:, t, :], y, w[:, h, t, e:e + 1], None, ALU.mult)
                    mm.then_inc(used, 1)

                def main(i, h, nxt):
                    gate_hidden(i, h, 0)
                    for e in range(E):
                        if e + 1 < E:
                            gate_hidden(i, h, e + 1)
                        add_output(i, h, e)
                        for at_e, part in ((2, norm), (8, choose_groups), (10, choose_experts), (12, weigh)):
                            if e == at_e:
                                nxt(part)
                    v.wait_ge(made_y, (i + 1) * (E + 1))
                    v.wait_ge(used, i * (E + 1) + E)
                    v.tensor_tensor(acc[:, :, :].rearrange("p t d -> p (t d)"), acc[:, :, :]
                                    .rearrange("p t d -> p (t d)"), bank[5][:, :], ALU.add).then_inc(used, 1)
                    v.wait_ge(used, (i + 1) * (E + 1))
                    v.scalar_tensor_tensor(out=group_of(x_all, i), in0=acc[:, :, :], scalar=tanh_g,
                                           in1=group_of(x_all, i), op0=ALU.mult, op1=ALU.add).then_inc(x_done, 1)
                over_groups(front, main, v)


def cross_attention(chip, name, gate, masked_scores, after):
    nc, dram, x_all, bank, ident = chip.nc, chip.dram, chip.x_all, chip.bank, chip.ident
    F, J, JP = 2, HEADS // 2, HEADS // 4
    HP = HEADS // 2
    U, LEAD = G * F, 3
    scale = HD ** -0.5
    W = 2 * HD + 2
    with Phase(chip, name) as ph:
        ln = LayerNorm(ph, "ln")
        wq, wk, wv, wo = (ph.sb(n, [P, D]) for n in ("wq", "wk", "wv", "wo"))
        bk, bq, bv, bo = ph.sb("bk", [P, F]), ph.sb("bq", [P, F]), ph.sb("bv", [P, D // 2]), ph.sb("bo", [P, D])
        of_head, k_bias, q_bias = ph.sb("of_head", [P, J]), ph.sb("k_bias", [P, F, J]), ph.sb("q_bias", [P, F])
        ctx_t = ph.sb("ctx_t", [P, 2, N])
        z, z_t = ph.sb("z", [P, 2, G, D]), ph.sb("z_t", [P, N])
        q_blocks, k_heads = ph.sb("q_blocks", [P, 2, F, G, P]), ph.sb("k_heads", [P, 2, F, G, J, S])
        v_blocks = ph.sb("v_blocks", [P, 2, BG, HP, W])
        probs, top, probs_t = ph.sb("probs", [P, U, 512]), ph.sb("top", [P, U, J]), ph.sb("probs_t", [P, 2, JP, P])
        rsum, o, o_t = ph.sb("rsum", [P, 2, 2 * HP, 2]), ph.sb("o", [P, G, D]), ph.sb("o_t", [P, N])
        out = ph.sb("out", [P, G, D])

        w_in, blocks_set, qk_consts = ph.sem("w_in"), ph.sem("blocks_set"), ph.sem("qk_consts")
        ctx_in = [ph.sem("ctx_in0"), ph.sem("ctx_in1")]
        z_done, z_turned, z_t_done = ph.sem("z"), ph.sem("z_turned"), ph.sem("z_t")
        q_made, k_made, v_made = ph.sem("q_made"), ph.sem("k_made"), ph.sem("v_made")
        q_out, k_out, v_out = ph.sem("q_out"), ph.sem("k_out"), ph.sem("v_out")
        scored, capped, topped = ph.sem("scored"), ph.sem("capped"), ph.sem("topped")
        shifted, exped = ph.sem("shifted"), ph.sem("exped")
        p_turned, p_t_done, pv_done = ph.sem("p_turned"), ph.sem("p_t"), ph.sem("pv")
        rsum_done, o_done = ph.sem("rsum"), ph.sem("o")
        o_turned, o_t_done, projected = ph.sem("o_turned"), ph.sem("o_t"), ph.sem("projected")
        proj_out = ph.sem("proj_out")
        caps = masked_scores(ph, chip)
        tail = after(ph, chip)
        ctx_t_dram = dram["ctx_t"].rearrange("p (g n) -> p g n", g=GROUPS)
        tanh_g = chip.tanh_g[:, gate:gate + 1]
        half_rows = lambda b: slice(b * S, (b + 1) * S)

        with nc.Block() as block:
            @block.sync
            def _(sp):
                names = ((wq, "wq"), (wk, "wk"), (wv, "wv"), (wo, "wo"), (bk, "bk"), (bv, "bv"), (bo, "bo"), (bq, "bq"))
                for dst, what in names:
                    sp.dma_start(dst[:, :], dram[f"{name}_{what}"]).then_inc(w_in, DMA)
                sp.dma_start(of_head[:, :], dram["of_head"]).then_inc(w_in, DMA)
                caps.load(sp)
                tail.load(sp)

                def step(i, h):
                    reuse(sp, v_made, i - 1)
                    sp.dma_start(ctx_t[:, h], ctx_t_dram[:, bass.ds(i, 1), :].rearrange("p a n -> p (a n)"))\
                        .then_inc(ctx_in[h], DMA)
                each_group(step, sp)

            @block.gpsimd
            def _(pool):
                pool.memset(q_blocks[:, :, :, :, :], 0.0).then_inc(blocks_set, 1)
                pool.memset(v_blocks[:, :, :, :, :], 0.0).then_inc(blocks_set, 1)
                pool.wait_ge(blocks_set, 2)
                for j2 in range(2):
                    pool.memset(v_blocks[half_rows(j2), :, :, :, 2 * HD + j2], 1.0).then_inc(blocks_set, 1)

                def rstd(i, h):
                    ln.pool_rstd(pool, i)

                def shift(i, u):
                    pool.wait_ge(topped, i * U + u + 1)
                    row = probs[:, u].rearrange("p (j k) -> p j k", k=S)
                    pool.tensor_tensor(row, row, top[:, u, :].unsqueeze(2).to_broadcast([P, J, S]), ALU.subtract)\
                        .then_inc(shifted, 1)

                def lead(i, h):
                    for u in range(LEAD):
                        shift(i, u)

                def front(i, h, *parts):
                    for part in parts or (rstd, lead):
                        part(i, h)

                def main(i, h, nxt):
                    shift(i, 3)
                    nxt(rstd)
                    for u in range(4, U):
                        shift(i, u)
                    nxt(lead)
                    tail.pool(pool, i, h)
                over_groups(front, main, pool)

            @block.tensor
            def _(pe):
                pe.wait_ge(w_in, 9 * DMA)

                def halves_of(dst, w, src, done):
                    moving = src.rearrange("p (t b s) -> p t b s", t=G, b=2)
                    for b in range(2):
                        for f in range(F):
                            mm = pe.matmul(dst[half_rows(b), f * N // 2:(f + 1) * N // 2],
                                           w[:, f * S:(f + 1) * S], moving[:, :, b, :], start=True, stop=True)
                    mm.then_inc(done, 1)

                def turn_z(i, h):
                    pe.wait_ge(z_done, i * G + G)
                    transposes(pe, bank[6], [z[:, h, t, :] for t in range(G)], ident).then_inc(z_turned, 1)
                    pe.wait_ge(ctx_in[h], loads(i, h))
                    reuse(pe, v_out, i * 2)
                    halves_of(bank[7], wk, ctx_t[:, h], k_made)

                def make_q(i, h):
                    pe.wait_ge(z_t_done, i + 1)
                    halves_of(bank[6], wq, z_t[:, :], q_made)

                def make_v(i, h):
                    pe.wait_ge(k_out, (i + 1) * F * J)
                    for tb in range(BG):
                        for j2 in range(2):
                            mm = pe.matmul(bank[7][half_rows(j2), tb * S:(tb + 1) * S],
                                           ctx_t[:, h, tb * S:(tb + 1) * S],
                                           wv[:, :].rearrange("p (a j d) -> p j a d", j=2, d=HD)[:, j2],
                                           start=True, stop=True)
                    mm.then_inc(v_made, 1)

                def scores(i, h, u):
                    t, f = u // F, u % F
                    if u == 0:
                        pe.wait_ge(q_out, (i + 1) * 4)
                        pe.wait_ge(k_out, (i + 1) * F * J)
                    reuse(pe, capped, i * U + u - 1)
                    pe.matmul(bank[u % 2][:, :], q_blocks[:, h, f, t, :],
                              k_heads[:, h, f, t].rearrange("p j k -> p (j k)"), start=True, stop=True)\
                        .then_inc(scored, 1)

                def turn(i, u):
                    pe.wait_ge(exped, i * U + u + 1)
                    reuse(pe, p_t_done, i * U + u - 1)
                    transposes(pe, bank[2 + u % 2], [probs[:, u, a * P:(a + 1) * P] for a in range(JP)], ident)\
                        .then_inc(p_turned, 1)

                def values(i, h, u):
                    t, f = u // F, u % F
                    pe.wait_ge(p_t_done, i * U + u + 1)
                    if u == 0:
                        pe.wait_ge(v_out, i * 2 + 2)
                        reuse(pe, o_t_done, i)
                    if u == U // 2:
                        reuse(pe, proj_out, i)
                    for a in range(JP):
                        hp = f * JP + a
                        c = ((t % 2) * HP + hp) * W
                        for b in range(2):
                            mm = pe.matmul(bank[4 + t // 2][half_rows(b), c:c + W],
                                           probs_t[:, u % 2, a, half_rows(b)], v_blocks[:, h, t * 2 + b, hp, :],
                                           start=True, stop=True)
                    mm.then_inc(pv_done, 1)

                def front(i, h, *parts):
                    for part in parts or (turn_z, make_q, make_v, lead0, lead1, lead2):
                        part(i, h)
                lead0, lead1, lead2 = (lambda i, h, u=u: scores(i, h, u) for u in range(LEAD))

                def main(i, h, nxt):
                    for u in range(U):
                        turn(i, u)
                        if u:
                            values(i, h, u - 1)
                        if u + LEAD < U:
                            scores(i, h, u + LEAD)
                        if u == 2:
                            nxt(turn_z)
                        if u == 3:
                            nxt(make_q)
                        if u == 6:
                            nxt(make_v)
                    values(i, h, U - 1)
                    nxt(lead0, lead1)
                    pe.wait_ge(o_done, i * 2 + 2)
                    transposes(pe, bank[4], [o[:, t, :] for t in range(G)], ident).then_inc(o_turned, 1)
                    nxt(lead2)
                    pe.wait_ge(o_t_done, i + 1)
                    for t in range(G):
                        mm = pe.matmul(bank[5][:, t * D:(t + 1) * D], o_t[:, t * P:(t + 1) * P], wo[:, :],
                                       start=True, stop=True)
                    mm.then_inc(projected, 1)
                over_groups(front, main, pe)

            @block.scalar
            def _(act):
                act.wait_ge(w_in, 9 * DMA)
                act.wait_ge(qk_consts, 3)
                act.wait_ge(blocks_set, 4)

                def z_out(i, h):
                    act.wait_ge(z_turned, i + 1)
                    act.activation(z_t[:, :], bank[6][:, :], ACT.Identity).then_inc(z_t_done, 1)

                def q_parts(i, h):
                    act.wait_ge(q_made, i + 1)
                    reuse(act, scored, (i - 1) * U)
                    for b in range(2):
                        for f in range(F):
                            r = half_rows(b)
                            act.activation(q_blocks[r, h, f, :, b * S:(b + 1) * S],
                                           bank[6][r, f * N // 2:(f + 1) * N // 2].rearrange("p (t s) -> p t s", t=G),
                                           ACT.Identity, bias=q_bias[r, f:f + 1], scale=scale).then_inc(q_out, 1)

                def k_parts(i, h, heads):
                    if heads.start == 0:
                        act.wait_ge(k_made, i + 1)
                        reuse(act, scored, (i - 1) * U)
                    for j in heads:
                        for f in range(F):
                            act.activation(k_heads[:, h, f, :, j, :],
                                           bank[7][:, f * N // 2:(f + 1) * N // 2].rearrange("p (t s) -> p t s", t=G),
                                           ACT.Identity, bias=k_bias[:, f, j:j + 1], scale=of_head[:, j:j + 1])\
                                .then_inc(k_out, 1)
                k0, k1, k2, k3 = (lambda i, h, a=a: k_parts(i, h, range(a, a + 2)) for a in range(0, J, 2))

                def exp(i, u):
                    act.wait_ge(shifted, i * U + u + 1)
                    act.activation(probs[:, u], probs[:, u], ACT.Exp).then_inc(exped, 1)

                def turned(i, u):
                    act.wait_ge(p_turned, i * U + u + 1)
                    reuse(act, pv_done, i * U + u - 1)
                    act.activation(probs_t[:, u % 2].rearrange("p a q -> p (a q)"), bank[2 + u % 2][:, :],
                                   ACT.Identity).then_inc(p_t_done, 1)

                def lead(i, h):
                    for u in range(LEAD):
                        exp(i, u)

                def front(i, h, *parts):
                    for part in parts or (z_out, k0, k1, k2, k3, q_parts, lead):
                        part(i, h)

                def main(i, h, nxt):
                    for u in range(U):
                        turned(i, u)
                        if u + LEAD < U:
                            exp(i, u + LEAD)
                        if 2 <= u < 6:
                            nxt(*((z_out, k0), (k1,), (q_parts, k2), (k3,))[u - 2])
                    nxt(lambda i, h: exp(i, 0))
                    act.wait_ge(o_turned, i + 1)
                    act.activation(o_t[:, :], bank[4][:, :], ACT.Identity).then_inc(o_t_done, 1)
                    nxt(lambda i, h: exp(i, 1), lambda i, h: exp(i, 2))
                over_groups(front, main, act)

            @block.vector
            def _(v):
                v.wait_ge(w_in, 9 * DMA)
                v.wait_ge(blocks_set, 4)
                v.tensor_scalar(q_bias[:, :], bq[:, :], scale, None, ALU.mult).then_inc(qk_consts, 1)
                for f in range(F):
                    v.tensor_scalar(k_bias[:, f, :], of_head[:, :], bk[:, f:f + 1], None, ALU.mult).then_inc(qk_consts, 1)
                caps.vector_setup(v)
                tail.vector_setup(v)

                def stats(i, h):
                    ln.vector_stats(v, i, lambda t: tile_of(x_all, i, t))

                def apply(i, h):
                    ln.vector_apply(v, i, lambda t: tile_of(x_all, i, t), z[:, h], z_done)

                def value_rows(i, h):
                    v.wait_ge(v_made, i + 1)
                    reuse(v, pv_done, (i - 1) * U)
                    for j2 in range(2):
                        r = half_rows(j2)
                        v.tensor_tensor(v_blocks[r, h, :, :, j2 * HD:(j2 + 1) * HD],
                                        bank[7][r, :].rearrange("p (t a d) -> p t a d", t=BG, a=HP),
                                        bv[r, :].rearrange("p (a d) -> p a d", a=HP).unsqueeze(1)
                                        .to_broadcast([S, BG, HP, HD]), ALU.add).then_inc(v_out, 1)

                def cap(i, h, u):
                    n = i * U + u + 1
                    row = probs[:, u].rearrange("p (j k) -> p j k", k=S)
                    v.wait_ge(scored, n)
                    reuse(v, p_turned, (i - 1) * U + u + 1)
                    caps.vector(v, i, h, u // F, row, bank[u % 2][:, :].rearrange("p (j k) -> p j k", k=S), capped)
                    v.wait_ge(capped, n)
                    v.tensor_reduce(top[:, u, :], row, AX.X, ALU.max).then_inc(topped, 1)

                def lead(i, h):
                    caps.table(v, i, h)
                    for u in range(LEAD):
                        cap(i, h, u)

                def front(i, h, *parts):
                    for part in parts or (stats, apply, value_rows, lead):
                        part(i, h)

                def normalize(i, pair):
                    pv = bank[4 + pair][:, 0:2 * HP * W].rearrange("p (a w) -> p a w", w=W)
                    n = i * 2 + pair + 1
                    v.wait_ge(pv_done, i * U + (pair + 1) * U // 2)
                    v.reciprocal(rsum[:, pair], pv[:, :, 2 * HD:W]).then_inc(rsum_done, 1)
                    v.wait_ge(rsum_done, n)
                    v.tensor_tensor(o[:, 2 * pair:2 * pair + 2, :].rearrange("p t (a j d) -> p (t a) j d", a=HP, j=2),
                                    pv[:, :, 0:2 * HD].rearrange("p a (j d) -> p a j d", j=2),
                                    rsum[:, pair].unsqueeze(3).to_broadcast([P, 2 * HP, 2, HD]), ALU.mult)\
                        .then_inc(o_done, 1)

                def main(i, h, nxt):
                    cap(i, h, 3)
                    nxt(stats)
                    cap(i, h, 4)
                    nxt(apply)
                    cap(i, h, 5)
                    cap(i, h, 6)
                    normalize(i, 0)
                    cap(i, h, 7)
                    nxt(value_rows)
                    normalize(i, 1)
                    nxt(lead)
                    v.wait_ge(projected, i + 1)
                    v.tensor_tensor(out[:, :, :], bank[5][:, :].rearrange("p (t d) -> p t d", t=G),
                                    bo[:, :].unsqueeze(1).to_broadcast([P, G, D]), ALU.add).then_inc(proj_out, 1)
                    v.wait_ge(proj_out, i + 1)
                    tail.vector(v, i, h, out, z[:, h], tanh_g)
                over_groups(front, main, v)


class QueryKeyCaps:

    def __init__(self, ph, chip):
        self.chip = chip
        self.mask, self.maskf = ph.sb("mask", [P, S], I32), ph.sb("maskf", [P, S])
        self.cap = ph.sb("cap", [P, S])
        self.mask_in, self.cap_steps = ph.sem("mask_in"), ph.sem("cap_steps")

    def load(self, sp):
        sp.dma_start(self.mask[:, :], self.chip.dram["l2_mask"]).then_inc(self.mask_in, DMA)

    def vector_setup(self, v):
        v.wait_ge(self.mask_in, DMA)
        v.tensor_copy(self.maskf[:, :], self.mask[:, :]).then_inc(self.cap_steps, 1)
        v.wait_ge(self.cap_steps, 1)
        v.tensor_scalar(self.maskf[:, :], self.maskf[:, :], 0.0, None, ALU.is_equal).then_inc(self.cap_steps, 1)
        v.wait_ge(self.cap_steps, 2)
        v.tensor_scalar(self.cap[:, :], self.maskf[:, :], -BIG, BIG, ALU.mult, ALU.add).then_inc(self.cap_steps, 1)
        v.wait_ge(self.cap_steps, 3)
        v.scalar_tensor_tensor(out=self.cap[:, :], in0=self.maskf[:, :], scalar=-1e9, in1=self.cap[:, :],
                               op0=ALU.mult, op1=ALU.add).then_inc(self.cap_steps, 1)
        v.wait_ge(self.cap_steps, 4)

    def table(self, v, i, h):
        pass

    def vector(self, v, i, h, t, out, scores, capped):
        v.tensor_tensor(out, scores, self.cap[:, :].unsqueeze(1).to_broadcast([P, 8, S]), ALU.min).then_inc(capped, 1)


class PaddingCaps:

    def __init__(self, ph, chip):
        self.chip = chip
        self.mask = ph.sb("mask", [P, TILES * S], U8)
        self.maskf, self.cap = ph.sb("maskf", [P, G * S]), ph.sb("cap", [P, 2, G * S])
        self.mask_in, self.cap_steps = ph.sem("mask_in"), ph.sem("cap_steps")

    def load(self, sp):
        sp.dma_start(self.mask[:, :], self.chip.dram["l3_mask"]).then_inc(self.mask_in, DMA)

    def vector_setup(self, v):
        v.wait_ge(self.mask_in, DMA)

    def table(self, v, i, h):
        v.tensor_scalar(self.maskf[:, :], self.mask[:, bass.ds(i * G * S, G * S)], 1.0, None, ALU.min)\
            .then_inc(self.cap_steps, 1)
        v.wait_ge(self.cap_steps, i * 4 + 1)
        v.tensor_scalar(self.cap[:, h], self.maskf[:, :], -BIG, BIG, ALU.mult, ALU.add).then_inc(self.cap_steps, 1)
        for k in range(2):
            v.wait_ge(self.cap_steps, i * 4 + 2 + k)
            v.scalar_tensor_tensor(out=self.cap[:, h], in0=self.maskf[:, :], scalar=-BIG, in1=self.cap[:, h],
                                   op0=ALU.mult, op1=ALU.add).then_inc(self.cap_steps, 1)
        v.wait_ge(self.cap_steps, i * 4 + 4)

    def vector(self, v, i, h, t, out, scores, capped):
        v.tensor_tensor(out, scores, self.cap[:, h, t * S:(t + 1) * S].unsqueeze(1).to_broadcast([P, 8, S]),
                        ALU.min).then_inc(capped, 1)


class AddToX:

    def __init__(self, ph, chip):
        self.chip, self.x_done = chip, ph.sem("x")

    def load(self, sp):
        pass

    def vector_setup(self, v):
        pass

    def pool(self, pool, i, h):
        pass

    def vector(self, v, i, h, out, z, tanh_g):
        x = self.chip.x_all
        v.scalar_tensor_tensor(out=group_of(x, i), in0=out[:, :, :], scalar=tanh_g, in1=group_of(x, i),
                               op0=ALU.mult, op1=ALU.add).then_inc(self.x_done, 1)


def l2_ffn(chip):
    nc, dram, x_all, bank, ident = chip.nc, chip.dram, chip.x_all, chip.bank, chip.ident
    E, C = L2_E, L2_H // P
    with Phase(chip, "l2ffn") as ph:
        ln, ln2 = LayerNorm(ph, "ln"), LayerNorm(ph, "ln2")
        w1, w2 = ph.sb("w1", [P, E, L2_H]), ph.sb("w2", [P, E, C, D])
        wr, gamma, beta = ph.sb("wr", [P, E]), ph.sb("gamma", [P, D]), ph.sb("beta", [P, D])
        n, z, z_t = ph.sb("n", [P, 2, G, D]), ph.sb("z", [P, G, D]), ph.sb("z_t", [P, 2, N])
        best, rsum = ph.sb("best", [P, G]), ph.sb("rsum", [P, G])
        prob, best8 = ph.sb("prob", [P, G, E]), ph.sb("best8", [P, G, 8])
        sel, tie, tie_no, n_above = (ph.sb("sel", [P, G, E]), ph.sb("tie", [P, G, E]), ph.sb("tie_no", [P, G, E]),
                                     ph.sb("n_above", [P, G]))
        ones, w = ph.sb("ones", [P, E]), ph.sb("w", [P, 2, G, E])
        hid, acc = ph.sb("hid", [P, 2, C, N]), ph.sb("acc", [P, G, D])
        w_in, ones_set = ph.sem("w_in"), ph.sem("ones_set")
        n_done, z_norm, z_done = ph.sem("n"), ph.sem("z_norm"), ph.sem("z")
        z_turned, z_t_done, gated = ph.sem("z_turned"), ph.sem("z_t"), ph.sem("gated")
        route, prob_done = ph.sem("route_steps"), ph.sem("prob")
        made_h, hid_done, made_y, used, x_done = (ph.sem("made_h"), ph.sem("hid"), ph.sem("made_y"), ph.sem("used"),
                                                  ph.sem("x"))
        tanh_g = chip.tanh_g[:, 6:7]
        PARTS = (2, 5 + 2 * G, 5)
        STEPS = sum(PARTS)
        row = lambda ap: ap[:, :].unsqueeze(1).to_broadcast([P, G, D])

        with nc.Block() as block:
            @block.sync
            def _(sp):
                for dst, name in ((wr[:, :], "l2_wr"), (gamma[:, :], "l2_gamma"), (beta[:, :], "l2_beta"),
                                  (w1[:, :, :], "l2_w1"), (w2[:, :, :, :], "l2_w2")):
                    sp.dma_start(dst, dram[name]).then_inc(w_in, DMA)

            @block.gpsimd
            def _(pool):
                pool.memset(ones[:, :], 1.0).then_inc(ones_set, 1)

                def step(i, h):
                    ln.pool_rstd(pool, i)
                    ln2.pool_rstd(pool, i)
                each_group(step, pool)

            @block.tensor
            def _(pe):
                pe.wait_ge(w_in, 5 * DMA)

                def turn(i, h):
                    pe.wait_ge(z_done, i + 1)
                    transposes(pe, bank[0], [z[:, t, :] for t in range(G)], ident).then_inc(z_turned, 1)

                def router(i, h):
                    pe.wait_ge(z_t_done, i + 1)
                    reuse(pe, route, (i - 1) * STEPS + 2)
                    for t in range(G):
                        mm = pe.matmul(bank[7][:, t * E:(t + 1) * E], z_t[:, h, t * P:(t + 1) * P], wr[:, :],
                                       start=True, stop=True)
                    mm.then_inc(gated, 1)

                def front(i, h, *parts):
                    for part in parts or (turn, router):
                        part(i, h)

                def hidden(i, h, e):
                    for c in range(C):
                        use = (i * E + e) * C + c
                        reuse(pe, hid_done, use - 3)
                        pe.matmul(bank[1 + c][:, :], w1[:, e, c * P:(c + 1) * P], z_t[:, h], start=True, stop=True)\
                            .then_inc(made_h, 1)

                def outputs(i, h, e):
                    pe.wait_ge(hid_done, (i * E + e + 1) * C)
                    reuse(pe, used, i * E + e - 1)
                    for t in range(G):
                        for c in range(C):
                            mm = pe.matmul(bank[5 + e % 2][:, t * D:(t + 1) * D],
                                           hid[:, e % 2, c, t * P:(t + 1) * P], w2[:, e, c, :],
                                           start=(c == 0), stop=(c == C - 1))
                    mm.then_inc(made_y, 1)

                def main(i, h, nxt):
                    hidden(i, h, 0)
                    for e in range(E):
                        if e + 1 < E:
                            hidden(i, h, e + 1)
                        outputs(i, h, e)
                        for at, part in ((3, turn), (4, router)):
                            if e == at:
                                nxt(part)
                over_groups(front, main, pe)

            @block.scalar
            def _(act):
                def z_out(i, h):
                    act.wait_ge(z_turned, i + 1)
                    act.activation(z_t[:, h], bank[0][:, :], ACT.Identity).then_inc(z_t_done, 1)

                def exps(i, h):
                    act.wait_ge(route, i * STEPS + 2)
                    act.activation(prob[:, :, :], prob[:, :, :], ACT.Exp, scale=1.0 / L2_TEMP).then_inc(prob_done, 1)

                def front(i, h, *parts):
                    for part in parts or (z_out, exps):
                        part(i, h)

                def main(i, h, nxt):
                    for e in range(E):
                        for c in range(C):
                            act.wait_ge(made_h, (i * E + e) * C + c + 1)
                            if c == 0:
                                reuse(act, made_y, i * E + e - 1)
                            act.activation(hid[:, e % 2, c], bank[1 + c][:, :], ACT.Silu).then_inc(hid_done, 1)
                        for at, part in ((4, z_out), (5, exps)):
                            if e == at:
                                nxt(part)
                over_groups(front, main, act)

            @block.vector
            def _(v):
                v.wait_ge(w_in, 5 * DMA)
                v.wait_ge(ones_set, 1)
                at = steps = 0

                def step(instruction):
                    nonlocal steps
                    steps += 1
                    instruction.then_inc(route, 1)

                def settled():
                    v.wait_ge(route, at + steps)

                def norm(i, h):
                    ln.vector_stats(v, i, lambda t: tile_of(x_all, i, t))
                    ln.vector_apply(v, i, lambda t: tile_of(x_all, i, t), n[:, h], n_done)
                    wait_apart(v, n_done, i * G + G, chip.passed["v"])
                    ln2.vector_stats(v, i, lambda t: n[:, h, t, :])

                def norm_again(i, h):
                    ln2.vector_apply(v, i, lambda t: n[:, h, t, :], z, z_norm)
                    v.wait_ge(z_norm, i * (G + 1) + G)
                    v.tensor_tensor(z[:, :, :], z[:, :, :], row(gamma), ALU.mult).then_inc(z_norm, 1)
                    v.wait_ge(z_norm, (i + 1) * (G + 1))
                    v.tensor_tensor(z[:, :, :], z[:, :, :], row(beta), ALU.add).then_inc(z_done, 1)

                def shift(i, h):
                    nonlocal at, steps
                    at, steps = i * STEPS, 0
                    logits = bank[7][:, 0:G * E].rearrange("p (t e) -> p t e", t=G)
                    v.wait_ge(gated, i + 1)
                    step(v.tensor_reduce(best[:, :], logits, AX.X, ALU.max))
                    settled()
                    step(v.tensor_tensor(prob[:, :, :], logits, best[:, :].unsqueeze(2).to_broadcast([P, G, E]),
                                         ALU.subtract))

                def choose(i, h):
                    nonlocal at, steps
                    at, steps = i * STEPS, PARTS[0]
                    wait_apart(v, prob_done, i + 1, chip.passed["v"])
                    for t in range(G):
                        step(v.max(best8[:, t, :], prob[:, t, :]))
                    settled()
                    second = best8[:, :, 1].unsqueeze(2).to_broadcast([P, G, E])
                    step(v.tensor_tensor(sel[:, :, :], prob[:, :, :], second, ALU.is_gt))
                    step(v.tensor_tensor(tie[:, :, :], prob[:, :, :], second, ALU.is_equal))
                    settled()
                    step(v.tensor_reduce(n_above[:, :], sel[:, :, :], AX.X, ALU.add))
                    step(v.tensor_reduce(rsum[:, :], prob[:, :, :], AX.X, ALU.add))
                    for t in range(G):
                        step(v.tensor_tensor_scan(tie_no[:, t, :], ones[:, :], tie[:, t, :], 0.0, ALU.mult, ALU.add))
                    settled()
                    step(v.reciprocal(rsum[:, :], rsum[:, :]))

                def weigh(i, h):
                    nonlocal at, steps
                    at, steps = i * STEPS, PARTS[0] + PARTS[1]
                    step(v.tensor_tensor(tie_no[:, :, :], tie_no[:, :, :], n_above[:, :].unsqueeze(2)
                                         .to_broadcast([P, G, E]), ALU.add))
                    settled()
                    step(v.scalar_tensor_tensor(out=tie[:, :, :], in0=tie_no[:, :, :], scalar=2.0,
                                                in1=tie[:, :, :], op0=ALU.is_le, op1=ALU.mult))
                    settled()
                    step(v.tensor_tensor(sel[:, :, :], sel[:, :, :], tie[:, :, :], ALU.add))
                    settled()
                    step(v.tensor_tensor(sel[:, :, :], sel[:, :, :], prob[:, :, :], ALU.mult))
                    settled()
                    step(v.tensor_tensor(w[:, h], sel[:, :, :], rsum[:, :].unsqueeze(2).to_broadcast([P, G, E]),
                                         ALU.mult))
                    assert steps == STEPS

                def front(i, h, *parts):
                    for part in parts or (norm, norm_again, shift, choose, weigh):
                        part(i, h)

                def main(i, h, nxt):
                    for e in range(E):
                        v.wait_ge(made_y, i * E + e + 1)
                        if e == 0:
                            v.wait_ge(route, (i + 1) * STEPS)
                            reuse(v, x_done, i)
                        else:
                            v.wait_ge(used, i * E + e)
                        for t in range(G):
                            mm = v.scalar_tensor_tensor(
                                out=acc[:, t, :], in0=bank[5 + e % 2][:, t * D:(t + 1) * D], scalar=w[:, h, t, e:e + 1],
                                in1=acc[:, t, :] if e else n[:, h, t, :], op0=ALU.mult, op1=ALU.add)
                        mm.then_inc(used, 1)
                        for at_e, part in ((0, norm), (1, norm_again), (4, shift), (5, choose), (6, weigh)):
                            if e == at_e:
                                nxt(part)
                    v.wait_ge(used, (i + 1) * E)
                    v.scalar_tensor_tensor(out=group_of(x_all, i), in0=acc[:, :, :], scalar=tanh_g,
                                           in1=group_of(x_all, i), op0=ALU.mult, op1=ALU.add).then_inc(x_done, 1)
                over_groups(front, main, v)


class NormToY:

    def __init__(self, ph, chip, y_all):
        self.chip, self.y_all = chip, y_all
        self.ln = LayerNorm(ph, "ln1")
        self.gain, self.bias = ph.sb("ln1_g", [P, D]), ph.sb("ln1_b", [P, D])
        self.normed = ph.sb("normed", [P, G, D])
        self.gain_in, self.res_done, self.normed_done = ph.sem("gain_in"), ph.sem("res"), ph.sem("normed")
        self.gained, self.y_done = ph.sem("gained"), ph.sem("y")

    def load(self, sp):
        sp.dma_start(self.gain[:, :], self.chip.dram["l3_ln1_g"]).then_inc(self.gain_in, DMA)
        sp.dma_start(self.bias[:, :], self.chip.dram["l3_ln1_b"]).then_inc(self.gain_in, DMA)

    def vector_setup(self, v):
        v.wait_ge(self.gain_in, 2 * DMA)

    def pool(self, pool, i, h):
        self.ln.pool_rstd(pool, i)

    def vector(self, v, i, h, out, z, tanh_g):
        row = lambda ap: ap[:, :].unsqueeze(1).to_broadcast([P, G, D])
        v.tensor_tensor(out[:, :, :], out[:, :, :], z, ALU.add).then_inc(self.res_done, 1)
        wait_apart(v, self.res_done, i + 1, self.chip.passed["v"])
        self.ln.vector_stats(v, i, lambda t: out[:, t, :])
        self.ln.vector_apply(v, i, lambda t: out[:, t, :], self.normed, self.normed_done)
        v.wait_ge(self.normed_done, i * G + G)
        v.tensor_tensor(self.normed[:, :, :], self.normed[:, :, :], row(self.gain), ALU.mult).then_inc(self.gained, 1)
        v.wait_ge(self.gained, i + 1)
        v.tensor_tensor(group_of(self.y_all, i), self.normed[:, :, :], row(self.bias), ALU.add)\
            .then_inc(self.y_done, 1)


def l3_mlp(chip, y_all):
    nc, dram, x_all, bank, ident = chip.nc, chip.dram, chip.x_all, chip.bank, chip.ident
    C = FFN // P
    with Phase(chip, "l3mlp") as ph:
        ln = LayerNorm(ph, "ln")
        w1, w2, b1 = ph.sb("w1", [P, FFN]), ph.sb("w2", [P, C, D]), ph.sb("b1", [P, C])
        b2, ln_g, ln_b = ph.sb("b2", [P, D]), ph.sb("ln_g", [P, D]), ph.sb("ln_b", [P, D])
        y, y_t, hid = ph.sb("y", [P, 2, G, D]), ph.sb("y_t", [P, 2, N]), ph.sb("hid", [P, C, N])
        res, normed = ph.sb("res", [P, G, D]), ph.sb("normed", [P, G, D])
        w_in, affine = ph.sem("w_in"), ph.sem("affine")
        y_done, y_turned, y_t_done = ph.sem("y"), ph.sem("y_turned"), ph.sem("y_t")
        made_h, hid_done, made_o, res_done = ph.sem("made_h"), ph.sem("hid"), ph.sem("made_o"), ph.sem("res")
        normed_done, gained, moved, x_done = ph.sem("normed"), ph.sem("gained"), ph.sem("moved"), ph.sem("x")
        tanh_g = chip.tanh_g[:, 3:4]
        row = lambda ap: ap[:, :].unsqueeze(1).to_broadcast([P, G, D])

        with nc.Block() as block:
            @block.sync
            def _(sp):
                for dst, name in ((w1[:, :], "l3_w1"), (w2[:, :, :], "l3_w2"), (b1[:, :], "l3_b1"),
                                  (b2[:, :], "l3_b2"), (ln_g[:, :], "l3_ln2_g"), (ln_b[:, :], "l3_ln2_b")):
                    sp.dma_start(dst, dram[name]).then_inc(w_in, DMA)

            @block.gpsimd
            def _(pool):
                def front(i, h):
                    reuse(pool, res_done, (i - 1) * 2)
                    pool.tensor_copy(y[:, h], group_of(y_all, i)).then_inc(y_done, 1)

                def main(i, h, nxt):
                    nxt()
                    ln.pool_rstd(pool, i)
                over_groups(front, main, pool)

            @block.tensor
            def _(pe):
                pe.wait_ge(w_in, 6 * DMA)

                def front(i, h):
                    pe.wait_ge(y_done, i + 1)
                    transposes(pe, bank[h], [y[:, h, t, :] for t in range(G)], ident).then_inc(y_turned, 1)

                def main(i, h, nxt):
                    pe.wait_ge(y_t_done, i + 1)
                    for c in range(C):
                        reuse(pe, hid_done, i * C + c - 3)
                        pe.matmul(bank[2 + c][:, :], w1[:, c * P:(c + 1) * P], y_t[:, h], start=True, stop=True)\
                            .then_inc(made_h, 1)
                    nxt()
                    pe.wait_ge(hid_done, i * C + C)
                    reuse(pe, res_done, (i - 1) * 2)
                    for t in range(G):
                        for c in range(C):
                            mm = pe.matmul(bank[6 + h][:, t * D:(t + 1) * D], hid[:, c, t * P:(t + 1) * P],
                                           w2[:, c, :], start=(c == 0), stop=(c == C - 1))
                    mm.then_inc(made_o, 1)
                over_groups(front, main, pe)

            @block.scalar
            def _(act):
                act.wait_ge(w_in, 6 * DMA)

                def front(i, h):
                    act.wait_ge(y_turned, i + 1)
                    act.activation(y_t[:, h], bank[h][:, :], ACT.Identity).then_inc(y_t_done, 1)

                def main(i, h, nxt):
                    reuse(act, made_o, i)
                    for c in range(C):
                        act.wait_ge(made_h, i * C + c + 1)
                        act.activation(hid[:, c], bank[2 + c][:, :], ACT.Gelu, bias=b1[:, c:c + 1])\
                            .then_inc(hid_done, 1)
                    nxt()
                over_groups(front, main, act)

            @block.vector
            def _(v):
                v.wait_ge(w_in, 6 * DMA)
                v.tensor_scalar(ln_g[:, :], ln_g[:, :], tanh_g, None, ALU.mult).then_inc(affine, 1)
                v.tensor_scalar(ln_b[:, :], ln_b[:, :], tanh_g, None, ALU.mult).then_inc(affine, 1)
                v.wait_ge(affine, 2)

                def step(i, h):
                    v.wait_ge(made_o, i + 1)
                    v.tensor_tensor(res[:, :, :], bank[6 + h][:, :].rearrange("p (t d) -> p t d", t=G), row(b2),
                                    ALU.add).then_inc(res_done, 1)
                    v.wait_ge(res_done, i * 2 + 1)
                    v.tensor_tensor(res[:, :, :], res[:, :, :], y[:, h], ALU.add).then_inc(res_done, 1)
                    wait_apart(v, res_done, i * 2 + 2, chip.passed["v"])
                    ln.vector_stats(v, i, lambda t: res[:, t, :])
                    ln.vector_apply(v, i, lambda t: res[:, t, :], normed, normed_done)
                    v.wait_ge(normed_done, i * G + G)
                    v.tensor_tensor(normed[:, :, :], normed[:, :, :], row(ln_g), ALU.mult).then_inc(gained, 1)
                    v.wait_ge(gained, i + 1)
                    v.tensor_tensor(normed[:, :, :], normed[:, :, :], row(ln_b), ALU.add).then_inc(moved, 1)
                    v.wait_ge(moved, i + 1)
                    v.tensor_tensor(group_of(x_all, i), normed[:, :, :], group_of(x_all, i), ALU.add)\
                        .then_inc(x_done, 1)
                each_group(step, v)


def l3_tree(chip):
    nc, dram, x_all, bank, ident = chip.nc, chip.dram, chip.x_all, chip.bank, chip.ident
    NODES, C = LEAVES - 1, LEAVES // P
    with Phase(chip, "l3tree") as ph:
        ln = LayerNorm(ph, "ln")
        wq, rt, vt, wo = ph.sb("wq", [P, D]), ph.sb("rt", [P, NODES]), ph.sb("vt", [P, LEAVES]), ph.sb("wo", [P, D])
        wr, vo, bo = ph.sb("wr", [P, LEAVES]), ph.sb("vo", [P, C, D]), ph.sb("bo", [P, D])
        z, z_t = ph.sb("z", [P, G, D]), ph.sb("z_t", [P, 2, N])
        gate, lp = ph.sb("gate", [P, 2, G, LEAVES]), ph.sb("lp", [P, 2, G, LEAVES])
        lp_t, out, x_out = ph.sb("lp_t", [P, C, N]), ph.sb("out", [P, G, D]), ph.sb("x_out", [P, 2, G, D])
        w_in, merged, merged_out = ph.sem("w_in"), ph.sem("merged"), ph.sem("merged_out")
        z_done, z_turned, z_t_done = ph.sem("z"), ph.sem("z_turned"), ph.sem("z_t")
        gated, gate_done, levels = ph.sem("gated"), ph.sem("gate"), ph.sem("levels")
        lp_turned, lp_t_done, summed, biased, x_done = (ph.sem("lp_turned"), ph.sem("lp_t"), ph.sem("summed"),
                                                        ph.sem("biased"), ph.sem("x"))
        stored = [ph.sem("stored0"), ph.sem("stored1")]
        out_dram = dram["out"].rearrange("(n p) d -> p n d", p=P)
        tanh_g = chip.tanh_g[:, 7:8]
        DEPTH = LEAVES.bit_length() - 1
        STEPS = 2 * DEPTH

        with nc.Block() as block:
            @block.sync
            def _(sp):
                for dst, name in ((wq, "l3_tq"), (rt, "l3_rt"), (vt, "l3_vt"), (wo, "l3_two"), (bo, "l3_tbo")):
                    sp.dma_start(dst[:, :], dram[name]).then_inc(w_in, DMA)

                def step(i, h):
                    sp.wait_ge(x_done, i + 1)
                    sp.dma_start(group_of(out_dram, i), x_out[:, h]).then_inc(stored[h], DMA)
                each_group(step, sp)
                for h in range(2):
                    sp.wait_ge(stored[h], loads(GROUPS - 2 + h, h))

            @block.gpsimd
            def _(pool):
                each_group(lambda i, h: ln.pool_rstd(pool, i), pool)

            @block.tensor
            def _(pe):
                pe.wait_ge(w_in, 5 * DMA)
                pe.matmul(bank[0][:, 0:NODES], wq[:, :], rt[:, :], start=True, stop=True).then_inc(merged, 1)
                for c in range(C):
                    mm = pe.matmul(bank[1][:, c * D:(c + 1) * D], vt[:, c * P:(c + 1) * P], wo[:, :],
                                   start=True, stop=True)
                mm.then_inc(merged, 1)
                pe.wait_ge(merged_out, 2)

                def front(i, h):
                    pe.wait_ge(z_done, i * G + G)
                    transposes(pe, bank[0], [z[:, t, :] for t in range(G)], ident).then_inc(z_turned, 1)
                    pe.wait_ge(z_t_done, i + 1)
                    reuse(pe, gate_done, i * 2)
                    for t in range(G):
                        c = (t % 2) * LEAVES
                        mm = pe.matmul(bank[1 + t // 2][:, c:c + NODES], z_t[:, h, t * P:(t + 1) * P],
                                       wr[:, 0:NODES], start=True, stop=True)
                        if t % 2:
                            mm.then_inc(gated, 1)

                def main(i, h, nxt):
                    pe.wait_ge(levels, (i + 1) * STEPS)
                    reuse(pe, lp_t_done, i * C)
                    for c in range(C):
                        transposes(pe, bank[3 + c], [lp[:, 1, t, c * P:(c + 1) * P] for t in range(G)], ident)\
                            .then_inc(lp_turned, 1)
                    nxt()
                    pe.wait_ge(lp_t_done, i * C + C)
                    reuse(pe, biased, i)
                    for t in range(G):
                        for c in range(C):
                            mm = pe.matmul(bank[5][:, t * D:(t + 1) * D], lp_t[:, c, t * P:(t + 1) * P], vo[:, c, :],
                                           start=(c == 0), stop=(c == C - 1))
                    mm.then_inc(summed, 1)
                over_groups(front, main, pe)

            @block.scalar
            def _(act):
                def front(i, h):
                    act.wait_ge(z_turned, i + 1)
                    act.activation(z_t[:, h], bank[0][:, :], ACT.Identity).then_inc(z_t_done, 1)
                    for b in range(2):
                        act.wait_ge(gated, i * 2 + b + 1)
                        act.activation(gate[:, h, 2 * b:2 * b + 2, 0:NODES],
                                       bank[1 + b][:, :].rearrange("p (t m) -> p t m", t=2)[:, :, 0:NODES],
                                       ACT.Sigmoid).then_inc(gate_done, 1)

                def main(i, h, nxt):
                    for c in range(C):
                        act.wait_ge(lp_turned, i * C + c + 1)
                        act.activation(lp_t[:, c], bank[3 + c][:, :], ACT.Identity).then_inc(lp_t_done, 1)
                    nxt()
                over_groups(front, main, act)

            @block.vector
            def _(v):
                v.wait_ge(merged, 2)
                v.tensor_copy(wr[:, 0:NODES], bank[0][:, 0:NODES]).then_inc(merged_out, 1)
                v.tensor_copy(vo[:, :, :].rearrange("p c d -> p (c d)"), bank[1][:, 0:C * D]).then_inc(merged_out, 1)

                def front(i, h):
                    ln.vector_stats(v, i, lambda t: tile_of(x_all, i, t))
                    ln.vector_apply(v, i, lambda t: tile_of(x_all, i, t), z, z_done)

                def main(i, h, nxt):
                    v.wait_ge(gate_done, i * 2 + 2)
                    reuse(v, lp_turned, i * C)
                    for level in range(DEPTH):
                        n = 1 << level
                        src, dst = lp[:, level % 2], lp[:, (level + 1) % 2]
                        if DEPTH % 2 == 0:
                            src, dst = lp[:, (level + 1) % 2], lp[:, level % 2]
                        kids = dst[:, :, 0:2 * n].rearrange("p t (a k) -> p t a k", k=2)
                        g = gate[:, h, :, n - 1:2 * n - 1]
                        if level == 0:
                            v.tensor_scalar(kids[:, :, :, 1], g, 1.0, None, ALU.mult).then_inc(levels, 1)
                            v.tensor_scalar(kids[:, :, :, 0], g, -1.0, 1.0, ALU.mult, ALU.add).then_inc(levels, 1)
                            continue
                        v.wait_ge(levels, i * STEPS + 2 * level)
                        v.tensor_tensor(kids[:, :, :, 1], src[:, :, 0:n], g, ALU.mult).then_inc(levels, 1)
                        v.wait_ge(levels, i * STEPS + 2 * level + 1)
                        v.tensor_tensor(kids[:, :, :, 0], src[:, :, 0:n], kids[:, :, :, 1], ALU.subtract)\
                            .then_inc(levels, 1)
                    nxt()
                    v.wait_ge(summed, i + 1)
                    v.tensor_tensor(out[:, :, :], bank[5][:, :].rearrange("p (t d) -> p t d", t=G),
                                    bo[:, :].unsqueeze(1).to_broadcast([P, G, D]), ALU.add).then_inc(biased, 1)
                    reuse(v, stored[h], loads(i - 2, h))
                    v.wait_ge(biased, i + 1)
                    v.scalar_tensor_tensor(out=x_out[:, h], in0=out[:, :, :], scalar=tanh_g,
                                           in1=group_of(x_all, i), op0=ALU.mult, op1=ALU.add).then_inc(x_done, 1)
                over_groups(front, main, v)


def load_x(chip, name):
    view = chip.dram[name].rearrange("(n p) d -> p n d", p=P)
    with Phase(chip, f"load_{name}") as ph:
        loaded = ph.sem("loaded")
        with chip.nc.Block() as block:
            @block.sync
            def _(sp):
                for i in range(2):
                    half = slice(i * TILES // 2, (i + 1) * TILES // 2)
                    sp.dma_start(chip.x_all[:, half], view[:, half]).then_inc(loaded, DMA)
                sp.wait_ge(loaded, 2 * DMA)


def build(nc, dram):
    with ExitStack() as ctx:
        chip = Chip(nc, ctx, dram)
        constants(chip)
        l0_mix(chip)
        with ExitStack() as l0:
            y1_all = l0.enter_context(nc.sbuf_tensor("y1_all", [P, TILES, D], F32))
            logits = l0.enter_context(nc.sbuf_tensor("l0_logits", [P, TILES, L0_E], F32))
            weight = l0.enter_context(nc.sbuf_tensor("l0_weight", [P, TILES, L0_E], F32))
            l0_attention(chip, y1_all, logits)
            l0_route(chip, logits, weight)
            l0_experts(chip, y1_all, weight)
        load_x(chip, "x2")
        l1_mix(chip)
        l1_ffn(chip)
        cross_attention(chip, "l2", 2, QueryKeyCaps, AddToX)
        l2_ffn(chip)
        with nc.sbuf_tensor("y_all", [P, TILES, D], F32) as y_all:
            cross_attention(chip, "l3", 3, PaddingCaps, lambda ph, c: NormToY(ph, c, y_all))
            l3_mlp(chip, y_all)
        l3_tree(chip)


def layouts(i):
    rows = lambda a: np.broadcast_to(np.asarray(a).reshape(1, -1), (P, np.asarray(a).size))
    cols = lambda a: np.asarray(a).reshape(-1, P).T
    halves = lambda a: np.concatenate([np.asarray(a).reshape(2, S).T] * 2)
    by_parity = lambda a: np.repeat(np.asarray(a).reshape(HEADS // 2, 2, HD).transpose(1, 0, 2).reshape(2, -1), S, axis=0)
    s = np.arange(P)
    age = s[None, :] - s[:, None]
    same = (s[None, :] // S) == (s[:, None] // S)
    out = {
        "x": i["x"].reshape(TOKENS, D),
        "ctx": i["ctx_1024"].reshape(TOKENS, D),
        "ctx_t": i["ctx_1024"].reshape(TOKENS, D).T,
        "g_xattn": rows(i["g_xattn"]),
        "g_ffn": rows(i["g_ffn"]),
        "ident": np.eye(P, dtype=np.float32),
        "later": (s[:, None] < s[None, :]).astype(np.float32),
        "l0_first": rows(np.arange(L0_E, 0, -1, dtype=np.float32)),
        "l0_wqkv": i["L0_ffn_in_proj_w"].T,
        "l0_b_cols": cols(i["L0_ffn_in_proj_b"]),
        "l0_bv": rows(i["L0_ffn_in_proj_b"][2 * D:]),
        "l0_wo": i["L0_ffn_out_proj_w"].T,
        "l0_bo": rows(i["L0_ffn_out_proj_b"]),
        "l0_ln1_g": rows(i["L0_ffn_ln1_g"]),
        "l0_ln1_b": rows(i["L0_ffn_ln1_b"]),
        "l0_ln2_g": rows(i["L0_ffn_ln2_g"]),
        "l0_ln2_b": rows(i["L0_ffn_ln2_b"]),
        "l0_wg": i["L0_ffn_wg"],
        "l0_w1_t": i["L0_ffn_w1"].reshape(L0_E, D, L0_FF // P, P).transpose(3, 0, 2, 1),
        "l0_w2": i["L0_ffn_w2"].reshape(L0_E, L0_FF // P, P, D).transpose(2, 0, 1, 3),
        "l0_b1": i["L0_ffn_b1"].reshape(L0_E, L0_FF // P, P).transpose(2, 0, 1),
        "l0_b2": i["L0_ffn_b2"],
        "block_of": (s[:, None] // S == np.arange(2)[None, :]).astype(np.float32),
        "l1_w_sim": cols(i["L1_xattn_w_sim"]),
        "l1_b_sim": rows(i["L1_xattn_b_sim"]),
        "l1_wqv": i["L1_xattn_W_qv"].reshape(4, D, D).transpose(1, 0, 2),
        "l1_bqv": rows(i["L1_xattn_b_qv"]),
        "l1_wg": i["L1_ffn_Wg"].T,
        "l1_w1": i["L1_ffn_W1"].transpose(2, 0, 1),
        "l1_w3": i["L1_ffn_W3"].transpose(2, 0, 1),
        "l1_w2": i["L1_ffn_W2"].transpose(2, 0, 1),
        "l1_b1": i["L1_ffn_b1"].T,
        "l1_b3": i["L1_ffn_b3"].T,
        "l1_b2": i["L1_ffn_b2"],
        "earlier4": np.broadcast_to(np.tri(L1_GROUPS, k=-1, dtype=np.float32), (P, L1_GROUPS, L1_GROUPS)),
        "of_head": (s[:, None] % S // HD == np.arange(HEADS // 2)[None, :]).astype(np.float32),
        "l2_mask": np.concatenate([i["mask_1x1xSxS2_ik0"][0, 0]] * 2),
        "l2_wq": i["L2_xattn_w_q"].T,
        "l2_wk": i["L2_xattn_w_k"].T,
        "l2_wv": i["L2_xattn_w_v"].T,
        "l2_wo": i["L2_xattn_w_o"].T,
        "l2_bq": halves(i["L2_xattn_b_q"]),
        "l2_bk": halves(i["L2_xattn_b_k"]),
        "l2_bv": by_parity(i["L2_xattn_b_v"]),
        "l2_bo": rows(i["L2_xattn_b_o"]),
        "l2_wr": i["L2_ffn_router_w"].T,
        "l2_gamma": rows(i["L2_ffn_gamma"]),
        "l2_beta": rows(i["L2_ffn_beta"]),
        "l2_w1": i["L2_ffn_W1"].transpose(1, 0, 2),
        "l2_w2": i["L2_ffn_W2"].reshape(L2_E, L2_H // P, P, D).transpose(2, 0, 1, 3),
        "l3_mask": np.repeat(i["mask_BxS2_bf0"].reshape(TILES, 2, S).transpose(1, 0, 2), S, axis=0).reshape(P, -1),
        "l3_wq": i["L3_xattn_Wq"],
        "l3_wk": i["L3_xattn_Wk"],
        "l3_wv": i["L3_xattn_Wv"],
        "l3_wo": i["L3_xattn_Wo"],
        "l3_bq": halves(i["L3_xattn_bq"]),
        "l3_bk": halves(i["L3_xattn_bk"]),
        "l3_bv": by_parity(i["L3_xattn_bv"]),
        "l3_bo": rows(i["L3_xattn_bo"]),
        "l3_ln1_g": rows(i["L3_xattn_ln1_g"]),
        "l3_ln1_b": rows(i["L3_xattn_ln1_b"]),
        "l3_w1": i["L3_xattn_W1"],
        "l3_b1": cols(i["L3_xattn_b1"]),
        "l3_w2": i["L3_xattn_W2"].reshape(FFN // P, P, D).transpose(1, 0, 2),
        "l3_b2": rows(i["L3_xattn_b2"]),
        "l3_ln2_g": rows(i["L3_xattn_ln2_g"]),
        "l3_ln2_b": rows(i["L3_xattn_ln2_b"]),
        "l3_tq": i["L3_ffn_Wq"],
        "l3_rt": i["L3_ffn_routers"].T,
        "l3_vt": i["L3_ffn_leaf_values"].T,
        "l3_two": i["L3_ffn_Wout_w"].T,
        "l3_tbo": rows(i["L3_ffn_Wout_b"]),
        "powers": np.where((age >= 0) & same, DECAY ** np.maximum(age, 0).astype(np.float64), 0.0).astype(np.float32),
    }
    return {k: np.ascontiguousarray(v) for k, v in out.items()}


def kernel(**inputs):
    import concourse.bacc as bacc
    from concourse.bass_utils import run_bass_kernel_spmd

    arrays = {f"in_{k}": v for k, v in layouts({k: np.asarray(v) for k, v in inputs.items()}).items()}
    nc = bacc.Bacc("TRN2", target_bir_lowering=False, num_devices=1)
    dram = {k[3:]: nc.dram_tensor(k, a.shape, mybir.dt.from_np(a.dtype), kind="ExternalInput").ap()
            for k, a in arrays.items()}
    for name, shape in (("x1", (TOKENS, D)), ("y1_t", (P, TOKENS)), ("x2", (TOKENS, D))):
        dram[name] = nc.dram_tensor(f"scratch_{name}", shape, F32, kind="Internal").ap()
    dram["out"] = nc.dram_tensor("out", (TOKENS, D), F32, kind="ExternalOutput").ap()
    build(nc, dram)
    r = run_bass_kernel_spmd(nc, [arrays], core_ids=[0])
    return r.results[0]["out"].reshape(B, S, D)
```

```python
from contextlib import ExitStack

import numpy as np

import concourse.bass as bass
from concourse import mybir

F32 = mybir.dt.float32
F32R = mybir.dt.float32r
U8 = mybir.dt.uint8
I32 = mybir.dt.int32
ALU = mybir.AluOpType
ACT = mybir.ActivationFunctionType
AX = mybir.AxisListType

P = 128
B, S, D = 128, 64, 128
TOKENS = B * S
TILES = TOKENS // P
G = 4
GROUPS = TILES // G
N = G * P
BG = N // S
LN_EPS = 1e-5
DMA = 16

DECAY = 0.9
L0_HEADS, L0_HD = 4, 32
L0_E, L0_FF = 8, 512
L0_CAP = TOKENS // L0_E
L1_E, L1_GROUPS, L1_TOPK, L1_TOPG, ROUTE_SCALE = 16, 4, 4, 2, 2.5
HEADS, HD = 16, 8
L2_E, L2_H, L2_TEMP = 8, 512, 1.5
FFN = 512
LEAVES = 256
BIG = 3.4028234e38


def reuse(eng, sem, value):
    if not (isinstance(value, int) and value <= 0):
        eng.wait_ge(sem, value)


def wait_apart(eng, sem, value, passed):
    eng.wait_ge(sem, value)
    eng.sem_inc(passed, 1)


def over_groups(front, main, eng):
    front(0, 0)
    main(0, 0, lambda *parts: front(1, 1, *parts))
    main(1, 1, lambda *parts: front(2, 0, *parts))
    with eng.Fori(1, GROUPS // 2 - 1) as pair:
        main(pair * 2, 0, lambda *parts: front(pair * 2 + 1, 1, *parts))
        main(pair * 2 + 1, 1, lambda *parts: front(pair * 2 + 2, 0, *parts))
    main(GROUPS - 2, 0, lambda *parts: front(GROUPS - 1, 1, *parts))
    main(GROUPS - 1, 1, lambda *parts: None)


def ago(i, back, do):
    if not isinstance(i, int) or 0 <= i - back < GROUPS:
        do(i - back)


def over_lagging(front, main, eng, lag):
    peeled = lag + lag % 2
    front(0, 0)
    for i in range(peeled):
        main(i, i % 2, lambda *parts, i=i: front(i + 1, (i + 1) % 2, *parts))
    with eng.Fori(peeled // 2, GROUPS // 2 - 1) as pair:
        main(pair * 2, 0, lambda *parts: front(pair * 2 + 1, 1, *parts))
        main(pair * 2 + 1, 1, lambda *parts: front(pair * 2 + 2, 0, *parts))
    main(GROUPS - 2, 0, lambda *parts: front(GROUPS - 1, 1, *parts))
    for i in range(GROUPS - 1, GROUPS + lag):
        main(i, i % 2, lambda *parts: None)


def loads(i, h, count=1):
    return (i - h) * (count * DMA // 2) + count * DMA


def each_group(step, eng):
    step(0, 0)
    step(1, 1)
    with eng.Fori(1, GROUPS // 2) as pair:
        step(pair * 2, 0)
        step(pair * 2 + 1, 1)


class Chip:

    def __init__(self, nc, ctx, dram):
        self.nc, self.dram = nc, dram
        self.x_all = ctx.enter_context(nc.sbuf_tensor("x_all", [P, TILES, D], F32))
        self.ident = ctx.enter_context(nc.sbuf_tensor("ident", [P, P], F32))
        self.tanh_g = ctx.enter_context(nc.sbuf_tensor("tanh_g", [P, 8], F32))
        self.neg_half = ctx.enter_context(nc.sbuf_tensor("neg_half", [P, G], F32))
        self.passed = {e: ctx.enter_context(nc.semaphore(f"passed_{e}")) for e in ("v", "pool", "act", "pe")}
        self.bank = [ctx.enter_context(nc.psum_tensor(f"bank{k}", [P, 512], F32)) for k in range(8)]


class Phase:

    def __init__(self, chip, name):
        self.chip, self.nc, self.name = chip, chip.nc, name
        self.ctx, self.sems = ExitStack(), []

    def __enter__(self):
        return self

    def __exit__(self, *failure):
        self.ctx.close()
        if failure[0] is None:
            self.nc.clear_and_free_semaphores(self.sems)
            self.nc.all_engine_barrier()

    def sem(self, what):
        self.sems.append(self.nc.alloc_semaphore(f"{self.name}_{what}"))
        return self.sems[-1]

    def sb(self, what, shape, dt=F32):
        return self.ctx.enter_context(self.nc.sbuf_tensor(f"{self.name}_{what}", shape, dt))


class Ahead:

    def __init__(self, chip, ctx, name, **shapes):
        self.dram, self.names = chip.dram, [f"{name}_{what}" for what in shapes]
        self.tensors = [ctx.enter_context(chip.nc.sbuf_tensor(f"{name}_{what}_ahead", shape, F32))
                        for what, shape in shapes.items()]
        self.loaded = ctx.enter_context(chip.nc.semaphore(f"{name}_weights_ahead"))

    def start(self, sp):
        for tensor, name in zip(self.tensors, self.names):
            sp.dma_start(tensor[(slice(None),) * len(tensor.shape)], self.dram[name]).then_inc(self.loaded, DMA)

    def wait(self, eng):
        eng.wait_ge(self.loaded, len(self.tensors) * DMA)


class LayerNorm:

    def __init__(self, ph, what):
        self.chip = ph.chip
        self.stats = ph.sb(f"{what}_stats", [P, G, 6])
        self.mv = ph.sb(f"{what}_mv", [P, G, 2])
        self.var_eps = ph.sb(f"{what}_var_eps", [P, G])
        self.rstd = ph.sb(f"{what}_rstd", [P, G])
        self.stats_done = ph.sem(f"{what}_stats")
        self.var_done = ph.sem(f"{what}_var")
        self.eps_added = ph.sem(f"{what}_eps")
        self.rstd_done = ph.sem(f"{what}_rstd")

    def vector_stats(self, v, i, tile):
        for t in range(G):
            v.bn_stats(self.stats[:, t, :], tile(t)).then_inc(self.stats_done, 1)
        wait_apart(v, self.stats_done, i * G + G, self.chip.passed["v"])
        for t in range(G):
            v.bn_aggr(self.mv[:, t, :], self.stats[:, t, :]).then_inc(self.var_done, 1)

    def pool_rstd(self, pool, i):
        wait_apart(pool, self.var_done, i * G + G, self.chip.passed["pool"])
        pool.tensor_scalar(self.var_eps[:, :], self.mv[:, :, 1], LN_EPS, None, ALU.add).then_inc(self.eps_added, 1)
        pool.wait_ge(self.eps_added, i + 1)
        pool.tensor_tensor(self.rstd[:, :], self.var_eps[:, :], self.chip.neg_half[:, :], ALU.pow)\
            .then_inc(self.rstd_done, 1)

    def vector_apply(self, v, i, tile, out, done):
        v.wait_ge(self.rstd_done, i + 1)
        for t in range(G):
            v.tensor_scalar(out[:, t, :], tile(t), self.mv[:, t, 0:1], self.rstd[:, t:t + 1],
                            ALU.subtract, ALU.mult).then_inc(done, 1)


def split_product(pe, out, high_low, moving):
    w_high, w_low = high_low
    m_high, m_low = moving
    pe.matmul(out, w_high, m_high, start=True, stop=False)
    pe.matmul(out, w_high, m_low, start=False, stop=False)
    return pe.matmul(out, w_low, m_high, start=False, stop=True)


def group_of(tensor, i):
    return tensor[:, bass.ds(i * G, G), :]


def tile_of(tensor, i, t):
    return tensor[:, bass.ds(i * G + t, 1), :].rearrange("p a d -> p (a d)")


def transposes(pe, bank, tiles, ident):
    for t, src in enumerate(tiles):
        done = pe.transpose(bank[:, t * P:(t + 1) * P], src, ident[:, :])
    return done


def constants(chip):
    nc, dram = chip.nc, chip.dram
    with Phase(chip, "const") as ph:
        loaded, gates, filled = ph.sem("loaded"), ph.sem("gates"), ph.sem("filled")
        g_raw = ph.sb("g_raw", [P, 8])
        with nc.Block() as block:
            @block.sync
            def _(sp):
                sp.dma_start(chip.ident[:, :], dram["ident"]).then_inc(loaded, DMA)
                sp.dma_start(g_raw[:, 0:4], dram["g_xattn"]).then_inc(loaded, DMA)
                sp.dma_start(g_raw[:, 4:8], dram["g_ffn"]).then_inc(loaded, DMA)
                sp.wait_ge(loaded, 3 * DMA)

            @block.gpsimd
            def _(pool):
                pool.memset(chip.neg_half[:, :], -0.5).then_inc(filled, 1)

            @block.scalar
            def _(act):
                act.wait_ge(loaded, 3 * DMA)
                act.activation(chip.tanh_g[:, :], g_raw[:, :], ACT.Tanh).then_inc(gates, 1)


def l0_mix(chip):
    nc, dram, x_all, bank = chip.nc, chip.dram, chip.x_all, chip.bank
    with Phase(chip, "l0mix") as ph:
        ln = LayerNorm(ph, "ln")
        powers = ph.sb("powers", [P, P])
        ctx = ph.sb("ctx", [P, 2, G, D])
        kv = ph.sb("kv", [P, 2, N])
        xn = ph.sb("xn", [P, 2, G, D])
        scaled = ph.sb("scaled", [P, N])
        x_out = ph.sb("x_out", [P, 2, G, D])
        w_in, kv_done = ph.sem("w_in"), ph.sem("kv")
        loaded, stored = [ph.sem("loaded0"), ph.sem("loaded1")], [ph.sem("stored0"), ph.sem("stored1")]
        xn_done, r_done, scaled_done = ph.sem("xn"), ph.sem("r"), ph.sem("scaled")
        out_done = ph.sem("out")
        x_dram = dram["x"].rearrange("(n p) d -> p n d", p=P)
        ctx_dram = dram["ctx"].rearrange("(n p) d -> p n d", p=P)
        x1_dram = dram["x1"].rearrange("(n p) d -> p n d", p=P)
        tanh_g = chip.tanh_g[:, 0:1]

        with nc.Block() as block:
            @block.sync
            def _(sp):
                sp.dma_start(powers[:, :], dram["powers"]).then_inc(w_in, DMA)

                def step(i, h):
                    reuse(sp, kv_done, i - 1)
                    sp.dma_start(group_of(x_all, i), group_of(x_dram, i)).then_inc(loaded[h], DMA)
                    sp.dma_start(ctx[:, h], group_of(ctx_dram, i)).then_inc(loaded[h], DMA)
                each_group(step, sp)

            @block.scalar
            def _(act):
                def step(i, h):
                    act.wait_ge(loaded[h], loads(i, h, 2))
                    reuse(act, r_done, i - 1)
                    act.activation(kv[:, h], ctx[:, h].rearrange("p t d -> p (t d)"), ACT.Square)\
                        .then_inc(kv_done, 1)
                    act.wait_ge(out_done, i + 1)
                    act.dma_start(group_of(x1_dram, i), x_out[:, h]).then_inc(stored[h], DMA)
                each_group(step, act)
                for h in range(2):
                    act.wait_ge(stored[h], loads(GROUPS - 2 + h, h))

            @block.gpsimd
            def _(pool):
                each_group(lambda i, h: ln.pool_rstd(pool, i), pool)

            @block.tensor
            def _(pe):
                pe.wait_ge(w_in, DMA)

                def step(i, h):
                    pe.wait_ge(kv_done, i + 1)
                    reuse(pe, scaled_done, i - 1)
                    pe.matmul(bank[h][:, :], powers[:, :], kv[:, h], start=True, stop=True).then_inc(r_done, 1)
                each_group(step, pe)

            @block.vector
            def _(v):
                def front(i, h):
                    wait_apart(v, loaded[h], loads(i, h, 2), chip.passed["v"])
                    ln.vector_stats(v, i, lambda t: tile_of(x_all, i, t))

                def main(i, h, nxt):
                    ln.vector_apply(v, i, lambda t: tile_of(x_all, i, t), xn[:, h], xn_done)
                    nxt()
                    v.wait_ge(r_done, i + 1)
                    v.wait_ge(xn_done, i * G + G)
                    v.tensor_tensor(scaled[:, :], xn[:, h].rearrange("p t d -> p (t d)"), bank[h][:, :], ALU.mult)\
                        .then_inc(scaled_done, 1)
                    reuse(v, stored[h], loads(i - 2, h))
                    v.wait_ge(scaled_done, i + 1)
                    v.scalar_tensor_tensor(out=x_out[:, h], in0=scaled[:, :].rearrange("p (t d) -> p t d", t=G),
                                           scalar=tanh_g, in1=group_of(x_all, i), op0=ALU.mult, op1=ALU.add)\
                        .then_inc(out_done, 1)
                over_groups(front, main, v)


def l0_attention(chip, y1_all, logits, ahead):
    nc, dram, x_all, bank, ident = chip.nc, chip.dram, chip.x_all, chip.bank, chip.ident
    H, HD0 = L0_HEADS, L0_HD
    scale = HD0 ** -0.5
    with Phase(chip, "l0att") as ph:
        ln0, ln1 = LayerNorm(ph, "ln0"), LayerNorm(ph, "ln1")
        wqkv, wo = ph.sb("wqkv", [P, 3 * D]), ph.sb("wo", [P, D])
        b_cols, bq_scaled, k_bias = ph.sb("b_cols", [P, 3]), ph.sb("bq_scaled", [P, 1]), ph.sb("k_bias", [P, H])
        of_head, bv, bo = ph.sb("of_head", [P, H]), ph.sb("bv", [P, D]), ph.sb("bo", [P, D])
        ln_g, ln_b, wg = ph.sb("ln_g", [P, D]), ph.sb("ln_b", [P, D]), ph.sb("wg", [P, L0_E])
        z, z_t = ph.sb("z", [P, 2, G, D]), ph.sb("z_t", [P, 2, N])
        q_t, k_heads, val = ph.sb("q_t", [P, 2, N]), ph.sb("k_heads", [P, 2, G, H, P]), ph.sb("val", [P, 2, G, D])
        neg_top, sums, share = ph.sb("neg_top", [P, G, H]), ph.sb("sums", [P, G, H]), ph.sb("share", [P, G, H])
        probs, probs_t = ph.sb("probs", [P, G, H, P]), ph.sb("probs_t", [P, 2, H, P])
        o_t, residual = ph.sb("o_t", [P, 2, N]), ph.sb("residual", [P, 2, G, D])
        res, normed = ph.sb("res", [P, G, D]), ph.sb("normed", [P, G, D])
        y1, y1_t = ph.sb("y1", [P, 2, G, D]), ph.sb("y1_t", [P, 2, N])

        w_in, consts_done = ph.sem("w_in"), ph.sem("consts")
        x_in = [ph.sem("x_in0"), ph.sem("x_in1")]
        stored = [ph.sem("stored0"), ph.sem("stored1")]
        z_done, z_turned, z_t_done = ph.sem("z"), ph.sem("z_turned"), ph.sem("z_t")
        k_made, q_made, v_made = ph.sem("k_made"), ph.sem("q_made"), ph.sem("v_made")
        k_out, q_out, v_out = ph.sem("k_out"), ph.sem("q_out"), ph.sem("v_out")
        scored, topped, exped = ph.sem("scored"), ph.sem("topped"), ph.sem("exped")
        share_done, shared, p_turned, p_t_done = ph.sem("share"), ph.sem("shared"), ph.sem("p_turned"), ph.sem("p_t")
        o_made, o_t_done, proj_done = ph.sem("o_made"), ph.sem("o_t"), ph.sem("proj")
        residual_done, res_done, normed_done = ph.sem("residual"), ph.sem("res"), ph.sem("normed")
        gained, y1_done, y1_kept = ph.sem("gained"), ph.sem("y1"), ph.sem("y1_kept")
        y1_turned, y1_t_done, gated, logits_out = (ph.sem("y1_turned"), ph.sem("y1_t"), ph.sem("gated"),
                                                   ph.sem("logits_out"))
        x1_dram = dram["x1"].rearrange("(l n) d -> l n d", n=S)
        y1_t_dram = dram["y1_t"].rearrange("p (g n) -> p g n", g=GROUPS)
        row = lambda ap: ap[:, :].unsqueeze(1).to_broadcast([P, G, D])
        side = lambda ap: ap.rearrange("p t d -> p (t d)")

        def tile_ago(i, s, back, do):
            ago(i, (back - s + G - 1) // G, lambda g: do(g, (s - back) % G))

        def over_tiles(front, slot, parts, eng):
            def main(i, h, nxt):
                for s in range(G):
                    slot(i, h, s)
                    if s in parts:
                        nxt(*parts[s])
            over_lagging(front, main, eng, 3)

        with nc.Block() as block:
            @block.sync
            def _(sp):
                for dst, name in ((wqkv, "l0_wqkv"), (wo, "l0_wo"), (b_cols, "l0_b_cols"), (bv, "l0_bv"), (bo, "l0_bo"),
                                  (ln_g, "l0_ln1_g"), (ln_b, "l0_ln1_b"), (wg, "l0_wg"), (of_head, "l0_of_head")):
                    sp.dma_start(dst[:, :], dram[name]).then_inc(w_in, DMA)

                def step(i, h):
                    reuse(sp, z_done, (i - 1) * G)
                    sp.dma_start(group_of(x_all, i), group_of(x1_dram, i)).then_inc(x_in[h], DMA)
                    if isinstance(i, int) and i == 1:
                        ahead.start(sp)
                each_group(step, sp)

            @block.gpsimd
            def _(pool):
                pool.wait_ge(w_in, 9 * DMA)

                def rstd(i, h):
                    ln0.pool_rstd(pool, i)

                def normalize(i, t):
                    pool.wait_ge(share_done, i * G + t + 1)
                    pool.tensor_tensor(probs[:, t], probs[:, t], share[:, t, :].unsqueeze(2).to_broadcast([P, H, P]),
                                       ALU.mult).then_inc(shared, 1)

                def add_bias(i, h):
                    pool.wait_ge(z_done, i * G + G)
                    reuse(pool, res_done, i - 1)
                    pool.tensor_tensor(residual[:, h], z[:, h], row(bo), ALU.add).then_inc(residual_done, 1)

                def gain(i):
                    pool.wait_ge(normed_done, i * G + G)
                    pool.tensor_tensor(normed[:, :, :], normed[:, :, :], row(ln_g), ALU.mult).then_inc(gained, 1)

                def shift(i, h):
                    pool.wait_ge(gained, i + 1)
                    reuse(pool, y1_turned, i - 1)
                    reuse(pool, y1_kept, i - 1)
                    pool.tensor_tensor(y1[:, h], normed[:, :, :], row(ln_b), ALU.add).then_inc(y1_done, 1)

                def front(i, h, *parts):
                    rstd(0, 0)
                    rstd(1, 1)

                def slot(i, h, s):
                    tile_ago(i, s, 2, normalize)
                    if s == 1:
                        ago(i, 2, lambda g: ln1.pool_rstd(pool, g))
                    if s == 2:
                        ago(i, 0, lambda g: add_bias(g, h))
                        ago(i, -2, lambda g: rstd(g, h))
                        ago(i, 2, lambda g: gain(g))
                    if s == 3:
                        ago(i, 2, lambda g: shift(g, h))
                over_tiles(front, slot, {}, pool)

            @block.tensor
            def _(pe):
                pe.wait_ge(w_in, 9 * DMA)

                def turn_z(i, h):
                    pe.wait_ge(z_done, i * G + G)
                    reuse(pe, k_out, i * H)
                    transposes(pe, bank[6], [z[:, h, t, :] for t in range(G)], ident).then_inc(z_turned, 1)

                def make_qk(i, h):
                    reuse(pe, v_out, i)
                    pe.wait_ge(z_t_done, i + 1)
                    pe.matmul(bank[6][:, :], wqkv[:, D:2 * D], z_t[:, h], start=True, stop=True).then_inc(k_made, 1)
                    pe.matmul(bank[7][:, :], wqkv[:, 0:D], z_t[:, h], start=True, stop=True).then_inc(q_made, 1)

                def make_v(i, h):
                    pe.wait_ge(q_out, i + 1)
                    for t in range(G):
                        mm = pe.matmul(bank[7][:, t * D:(t + 1) * D], z_t[:, h, t * P:(t + 1) * P], wqkv[:, 2 * D:],
                                       start=True, stop=True)
                    mm.then_inc(v_made, 1)

                def scores(i, h, t):
                    if t == 0:
                        pe.wait_ge(q_out, i + 1)
                        pe.wait_ge(k_out, (i + 1) * H)
                    reuse(pe, exped, (i * G + t - 1) * H)
                    pe.matmul(bank[t % 2][:, :], q_t[:, h, t * P:(t + 1) * P],
                              k_heads[:, h, t].rearrange("p n m -> p (n m)"), start=True, stop=True).then_inc(scored, 1)

                def turn(i, t):
                    pe.wait_ge(shared, i * G + t + 1)
                    reuse(pe, p_t_done, i * G + t)
                    transposes(pe, bank[2], [probs[:, t, n, :] for n in range(H)], ident).then_inc(p_turned, 1)

                def values(i, h, t):
                    pe.wait_ge(p_t_done, i * G + t + 1)
                    if t == 0:
                        pe.wait_ge(v_out, i + 1)
                        reuse(pe, o_t_done, i)
                    for n in range(H):
                        mm = pe.matmul(bank[4][n * HD0:(n + 1) * HD0, t * P:(t + 1) * P],
                                       val[:, h, t, n * HD0:(n + 1) * HD0], probs_t[:, t % 2, n, :],
                                       start=True, stop=True)
                    mm.then_inc(o_made, 1)

                def project(i, h):
                    pe.wait_ge(o_t_done, i + 1)
                    reuse(pe, res_done, i)
                    for t in range(G):
                        mm = pe.matmul(bank[5][:, t * D:(t + 1) * D], o_t[:, h, t * P:(t + 1) * P], wo[:, :],
                                       start=True, stop=True)
                    mm.then_inc(proj_done, 1)

                def turn_y1(i, h):
                    pe.wait_ge(y1_done, i + 1)
                    reuse(pe, logits_out, i)
                    transposes(pe, bank[3], [y1[:, h, t, :] for t in range(G)], ident).then_inc(y1_turned, 1)

                def gate(i, h):
                    pe.wait_ge(y1_t_done, i + 1)
                    for t in range(G):
                        for b in range(2):
                            r = slice(b * S, (b + 1) * S)
                            mm = pe.matmul(bank[3][r, t * L0_E:(t + 1) * L0_E],
                                           y1_t[:, h, t * P + b * S:t * P + (b + 1) * S], wg[:, :],
                                           start=True, stop=True)
                    mm.then_inc(gated, 1)

                def front(i, h, *parts):
                    for part in parts or (turn_z, make_qk, make_v):
                        part(i, h)

                def slot(i, h, s):
                    ago(i, 0, lambda g: scores(g, h, s))
                    tile_ago(i, s, 3, turn)
                    ago(i, 1, lambda g: values(g, 1 - h, s))
                    if s == 0:
                        ago(i, 3, lambda g: turn_y1(g, 1 - h))
                        ago(i, 2, lambda g: project(g, h))
                    if s == 2:
                        ago(i, 3, lambda g: gate(g, 1 - h))
                over_tiles(front, slot, {0: (turn_z,), 1: (make_qk,), 2: (make_v,)}, pe)

            @block.scalar
            def _(act):
                act.wait_ge(w_in, 9 * DMA)
                act.wait_ge(consts_done, 2)

                def z_out(i, h):
                    act.wait_ge(z_turned, i + 1)
                    act.activation(z_t[:, h], bank[6][:, :], ACT.Identity).then_inc(z_t_done, 1)

                def q_part(i, h):
                    act.wait_ge(q_made, i + 1)
                    act.activation(q_t[:, h], bank[7][:, :], ACT.Identity, bias=bq_scaled[:, 0:1], scale=scale)\
                        .then_inc(q_out, 1)

                def k_parts(i, h):
                    act.wait_ge(k_made, i + 1)
                    reuse(act, scored, (i - 1) * G)
                    for n in range(H):
                        act.activation(k_heads[:, h, :, n, :], bank[6][:, :].rearrange("p (t m) -> p t m", t=G),
                                       ACT.Identity, bias=k_bias[:, n:n + 1], scale=of_head[:, n:n + 1]).then_inc(k_out, 1)

                def exp(i, t):
                    act.wait_ge(topped, i * G + t + 1)
                    reuse(act, p_turned, (i - 1) * G + t + 1)
                    for n in range(H):
                        act.activation(probs[:, t, n, :], bank[t % 2][:, n * P:(n + 1) * P], ACT.Exp,
                                       bias=neg_top[:, t, n:n + 1], accum_out=sums[:, t, n:n + 1]).then_inc(exped, 1)

                def turned(i, t):
                    act.wait_ge(p_turned, i * G + t + 1)
                    reuse(act, o_made, i * G + t - 1)
                    act.activation(probs_t[:, t % 2].rearrange("p n q -> p (n q)"), bank[2][:, :], ACT.Identity)\
                        .then_inc(p_t_done, 1)

                def o_out(i, h):
                    act.wait_ge(o_made, i * G + G)
                    reuse(act, proj_done, i - 1)
                    act.activation(o_t[:, h], bank[4][:, :], ACT.Identity).then_inc(o_t_done, 1)

                def y1_out(i, h):
                    act.wait_ge(y1_turned, i + 1)
                    reuse(act, stored[h], loads(i - 2, h))
                    act.activation(y1_t[:, h], bank[3][:, :], ACT.Identity).then_inc(y1_t_done, 1)

                def store(i, h):
                    act.wait_ge(y1_t_done, i + 1)
                    act.dma_start(y1_t_dram[:, bass.ds(i, 1), :].rearrange("p a n -> p (a n)"), y1_t[:, h])\
                        .then_inc(stored[h], DMA)

                def front(i, h, *parts):
                    for part in parts or (z_out, k_parts, q_part):
                        part(i, h)

                def slot(i, h, s):
                    if s == 0:
                        ago(i, 2, lambda g: o_out(g, h))
                    tile_ago(i, s, 1, exp)
                    tile_ago(i, s, 3, turned)
                    if s == 1:
                        ago(i, 3, lambda g: y1_out(g, 1 - h))
                    if s == 2:
                        ago(i, 3, lambda g: store(g, 1 - h))
                over_tiles(front, slot, {0: (z_out,), 2: (q_part, k_parts)}, act)
                for h in range(2):
                    act.wait_ge(stored[h], loads(GROUPS - 2 + h, h))

            @block.vector
            def _(v):
                v.wait_ge(w_in, 9 * DMA)
                v.tensor_scalar(bq_scaled[:, :], b_cols[:, 0:1], scale, None, ALU.mult).then_inc(consts_done, 1)
                v.tensor_scalar(k_bias[:, :], of_head[:, :], b_cols[:, 1:2], None, ALU.mult).then_inc(consts_done, 1)

                def stats(i, h):
                    wait_apart(v, x_in[h], loads(i, h), chip.passed["v"])
                    ln0.vector_stats(v, i, lambda t: tile_of(x_all, i, t))

                def apply(i, h):
                    reuse(v, residual_done, i - 1)
                    ln0.vector_apply(v, i, lambda t: tile_of(x_all, i, t), z[:, h], z_done)

                def value_rows(i, h):
                    v.wait_ge(v_made, i + 1)
                    reuse(v, o_made, (i - 1) * G)
                    v.tensor_tensor(val[:, h], bank[7][:, :].rearrange("p (t d) -> p t d", t=G), row(bv), ALU.add)\
                        .then_inc(v_out, 1)

                def top(i, t):
                    v.wait_ge(scored, i * G + t + 1)
                    reuse(v, exped, ((i - 1) * G + t + 1) * H)
                    v.tensor_reduce(neg_top[:, t, :], bank[t % 2][:, :].rearrange("p (n m) -> p n m", n=H), AX.X,
                                    ALU.max, negate=True).then_inc(topped, 1)

                def shares(i, t):
                    v.wait_ge(exped, (i * G + t + 1) * H)
                    v.reciprocal(share[:, t, :], sums[:, t, :]).then_inc(share_done, 1)

                def add_residual(i, h):
                    v.wait_ge(proj_done, i + 1)
                    v.wait_ge(residual_done, i + 1)
                    v.tensor_tensor(side(res[:, :, :]), bank[5][:, :], side(residual[:, h]), ALU.add).then_inc(res_done, 1)
                    wait_apart(v, res_done, i + 1, chip.passed["v"])
                    ln1.vector_stats(v, i, lambda t: res[:, t, :])

                def norm(i, h):
                    reuse(v, y1_done, i)
                    ln1.vector_apply(v, i, lambda t: res[:, t, :], normed, normed_done)

                def keep_y1(i, h):
                    v.wait_ge(y1_done, i + 1)
                    v.tensor_scalar(group_of(y1_all, i), y1[:, h], 1.0, None, ALU.mult).then_inc(y1_kept, 1)

                def keep_logits(i):
                    v.wait_ge(gated, i + 1)
                    v.tensor_scalar(logits[:, bass.ds(i * G, G), :],
                                    bank[3][:, 0:G * L0_E].rearrange("p (t e) -> p t e", t=G), 1.0, None, ALU.mult)\
                        .then_inc(logits_out, 1)

                def front(i, h, *parts):
                    if parts:
                        value_rows(i, h)
                    else:
                        for g in range(2):
                            stats(g, g)
                            apply(g, g)
                        value_rows(i, h)

                def slot(i, h, s):
                    tile_ago(i, s, 2, shares)
                    tile_ago(i, s, 0, top)
                    if s == 0:
                        ago(i, 3, lambda g: keep_y1(g, 1 - h))
                    if s == 1:
                        ago(i, 2, lambda g: add_residual(g, h))
                    if s == 2:
                        ago(i, 2, lambda g: norm(g, h))
                        ago(i, -2, lambda g: stats(g, h))
                    if s == 3:
                        ago(i, -2, lambda g: apply(g, h))
                        ago(i, 3, keep_logits)
                over_tiles(front, slot, {3: (value_rows,)}, v)


def l0_route(chip, logits, weight, ahead, w12, b12):
    nc, dram, bank = chip.nc, chip.dram, chip.bank
    E, C = L0_E, L0_FF // P
    with Phase(chip, "l0route") as ph:
        w1_t, w2 = ahead.tensors
        b1, b1_wide, b2 = ph.sb("b1", [P, E, C]), ph.sb("b1_wide", [P, E * C * E + 8]), ph.sb("b2", [E, D])
        b1_in, b1_zero, b1_spread, merged, merged_out = (ph.sem("b1_in"), ph.sem("b1_zero"), ph.sem("b1_spread"),
                                                         ph.sem("merged"), ph.sem("merged_out"))
        first, later = ph.sb("first", [P, E]), ph.sb("later", [P, P])
        best, total = ph.sb("best", [P, TILES]), ph.sb("total", [P, TILES])
        shifted, exps = ph.sb("shifted", [P, TILES, E]), ph.sb("exps", [P, TILES, E])
        hot, place = ph.sb("hot", [P, TILES, E]), ph.sb("place", [P, TILES, E])
        count, base = ph.sb("count", [P, E]), ph.sb("base", [P, E])
        ones = ph.sb("ones", [P, TILES])
        loaded, ones_set, done, exped, based = (ph.sem("loaded"), ph.sem("ones"), ph.sem("vector_steps"),
                                                ph.sem("exped"), ph.sem("based"))
        wide = lambda ap: ap[:, :].unsqueeze(2).to_broadcast([P, TILES, E])
        with nc.Block() as block:
            @block.sync
            def _(sp):
                sp.dma_start(first[:, :], dram["l0_first"]).then_inc(loaded, DMA)
                sp.dma_start(later[:, :], dram["later"]).then_inc(loaded, DMA)
                sp.dma_start(b1[:, :, :], dram["l0_b1"]).then_inc(b1_in, DMA)
                sp.dma_start(b2[:, :], dram["l0_b2"]).then_inc(b1_in, DMA)

            @block.gpsimd
            def _(pool):
                pool.memset(b1_wide[:, :], 0.0).then_inc(b1_zero, 1)
                pool.memset(ones[:, :], 1.0).then_inc(ones_set, 1)

            @block.scalar
            def _(act):
                act.wait_ge(done, 2)
                act.activation(exps[:, :, :], shifted[:, :, :], ACT.Exp).then_inc(exped, 1)
                act.wait_ge(merged, 1)
                for half in range(2):
                    act.activation(w12[:, half * 4:half * 4 + 4, :].rearrange("p e d -> p (e d)"), bank[1 + half][:, :],
                                   ACT.Identity).then_inc(merged_out, 1)

            @block.tensor
            def _(pe):
                ahead.wait(pe)
                for e in range(E):
                    for c in range(C):
                        mm = pe.matmul(bank[1 + e // 4][:, (e % 4) * D:(e % 4 + 1) * D], w1_t[:, e, c, :], w2[:, e, c, :],
                                       start=(c == 0), stop=(c == C - 1))
                mm.then_inc(merged, 1)
                pe.wait_ge(loaded, 2 * DMA)
                pe.wait_ge(done, 7)
                pe.matmul(bank[0][:, 0:E], later[:, :], count[:, :], start=True, stop=True).then_inc(based, 1)
                pe.wait_ge(b1_spread, 1)
                for k in range(E * C):
                    mm = pe.matmul(bank[3][0:E, 0:D], b1_wide[:, k * E:(k + 1) * E], w2[:, k // C, k % C, :],
                                   start=(k == 0), stop=(k == E * C - 1))
                mm.then_inc(merged, 1)

            @block.vector
            def _(v):
                v.wait_ge(loaded, 2 * DMA)
                v.tensor_reduce(best[:, :], logits[:, :, :], AX.X, ALU.max).then_inc(done, 1)
                v.wait_ge(done, 1)
                v.tensor_tensor(shifted[:, :, :], logits[:, :, :], wide(best), ALU.subtract).then_inc(done, 1)
                v.wait_ge(done, 2)
                v.tensor_scalar(hot[:, :, :], shifted[:, :, :], 0.0, None, ALU.is_equal).then_inc(done, 1)
                v.wait_ge(done, 3)
                v.tensor_tensor(place[:, :, :], hot[:, :, :], first[:, :].unsqueeze(1).to_broadcast([P, TILES, E]),
                                ALU.mult).then_inc(done, 1)
                v.wait_ge(done, 4)
                v.tensor_reduce(best[:, :], place[:, :, :], AX.X, ALU.max).then_inc(done, 1)
                v.wait_ge(done, 5)
                v.tensor_tensor(hot[:, :, :], place[:, :, :], wide(best), ALU.is_equal).then_inc(done, 1)
                v.wait_ge(done, 6)
                v.tensor_reduce(count[:, :], hot[:, :, :].rearrange("p n e -> p e n"), AX.X, ALU.add).then_inc(done, 1)
                v.wait_ge(b1_in, 2 * DMA)
                v.wait_ge(b1_zero, 1)
                v.tensor_copy(b1_wide[:, 0:E * (C * E + 1)].rearrange("p (e r) -> p e r", e=E)[:, :, 0:C * E]
                              .rearrange("p e (c k) -> p e c k", c=C)[:, :, :, 0], b1[:, :, :]).then_inc(b1_spread, 1)
                v.wait_ge(based, 1)
                v.tensor_copy(base[:, :], bank[0][:, 0:E]).then_inc(done, 1)
                v.wait_ge(done, 8)
                v.wait_ge(ones_set, 1)
                for e in range(E):
                    v.tensor_tensor_scan(place[:, :, e], ones[:, :], hot[:, :, e], base[:, e:e + 1], ALU.mult, ALU.add)\
                        .then_inc(done, 1)
                v.wait_ge(exped, 1)
                v.tensor_reduce(total[:, :], exps[:, :, :], AX.X, ALU.add).then_inc(done, 1)
                v.wait_ge(done, 9 + E)
                v.reciprocal(best[:, :], total[:, :]).then_inc(done, 1)
                v.scalar_tensor_tensor(out=weight[:, :, :], in0=place[:, :, :], scalar=float(L0_CAP),
                                       in1=hot[:, :, :], op0=ALU.is_le, op1=ALU.mult).then_inc(done, 1)
                v.wait_ge(done, 11 + E)
                v.tensor_tensor(weight[:, :, :], weight[:, :, :], wide(best), ALU.mult).then_inc(done, 1)
                v.wait_ge(merged, 2)
                v.tensor_tensor(b12[:, :], bank[3][0:E, 0:D], b2[:, :], ALU.add).then_inc(merged_out, 1)


def l0_experts(chip, y1_all, weight, w12, b12):
    nc, dram, x_all, bank, ident = chip.nc, chip.dram, chip.x_all, chip.bank, chip.ident
    E = L0_E
    with Phase(chip, "l0moe") as ph:
        ln = LayerNorm(ph, "ln")
        ln_g, ln_b = ph.sb("ln_g", [P, D]), ph.sb("ln_b", [P, D])
        y1_t = ph.sb("y1_t", [P, 2, N])
        w_now, w_t = ph.sb("w_now", [P, 2, G, E]), ph.sb("w_t", [E, N])
        acc, normed = ph.sb("acc", [P, 2, G, D]), ph.sb("normed", [P, 2, G, D])
        w_in, affine = ph.sem("w_in"), ph.sem("affine")
        y_in, stored = [ph.sem("y_in0"), ph.sem("y_in1")], [ph.sem("stored0"), ph.sem("stored1")]
        w_now_done, w_turned, w_t_done, biased = (ph.sem("w_now"), ph.sem("w_turned"), ph.sem("w_t"), ph.sem("biased"))
        started, made, used = ph.sem("started"), ph.sem("made"), ph.sem("used")
        normed_done, gained, moved, x2_done = ph.sem("normed"), ph.sem("gained"), ph.sem("moved"), ph.sem("x2")
        y1_t_dram = dram["y1_t"].rearrange("p (g n) -> p g n", g=GROUPS)
        x2_dram = dram["x2"].rearrange("(l n) d -> l n d", n=S)
        tanh_g = chip.tanh_g[:, 4:5]
        row = lambda ap: ap[:, :].unsqueeze(1).to_broadcast([P, G, D])

        with nc.Block() as block:
            @block.sync
            def _(sp):
                for dst, name in ((ln_g, "l0_ln2_g"), (ln_b, "l0_ln2_b")):
                    sp.dma_start(dst[:, :], dram[name]).then_inc(w_in, DMA)

                def main(i, h, nxt):
                    def load(g):
                        reuse(sp, made, (g - 1) * 2 * G)
                        sp.dma_start(y1_t[:, h], y1_t_dram[:, bass.ds(g, 1), :].rearrange("p a n -> p (a n)"))\
                            .then_inc(y_in[h], DMA)

                    def store(g):
                        sp.wait_ge(x2_done, g + 1)
                        sp.dma_start(group_of(x2_dram, g), group_of(x_all, g)).then_inc(stored[h], DMA)
                    ago(i, 0, load)
                    ago(i, 4, store)
                over_lagging(lambda i, h: None, main, sp, 4)
                for h in range(2):
                    sp.wait_ge(stored[h], loads(GROUPS - 2 + h, h))

            @block.gpsimd
            def _(pool):
                pool.wait_ge(affine, 2)

                def affine_part(i, h):
                    pool.wait_ge(normed_done, i * G + G)
                    pool.tensor_tensor(normed[:, h], normed[:, h], row(ln_g), ALU.mult).then_inc(gained, 1)
                    pool.wait_ge(gained, i + 1)
                    pool.tensor_tensor(normed[:, h], normed[:, h], row(ln_b), ALU.add).then_inc(moved, 1)

                def main(i, h, nxt):
                    ago(i, 1, lambda g: ln.pool_rstd(pool, g))
                    ago(i, 1, lambda g: affine_part(g, 1 - h))
                over_lagging(lambda i, h: None, main, pool, 2)

            @block.tensor
            def _(pe):
                def turn_w(i, h):
                    pe.wait_ge(w_now_done, i + 1)
                    reuse(pe, w_t_done, i)
                    for t in range(G):
                        mm = pe.transpose(bank[6][0:E, t * P:(t + 1) * P], w_now[:, h, t, :], ident[:, :])
                    mm.then_inc(w_turned, 1)

                def start(i, h):
                    pe.wait_ge(w_t_done, i + 1)
                    pe.wait_ge(y_in[h], loads(i, h))
                    reuse(pe, started, i)
                    for t in range(G):
                        out = bank[7][:, t * D:(t + 1) * D]
                        pe.matmul(out, w_t[:, t * P:(t + 1) * P], b12[:, :], start=True, stop=False)
                        mm = pe.matmul(out, y1_t[:, h, t * P:(t + 1) * P], ident[:, :], start=False, stop=True)
                    mm.then_inc(biased, 1)

                def experts(i, h, pair):
                    for half in range(2):
                        reuse(pe, used, (i * 2 + pair - 1) * 2 * E + (half + 1) * E)
                        for k in range(2):
                            t = 2 * pair + k
                            pe.matmul(bank[2 * k + half][:, :], y1_t[:, h, t * P:(t + 1) * P],
                                      w12[:, half * 4:half * 4 + 4, :].rearrange("p e d -> p (e d)"),
                                      start=True, stop=True).then_inc(made, 1)

                def front(i, h):
                    turn_w(i, h)
                    start(i, h)

                def main(i, h, nxt):
                    ago(i, 0, lambda g: experts(g, h, 0))
                    ago(i, -1, lambda g: turn_w(g, 1 - h))
                    ago(i, 0, lambda g: experts(g, h, 1))
                    ago(i, -1, lambda g: start(g, 1 - h))
                over_lagging(front, main, pe, 2)

            @block.scalar
            def _(act):
                def front(i, h):
                    act.wait_ge(w_turned, i + 1)
                    reuse(act, biased, i)
                    act.activation(w_t[:, :], bank[6][0:E, :], ACT.Identity).then_inc(w_t_done, 1)
                    act.wait_ge(biased, i + 1)
                    reuse(act, normed_done, (i - 1) * G)
                    act.activation(acc[:, h].rearrange("p t d -> p (t d)"), bank[7][:, :], ACT.Identity)\
                        .then_inc(started, 1)
                over_lagging(front, lambda i, h, nxt: ago(i, -1, lambda g: front(g, 1 - h)), act, 2)

            @block.vector
            def _(v):
                v.wait_ge(w_in, 2 * DMA)
                v.tensor_scalar(ln_g[:, :], ln_g[:, :], tanh_g, None, ALU.mult).then_inc(affine, 1)
                v.tensor_scalar(ln_b[:, :], ln_b[:, :], tanh_g, None, ALU.mult).then_inc(affine, 1)

                def take_weights(i, h):
                    reuse(v, w_turned, i - 1)
                    reuse(v, used, (i - 1) * G * E)
                    v.tensor_scalar(w_now[:, h], weight[:, bass.ds(i * G, G), :], 1.0, None, ALU.mult)\
                        .then_inc(w_now_done, 1)

                def accumulate(i, h, pair, experts):
                    for e in experts:
                        for k in range(2):
                            t = 2 * pair + k
                            if e % 4 == 0:
                                v.wait_ge(made, (i * 2 + pair) * 4 + e // 4 * 2 + k + 1)
                            if e:
                                v.wait_ge(used, (i * 2 + pair) * 2 * E + 2 * (e - 1) + k + 1)
                            elif k == 0:
                                v.wait_ge(started, i + 1)
                                v.wait_ge(w_now_done, i + 1)
                            v.scalar_tensor_tensor(
                                out=acc[:, h, t, :], in0=bank[2 * k + e // 4][:, (e % 4) * D:(e % 4 + 1) * D],
                                scalar=w_now[:, h, t, e:e + 1], in1=acc[:, h, t, :], op0=ALU.mult, op1=ALU.add)\
                                .then_inc(used, 1)

                def stats(i, h):
                    wait_apart(v, used, (i + 1) * G * E, chip.passed["v"])
                    ln.vector_stats(v, i, lambda t: acc[:, h, t, :])

                def norm(i, h):
                    reuse(v, x2_done, i - 1)
                    ln.vector_apply(v, i, lambda t: acc[:, h, t, :], normed[:, h], normed_done)

                def add_to_x(i, h):
                    v.wait_ge(moved, i + 1)
                    v.tensor_tensor(group_of(x_all, i), normed[:, h], group_of(x_all, i), ALU.add)\
                        .then_inc(x2_done, 1)

                def main(i, h, nxt):
                    ago(i, -1, lambda g: take_weights(g, 1 - h))
                    ago(i, 0, lambda g: accumulate(g, h, 0, range(0, 4)))
                    ago(i, 1, lambda g: stats(g, 1 - h))
                    ago(i, 0, lambda g: accumulate(g, h, 0, range(4, 8)))
                    ago(i, 1, lambda g: norm(g, 1 - h))
                    ago(i, 0, lambda g: accumulate(g, h, 1, range(8)))
                    ago(i, 2, lambda g: add_to_x(g, h))
                over_lagging(take_weights, main, v, 2)




def l1_mix(chip, ahead):
    nc, dram, x_all, bank, ident = chip.nc, chip.dram, chip.x_all, chip.bank, chip.ident
    with Phase(chip, "l1mix") as ph:
        ln = LayerNorm(ph, "ln")
        w_sim, b_sim = ph.sb("w_sim", [P, 3]), ph.sb("b_sim", [P, 1])
        wqv, bqv, block_of = ph.sb("wqv", [P, 4, D]), ph.sb("bqv", [P, D]), ph.sb("block_of", [P, 2])
        ctx, ctx_t = ph.sb("ctx", [P, 2, G, D]), ph.sb("ctx_t", [P, 2, N])
        e, e_t = ph.sb("e", [P, 2, G, D]), ph.sb("e_t", [P, 2, N])
        e_late, e_t_late = ph.sb("e_late", [P, 2, G, D]), ph.sb("e_t_late", [P, 2, N])
        key_t = ph.sb("key_t", [P, 2, N])
        top, own = ph.sb("top", [P, G]), ph.sb("own", [P, 2, G])
        sim, rsum = ph.sb("sim", [P, G, S]), ph.sb("rsum", [P, G])
        attn, attn_t = ph.sb("attn", [P, G, 2, S]), ph.sb("attn_t", [P, N])
        peak, peak_sum = ph.sb("peak", [G, 2]), ph.sb("peak_sum", [G, 2])
        pick, pick_two = ph.sb("pick", [G, 2, 2, S]), ph.sb("pick_two", [P, G, 2])
        hq_t, ehq_t, ehc_t = ph.sb("hq_t", [P, 2, N]), ph.sb("ehq_t", [P, N]), ph.sb("ehc_t", [P, N])
        out = ph.sb("out", [P, N])

        w_in, zeroed = ph.sem("w_in"), ph.sem("zeroed")
        x_in = [ph.sem("x_in0"), ph.sem("x_in1")]
        ctx_in = [ph.sem("ctx_in0"), ph.sem("ctx_in1")]
        e_done, e_turned, e_t_done, key_done = ph.sem("e"), ph.sem("e_turned"), ph.sem("e_t"), ph.sem("key")
        scored, topped, shifted, exped = ph.sem("scored"), ph.sem("topped"), ph.sem("shifted"), ph.sem("exped")
        summed, inverted, attn_done = ph.sem("summed"), ph.sem("inverted"), ph.sem("attn")
        attn_turned, attn_t_done, hq_done, hq_out = (ph.sem("attn_turned"), ph.sem("attn_t"), ph.sem("hq"),
                                                     ph.sem("hq_out"))
        own_done, own_turned, peaked, pick_shifted = (ph.sem("own"), ph.sem("own_turned"), ph.sem("peaked"),
                                                      ph.sem("pick_shifted"))
        pick_exped, pick_summed, pick_done, pick_turned = (ph.sem("pick_exped"), ph.sem("pick_summed"),
                                                           ph.sem("pick"), ph.sem("pick_turned"))
        pick_two_done, hc_made = ph.sem("pick_two"), ph.sem("hc_made")
        e_kept, e_t_kept = ph.sem("e_kept"), ph.sem("e_t_kept")
        feats_done, mixed, biased, x_done = ph.sem("feats"), ph.sem("mixed"), ph.sem("biased"), ph.sem("x")
        x2_dram = dram["x2"].rearrange("(n p) d -> p n d", p=P)
        ctx_dram = dram["ctx"].rearrange("(n p) d -> p n d", p=P)
        ctx_t_dram = dram["ctx_t"].rearrange("p (g n) -> p g n", g=GROUPS)
        tanh_g = chip.tanh_g[:, 1:2]
        tiles = lambda ap: ap.rearrange("p (t d) -> p t d", t=G)

        with nc.Block() as block:
            @block.sync
            def _(sp):
                for dst, name in ((w_sim[:, :], "l1_w_sim"), (b_sim[:, :], "l1_b_sim"), (wqv[:, :, :], "l1_wqv"),
                                  (bqv[:, :], "l1_bqv"), (block_of[:, :], "block_of")):
                    sp.dma_start(dst, dram[name]).then_inc(w_in, DMA)

                def load_x(i, h):
                    reuse(sp, x_in[h], loads(i - 2, h))
                    sp.dma_start(group_of(x_all, i), group_of(x2_dram, i)).then_inc(x_in[h], DMA)

                def load_ctx(i, h):
                    reuse(sp, hq_done, i - 1)
                    sp.dma_start(ctx[:, h], group_of(ctx_dram, i)).then_inc(ctx_in[h], DMA)
                    sp.dma_start(ctx_t[:, h], ctx_t_dram[:, bass.ds(i, 1), :].rearrange("p a n -> p (a n)"))\
                        .then_inc(ctx_in[h], DMA)

                def front(i, h):
                    load_x(0, 0)
                    load_x(1, 1)

                def main(i, h, nxt):
                    ago(i, 0, lambda g: load_ctx(g, h))
                    ago(i, -2, lambda g: load_x(g, h))
                    if isinstance(i, int) and i == 1:
                        ahead.start(sp)
                over_lagging(front, main, sp, 2)

            @block.gpsimd
            def _(pool):
                pool.memset(attn[:, :, :, :], 0.0).then_inc(zeroed, 1)
                over_lagging(lambda i, h: ln.pool_rstd(pool, i),
                             lambda i, h, nxt: ago(i, -1, lambda g: ln.pool_rstd(pool, g)), pool, 3)

            @block.tensor
            def _(pe):
                pe.wait_ge(w_in, 5 * DMA)

                def turn_e(i, h):
                    pe.wait_ge(e_done, i * G + G)
                    reuse(pe, e_t_done, i)
                    transposes(pe, bank[0], [e[:, h, t, :] for t in range(G)], ident).then_inc(e_turned, 1)

                def similarity(i, h):
                    pe.wait_ge(key_done, i + 1)
                    pe.wait_ge(ctx_in[h], loads(i, h, 2))
                    reuse(pe, own_done, i * 2)
                    reuse(pe, shifted, i)
                    for t in range(G):
                        for b in range(2):
                            c = slice(t * P + b * S, t * P + (b + 1) * S)
                            pe.matmul(bank[1][b * S:(b + 1) * S, t * S:(t + 1) * S], key_t[:, h, c], ctx_t[:, h, c],
                                      start=True, stop=True)
                            mm = pe.matmul(bank[1][b * S:(b + 1) * S, G * S + t:G * S + t + 1], e_t[:, h, c],
                                           w_sim[:, 0:1], start=True, stop=True)
                    mm.then_inc(scored, 1)

                def turn_rows(i, h):
                    pe.wait_ge(own_done, i * 2 + 2)
                    reuse(pe, pick_shifted, i)
                    pe.transpose(bank[2][0:G, 0:P], own[:, h, :], ident[:, :]).then_inc(own_turned, 1)
                    pe.wait_ge(attn_done, i * 2 + 2)
                    reuse(pe, attn_t_done, i)
                    transposes(pe, bank[3], [attn[:, t].rearrange("p b s -> p (b s)") for t in range(G)], ident)\
                        .then_inc(attn_turned, 1)

                def attend(i, h):
                    pe.wait_ge(attn_t_done, i + 1)
                    reuse(pe, hq_out, i)
                    for t in range(G):
                        mm = pe.matmul(bank[4][:, t * P:(t + 1) * P], ctx[:, h, t, :], attn_t[:, t * P:(t + 1) * P],
                                       start=True, stop=True)
                    mm.then_inc(hq_done, 1)

                def turn_pick(i, h):
                    reuse(pe, pick_two_done, i)
                    wait_apart(pe, pick_done, i + 1, chip.passed["pe"])
                    pe.transpose(bank[5][:, 0:G], pick[:, h].rearrange("p b s -> p (b s)"), ident[0:G, 0:G])\
                        .then_inc(pick_turned, 1)

                def pool_rows(i, h):
                    pe.wait_ge(pick_two_done, i + 1)
                    pe.wait_ge(e_kept, i + 1)
                    reuse(pe, feats_done, i * 2)
                    for t in range(G):
                        mm = pe.matmul(bank[6][:, 2 * t:2 * t + 2], e_late[:, h, t, :], pick_two[:, t, :],
                                       start=True, stop=True)
                    mm.then_inc(hc_made, 1)

                def mix(i, h):
                    pe.wait_ge(hq_out, i + 1)
                    pe.wait_ge(e_t_kept, i + 1)
                    pe.wait_ge(feats_done, i * 2 + 2)
                    reuse(pe, biased, i)
                    for t in range(G):
                        c = slice(t * P, (t + 1) * P)
                        for k, feat in enumerate((e_t_late[:, h, c], hq_t[:, h, c], ehq_t[:, c], ehc_t[:, c])):
                            mm = pe.matmul(bank[7][:, c], feat, wqv[:, k, :], start=(k == 0), stop=(k == 3))
                    mm.then_inc(mixed, 1)

                def main(i, h, nxt):
                    ago(i, 1, lambda g: turn_rows(g, 1 - h))
                    ago(i, 0, lambda g: similarity(g, h))
                    ago(i, 3, lambda g: mix(g, 1 - h))
                    ago(i, 2, lambda g: turn_pick(g, h))
                    ago(i, 1, lambda g: attend(g, 1 - h))
                    ago(i, -1, lambda g: turn_e(g, 1 - h))
                    ago(i, 2, lambda g: pool_rows(g, h))
                over_lagging(turn_e, main, pe, 3)

            @block.scalar
            def _(act):
                def e_out(i, h):
                    act.wait_ge(e_turned, i + 1)
                    reuse(act, e_t_kept, i - 1)
                    act.activation(e_t[:, h], bank[0][:, :], ACT.Identity).then_inc(e_t_done, 1)

                def keep_e(i, h):
                    act.wait_ge(e_done, i * G + G)
                    reuse(act, hc_made, i - 1)
                    act.activation(e_late[:, h], e[:, h], ACT.Identity).then_inc(e_kept, 1)
                    act.wait_ge(e_t_done, i + 1)
                    reuse(act, mixed, i - 1)
                    act.activation(e_t_late[:, h], e_t[:, h], ACT.Identity).then_inc(e_t_kept, 1)

                def exp_rows(i):
                    act.wait_ge(shifted, i + 1)
                    act.activation(sim[:, :, :], sim[:, :, :], ACT.Exp).then_inc(exped, 1)

                def attention_out(i):
                    act.wait_ge(attn_turned, i + 1)
                    act.activation(attn_t[:, :], bank[3][:, :], ACT.Identity).then_inc(attn_t_done, 1)

                def hq_part(i, h):
                    act.wait_ge(hq_done, i + 1)
                    reuse(act, mixed, i - 1)
                    act.activation(hq_t[:, h], bank[4][:, :], ACT.Identity).then_inc(hq_out, 1)

                def exp_pick(i, h):
                    act.wait_ge(pick_shifted, i + 1)
                    act.activation(pick[:, h], pick[:, h], ACT.Exp).then_inc(pick_exped, 1)

                def main(i, h, nxt):
                    ago(i, 1, attention_out)
                    ago(i, 0, exp_rows)
                    ago(i, 1, lambda g: keep_e(g, 1 - h))
                    ago(i, 1, lambda g: hq_part(g, 1 - h))
                    ago(i, -1, lambda g: e_out(g, 1 - h))
                    ago(i, 1, lambda g: exp_pick(g, 1 - h))
                over_lagging(e_out, main, act, 3)

            @block.vector
            def _(v):
                v.wait_ge(w_in, 5 * DMA)
                v.wait_ge(zeroed, 1)
                scores = bank[1][:, 0:G * S].rearrange("p (t s) -> p t s", t=G)
                wide = lambda ap: ap[:, :].unsqueeze(2).to_broadcast([P, G, S])
                maxima = bank[2][0:G, 0:P].rearrange("p (b s) -> p b s", b=2)
                over = lambda ap: ap[:, :].unsqueeze(2).to_broadcast([G, 2, S])

                def stats(i, h):
                    wait_apart(v, x_in[h], loads(i, h), chip.passed["v"])
                    ln.vector_stats(v, i, lambda t: tile_of(x_all, i, t))

                def apply(i, h):
                    reuse(v, e_kept, i - 1)
                    ln.vector_apply(v, i, lambda t: tile_of(x_all, i, t), e[:, h], e_done)

                def make_key(i, h):
                    v.wait_ge(e_t_done, i + 1)
                    v.tensor_scalar(key_t[:, h], e_t[:, h], w_sim[:, 2:3], w_sim[:, 1:2], ALU.mult, ALU.add)\
                        .then_inc(key_done, 1)

                def rows(i, h):
                    v.wait_ge(scored, i + 1)
                    v.tensor_reduce(top[:, :], scores, AX.X, ALU.max).then_inc(topped, 1)
                    v.wait_ge(topped, i + 1)
                    v.tensor_tensor(sim[:, :, :], scores, wide(top), ALU.subtract).then_inc(shifted, 1)
                    reuse(v, own_turned, i - 1)
                    v.tensor_tensor(own[:, h, :], bank[1][:, G * S:G * S + G], top[:, :], ALU.add).then_inc(own_done, 1)
                    v.wait_ge(own_done, i * 2 + 1)
                    v.tensor_scalar(own[:, h, :], own[:, h, :], b_sim[:, 0:1], None, ALU.add).then_inc(own_done, 1)

                def normalize_rows(i):
                    v.wait_ge(exped, i + 1)
                    v.tensor_reduce(rsum[:, :], sim[:, :, :], AX.X, ALU.add).then_inc(summed, 1)
                    v.wait_ge(summed, i + 1)
                    v.reciprocal(rsum[:, :], rsum[:, :]).then_inc(inverted, 1)
                    v.wait_ge(inverted, i + 1)
                    reuse(v, attn_turned, i)
                    for b in range(2):
                        r = slice(b * S, (b + 1) * S)
                        v.tensor_tensor(attn[r, :, b, :], sim[r, :, :], rsum[r, :].unsqueeze(2).to_broadcast([S, G, S]),
                                        ALU.mult).then_inc(attn_done, 1)

                def shift_pick(i, h):
                    v.wait_ge(own_turned, i + 1)
                    v.tensor_reduce(peak[:, :], maxima, AX.X, ALU.max).then_inc(peaked, 1)
                    v.wait_ge(peaked, i + 1)
                    reuse(v, pick_turned, i - 1)
                    v.tensor_tensor(pick[:, h], maxima, over(peak), ALU.subtract).then_inc(pick_shifted, 1)

                def normalize_pick(i, h):
                    v.wait_ge(pick_exped, i + 1)
                    v.tensor_reduce(peak_sum[:, :], pick[:, h], AX.X, ALU.add).then_inc(pick_summed, 1)
                    v.wait_ge(pick_summed, i * 2 + 1)
                    v.reciprocal(peak_sum[:, :], peak_sum[:, :]).then_inc(pick_summed, 1)
                    v.wait_ge(pick_summed, i * 2 + 2)
                    v.tensor_tensor(pick[:, h], pick[:, h], over(peak_sum), ALU.mult).then_inc(pick_done, 1)

                def spread_pick(i):
                    v.wait_ge(pick_turned, i + 1)
                    v.tensor_tensor(pick_two[:, :, :], bank[5][:, 0:G].unsqueeze(2).to_broadcast([P, G, 2]),
                                    block_of[:, :].unsqueeze(1).to_broadcast([P, G, 2]), ALU.mult)\
                        .then_inc(pick_two_done, 1)

                def times_hq(i, h):
                    v.wait_ge(hq_out, i + 1)
                    v.wait_ge(e_t_kept, i + 1)
                    reuse(v, mixed, i)
                    v.tensor_tensor(ehq_t[:, :], e_t_late[:, h], hq_t[:, h], ALU.mult).then_inc(feats_done, 1)

                def times_hc(i, h):
                    v.wait_ge(hc_made, i + 1)
                    v.tensor_tensor(ehc_t[:, :].rearrange("p (b s) -> p b s", b=BG),
                                    e_t_late[:, h].rearrange("p (b s) -> p b s", b=BG),
                                    bank[6][:, 0:BG].unsqueeze(2).to_broadcast([P, BG, S]), ALU.mult)\
                        .then_inc(feats_done, 1)

                def output(i):
                    v.wait_ge(mixed, i + 1)
                    reuse(v, x_done, i)
                    v.tensor_tensor(tiles(out[:, :]), tiles(bank[7][:, :]),
                                    bqv[:, :].unsqueeze(1).to_broadcast([P, G, D]), ALU.add).then_inc(biased, 1)
                    v.wait_ge(biased, i + 1)
                    v.scalar_tensor_tensor(out=group_of(x_all, i), in0=tiles(out[:, :]), scalar=tanh_g,
                                           in1=group_of(x_all, i), op0=ALU.mult, op1=ALU.add).then_inc(x_done, 1)

                def front(i, h):
                    stats(i, h)
                    apply(i, h)
                    make_key(i, h)

                def main(i, h, nxt):
                    ago(i, 2, lambda g: normalize_pick(g, h))
                    ago(i, -1, lambda g: stats(g, 1 - h))
                    ago(i, 0, lambda g: rows(g, h))
                    ago(i, -1, lambda g: apply(g, 1 - h))
                    ago(i, 1, lambda g: shift_pick(g, 1 - h))
                    ago(i, 0, normalize_rows)
                    ago(i, 2, spread_pick)
                    ago(i, 2, lambda g: times_hq(g, h))
                    ago(i, 3, output)
                    ago(i, -1, lambda g: make_key(g, 1 - h))
                    ago(i, 2, lambda g: times_hc(g, h))
                over_lagging(front, main, v, 3)


def l1_ffn(chip, ahead):
    nc, dram, x_all, bank, ident = chip.nc, chip.dram, chip.x_all, chip.bank, chip.ident
    E, EG, PER = L1_E, L1_GROUPS, L1_E // L1_GROUPS
    with Phase(chip, "l1ffn") as ph:
        ln = LayerNorm(ph, "ln")
        w1, w3, w2 = ahead.tensors
        wg, b1, b3, b2 = ph.sb("wg", [P, E]), ph.sb("b1", [P, E]), ph.sb("b3", [P, E]), ph.sb("b2", [E, D])
        earlier = ph.sb("earlier", [P, EG, EG])
        w13_high, w13_low = (ph.sb(n, [P, 2, E, P], F32R) for n in ("w13_high", "w13_low"))
        z, z_t = ph.sb("z", [P, G, D]), ph.sb("z_t", [P, N])
        z_high, z_low = ph.sb("z_high", [P, 2, N], F32R), ph.sb("z_low", [P, 2, N], F32R)
        gate, kept = ph.sb("gate", [P, G, E]), ph.sb("kept", [P, G, E])
        gtop, above, tied = ph.sb("gtop", [P, G, EG]), ph.sb("above", [P, G * EG, EG]), ph.sb("tied", [P, G * EG, EG])
        rank, gsel = ph.sb("rank", [P, G * EG]), ph.sb("gsel", [P, G * EG])
        best8, sel, tie = ph.sb("best8", [P, G, 8]), ph.sb("sel", [P, G, E]), ph.sb("tie", [P, G, E])
        n_above, tie_no = ph.sb("n_above", [P, G]), ph.sb("tie_no", [P, G, E])
        ones = ph.sb("ones", [P, E])
        wsum, w = ph.sb("wsum", [P, G]), ph.sb("w", [P, 2, G, E])
        w_t = ph.sb("w_t", [E, 2, N])
        K = 4
        act1, act3, hid = ph.sb("act1", [P, K, N]), ph.sb("act3", [P, K, N]), ph.sb("hid", [P, K, N])
        bias, acc = ph.sb("bias", [P, G, D]), ph.sb("acc", [P, G, D])

        w_in, ones_set = ph.sem("w_in"), ph.sem("ones_set")
        z_done, z_turned, z_t_done = ph.sem("z"), ph.sem("z_turned"), ph.sem("z_t")
        w_high_done, w_low_done = ph.sem("w_high"), ph.sem("w_low")
        z_high_done, z_low_done = ph.sem("z_high"), ph.sem("z_low")
        gated, gate_done, route = ph.sem("gated"), ph.sem("gate"), ph.sem("route_steps")
        w_turned, w_t_done = ph.sem("w_turned"), ph.sem("w_t")
        made1, made3 = ph.sem("made1"), ph.sem("made3")
        act1_done, act3_done, hid_done = ph.sem("act1"), ph.sem("act3"), ph.sem("hid")
        biased, bias_out = ph.sem("biased"), ph.sem("bias_out")
        made_y, used, x_done = ph.sem("made_y"), ph.sem("used"), ph.sem("x")
        tanh_g = chip.tanh_g[:, 5:6]
        PARTS = (5 + 2 * G, 6 + 2 * G, 7)
        STEPS = sum(PARTS)

        with nc.Block() as block:
            @block.sync
            def _(sp):
                for dst, name in ((wg[:, :], "l1_wg"), (b1[:, :], "l1_b1"), (b3[:, :], "l1_b3"), (b2[:, :], "l1_b2"),
                                  (earlier[:, :, :], "earlier4")):
                    sp.dma_start(dst, dram[name]).then_inc(w_in, DMA)

            @block.gpsimd
            def _(pool):
                pool.memset(ones[:, :], 1.0).then_inc(ones_set, 1)
                ahead.wait(pool)

                def gate_hidden(i, experts):
                    for e in experts:
                        pool.wait_ge(act3_done, i * E + e + 1)
                        reuse(pool, made_y, i * E + e - K + 1)
                        pool.tensor_tensor(hid[:, e % K], act1[:, e % K], act3[:, e % K], ALU.mult)\
                            .then_inc(hid_done, 1)

                def rstd(i, h):
                    ln.pool_rstd(pool, i)

                def split_weights(i, h):
                    for e in range(0, E, 4):
                        for k, source in enumerate((w1, w3)):
                            pool.wait_ge(w_high_done, e // 2 + k + 1)
                            pool.tensor_tensor(w13_low[:, k, e:e + 4, :], source[:, e:e + 4, :],
                                               w13_high[:, k, e:e + 4, :].bitcast(F32), ALU.subtract)\
                                .then_inc(w_low_done, 1)

                def lead(i, h):
                    gate_hidden(i, range(2))

                def front(i, h, *parts):
                    for part in parts or (rstd, split_weights, lead):
                        part(i, h)

                def main(i, h, nxt):
                    gate_hidden(i, range(2, 6))
                    nxt(rstd)
                    gate_hidden(i, range(6, E))
                    nxt(lead)
                over_groups(front, main, pool)

            @block.tensor
            def _(pe):
                pe.wait_ge(w_in, 5 * DMA)
                ahead.wait(pe)

                def turn(i, h):
                    pe.wait_ge(z_done, i * G + G)
                    reuse(pe, w_t_done, i)
                    transposes(pe, bank[0], [z[:, t, :] for t in range(G)], ident).then_inc(z_turned, 1)

                def router(i, h):
                    pe.wait_ge(z_t_done, i + 1)
                    reuse(pe, bias_out, i)
                    for t in range(G):
                        for b in range(2):
                            r = slice(b * S, (b + 1) * S)
                            mm = pe.matmul(bank[7][r, t * E:(t + 1) * E], z_t[:, t * P + b * S:t * P + (b + 1) * S],
                                           wg[:, :], start=True, stop=True)
                    mm.then_inc(gated, 1)

                def weights(i, h):
                    pe.wait_ge(route, (i + 1) * STEPS)
                    pe.wait_ge(z_low_done, i + 1)
                    for t in range(G):
                        mm = pe.transpose(bank[0][0:E, t * P:(t + 1) * P], w[:, h, t, :], ident[:, :])
                    mm.then_inc(w_turned, 1)

                def front(i, h, *parts):
                    for part in parts or (turn, router, weights, lead0, lead1):
                        part(i, h)

                def lead0(i, h):
                    hidden(i, h, 0)

                def lead1(i, h):
                    hidden(i, h, 1)

                def hidden(i, h, e):
                    k = e % 2
                    if e == 0:
                        pe.wait_ge(z_low_done, i + 1)
                    pe.wait_ge(w_low_done, e // 4 * 2 + 2)
                    z_parts = (z_high[:, h], z_low[:, h])
                    reuse(pe, act1_done, i * E + e - 1)
                    split_product(pe, bank[1 + k][:, :], (w13_high[:, 0, e, :], w13_low[:, 0, e, :]), z_parts)\
                        .then_inc(made1, 1)
                    reuse(pe, act3_done, i * E + e - 1)
                    split_product(pe, bank[3 + k][:, :], (w13_high[:, 1, e, :], w13_low[:, 1, e, :]), z_parts)\
                        .then_inc(made3, 1)

                def outputs(i, h, e):
                    k = e % 2
                    pe.wait_ge(hid_done, i * E + e + 1)
                    reuse(pe, used, i * E + e - 1)
                    for t in range(G):
                        mm = pe.matmul(bank[5 + k][:, t * D:(t + 1) * D], hid[:, e % K, t * P:(t + 1) * P], w2[:, e, :],
                                       start=True, stop=True)
                    mm.then_inc(made_y, 1)

                def main(i, h, nxt):
                    pe.wait_ge(w_t_done, i + 1)
                    for t in range(G):
                        mm = pe.matmul(bank[7][:, t * D:(t + 1) * D], w_t[:, h, t * P:(t + 1) * P], b2[:, :],
                                       start=True, stop=True)
                    mm.then_inc(biased, 1)
                    for e in range(E):
                        if e + 2 < E:
                            hidden(i, h, e + 2)
                        else:
                            nxt(lead1 if e + 1 == E else lead0)
                        outputs(i, h, e)
                        for at, part in ((6, turn), (8, router), (E - 1, weights)):
                            if e == at:
                                nxt(part)
                over_groups(front, main, pe)

            @block.scalar
            def _(act):
                act.wait_ge(w_in, 5 * DMA)
                ahead.wait(act)

                for e in range(0, E, 4):
                    for k, source in enumerate((w1, w3)):
                        act.activation(w13_high[:, k, e:e + 4, :], source[:, e:e + 4, :], ACT.Identity).then_inc(w_high_done, 1)

                def z_out(i, h):
                    act.wait_ge(z_turned, i + 1)
                    reuse(act, gated, i)
                    act.activation(z_t[:, :], bank[0][:, :], ACT.Identity).then_inc(z_t_done, 1)
                    act.activation(z_high[:, h], bank[0][:, :], ACT.Identity).then_inc(z_high_done, 1)

                def gates(i, h):
                    act.wait_ge(gated, i + 1)
                    act.activation(gate[:, :, :].rearrange("p t e -> p (t e)"), bank[7][:, 0:G * E], ACT.Sigmoid)\
                        .then_inc(gate_done, 1)

                def weights_out(i, h):
                    act.wait_ge(w_turned, i + 1)
                    act.activation(w_t[:, h], bank[0][0:E, :], ACT.Identity).then_inc(w_t_done, 1)

                def front(i, h, *parts):
                    for part in parts or (z_out, gates, weights_out, lead):
                        part(i, h)

                def drain(i, e):
                    act.wait_ge(made1, i * E + e + 1)
                    reuse(act, hid_done, i * E + e - K + 1)
                    act.activation(act1[:, e % K], bank[1 + e % 2][:, :], ACT.Silu, bias=b1[:, e:e + 1])\
                        .then_inc(act1_done, 1)
                    act.wait_ge(made3, i * E + e + 1)
                    act.activation(act3[:, e % K], bank[3 + e % 2][:, :], ACT.Identity, bias=b3[:, e:e + 1])\
                        .then_inc(act3_done, 1)

                def lead(i, h):
                    drain(i, 0)
                    drain(i, 1)

                def main(i, h, nxt):
                    act.wait_ge(biased, i + 1)
                    reuse(act, used, (i - 1) * E + 1)
                    act.activation(bias[:, :, :].rearrange("p t d -> p (t d)"), bank[7][:, :], ACT.Identity)\
                        .then_inc(bias_out, 1)
                    for e in range(2, E):
                        drain(i, e)
                        for at, part in ((8, z_out), (10, gates)):
                            if e == at:
                                nxt(part)
                    nxt(lead, weights_out)
                over_groups(front, main, act)

            @block.vector
            def _(v):
                v.wait_ge(w_in, 5 * DMA)
                ahead.wait(v)
                v.wait_ge(ones_set, 1)

                def stats(i, h):
                    ln.vector_stats(v, i, lambda t: tile_of(x_all, i, t))

                def apply(i, h):
                    ln.vector_apply(v, i, lambda t: tile_of(x_all, i, t), z, z_done)

                def z_rest(i, h):
                    v.wait_ge(z_high_done, i + 1)
                    reuse(v, made3, (i - 1) * E)
                    v.tensor_tensor(z_low[:, h], bank[0][:, :], z_high[:, h].bitcast(F32), ALU.subtract)\
                        .then_inc(z_low_done, 1)

                at = steps = 0

                def step(instruction):
                    nonlocal steps
                    steps += 1
                    instruction.then_inc(route, 1)

                def settled():
                    v.wait_ge(route, at + steps)

                def choose_groups(i, h):
                    nonlocal at, steps
                    at, steps = i * STEPS, 0
                    by_group = gate[:, :, :].rearrange("p t (g e) -> p t g e", g=EG)
                    v.wait_ge(gate_done, i + 1)
                    step(v.tensor_reduce(gtop[:, :, :], by_group, AX.X, ALU.max))
                    settled()
                    for t in range(G):
                        others = gtop[:, t, :].unsqueeze(1).to_broadcast([P, EG, EG])
                        own = gtop[:, t, :].unsqueeze(2).to_broadcast([P, EG, EG])
                        step(v.tensor_tensor(above[:, t * EG:(t + 1) * EG, :], others, own, ALU.is_gt))
                        step(v.tensor_tensor(tied[:, t * EG:(t + 1) * EG, :], others, own, ALU.is_equal))
                    settled()
                    step(v.tensor_tensor(tied[:, :, :].rearrange("p (t a) b -> p t a b", t=G),
                                         tied[:, :, :].rearrange("p (t a) b -> p t a b", t=G),
                                         earlier[:, :, :].unsqueeze(1).to_broadcast([P, G, EG, EG]), ALU.mult))
                    settled()
                    step(v.tensor_tensor(above[:, :, :], above[:, :, :], tied[:, :, :], ALU.add))
                    settled()
                    step(v.tensor_reduce(rank[:, :], above[:, :, :], AX.X, ALU.add))
                    settled()
                    step(v.tensor_scalar(gsel[:, :], rank[:, :], float(L1_TOPG), None, ALU.is_lt))
                    settled()
                    assert steps == PARTS[0]

                def choose_experts(i, h):
                    nonlocal at, steps
                    at, steps = i * STEPS, PARTS[0]
                    by_group = gate[:, :, :].rearrange("p t (g e) -> p t g e", g=EG)
                    wide = gsel[:, :].rearrange("p (t g) -> p t g", g=EG).unsqueeze(3).to_broadcast([P, G, EG, PER])
                    kept4 = kept[:, :, :].rearrange("p t (g e) -> p t g e", g=EG)
                    settled()
                    step(v.tensor_tensor(kept4, by_group, wide, ALU.mult))
                    settled()
                    step(v.tensor_tensor(kept4, kept4, wide, ALU.add))
                    settled()
                    step(v.tensor_scalar(kept[:, :, :], kept[:, :, :], -1.0, None, ALU.add))
                    wait_apart(v, route, at + steps, chip.passed["v"])
                    for t in range(G):
                        v.max(best8[:, t, :], kept[:, t, :]).then_inc(route, 1)
                    steps += G
                    settled()
                    fourth = best8[:, :, L1_TOPK - 1].unsqueeze(2).to_broadcast([P, G, E])
                    step(v.tensor_tensor(sel[:, :, :], kept[:, :, :], fourth, ALU.is_gt))
                    step(v.tensor_tensor(tie[:, :, :], kept[:, :, :], fourth, ALU.is_equal))
                    settled()
                    step(v.tensor_reduce(n_above[:, :], sel[:, :, :], AX.X, ALU.add))
                    for t in range(G):
                        v.tensor_tensor_scan(tie_no[:, t, :], ones[:, :], tie[:, t, :], 0.0, ALU.mult, ALU.add)\
                            .then_inc(route, 1)
                    steps += G
                    assert steps == PARTS[0] + PARTS[1]

                def weigh(i, h):
                    nonlocal at, steps
                    at, steps = i * STEPS, PARTS[0] + PARTS[1]
                    settled()
                    step(v.tensor_tensor(tie_no[:, :, :], tie_no[:, :, :], n_above[:, :].unsqueeze(2)
                                         .to_broadcast([P, G, E]), ALU.add))
                    settled()
                    step(v.scalar_tensor_tensor(out=tie[:, :, :], in0=tie_no[:, :, :], scalar=float(L1_TOPK),
                                                in1=tie[:, :, :], op0=ALU.is_le, op1=ALU.mult))
                    settled()
                    step(v.tensor_tensor(sel[:, :, :], sel[:, :, :], tie[:, :, :], ALU.add))
                    settled()
                    step(v.tensor_tensor(sel[:, :, :], sel[:, :, :], gate[:, :, :], ALU.mult))
                    settled()
                    step(v.tensor_reduce(wsum[:, :], sel[:, :, :], AX.X, ALU.add))
                    settled()
                    step(v.reciprocal(wsum[:, :], wsum[:, :]))
                    settled()
                    step(v.scalar_tensor_tensor(out=w[:, h], in0=sel[:, :, :], scalar=ROUTE_SCALE,
                                                in1=wsum[:, :].unsqueeze(2).to_broadcast([P, G, E]),
                                                op0=ALU.mult, op1=ALU.mult))
                    assert steps == STEPS

                def front(i, h, *parts):
                    for part in parts or (stats, apply, z_rest, choose_groups, choose_experts, weigh):
                        part(i, h)

                def add_output(i, h, e):
                    v.wait_ge(made_y, i * E + e + 1)
                    if e:
                        v.wait_ge(used, i * E + e)
                    else:
                        v.wait_ge(bias_out, i + 1)
                        reuse(v, x_done, i)
                    for t in range(G):
                        y = bank[5 + e % 2][:, t * D:(t + 1) * D]
                        before = acc[:, t, :] if e else bias[:, t, :]
                        mm = v.scalar_tensor_tensor(out=acc[:, t, :], in0=y, scalar=w[:, h, t, e:e + 1],
                                                    in1=before, op0=ALU.mult, op1=ALU.add)
                    mm.then_inc(used, 1)

                def main(i, h, nxt):
                    for e in range(E):
                        add_output(i, h, e)
                        for at_e, part in ((0, stats), (4, apply), (8, z_rest), (9, choose_groups), (11, choose_experts), (12, weigh)):
                            if e == at_e:
                                nxt(part)
                    v.wait_ge(used, (i + 1) * E)
                    v.scalar_tensor_tensor(out=group_of(x_all, i), in0=acc[:, :, :], scalar=tanh_g,
                                           in1=group_of(x_all, i), op0=ALU.mult, op1=ALU.add).then_inc(x_done, 1)
                over_groups(front, main, v)


UNITS = 2 * G


def over_slots(front, slot, parts, eng):
    def main(i, h, nxt):
        for s in range(UNITS):
            slot(i, h, s)
            if s in parts:
                nxt(*parts[s])
    over_lagging(front, main, eng, 1)


def unit_ago(i, s, back, do):
    ago(i, 0 if s >= back else 1, lambda g: do(g, (s - back) % UNITS))


def cross_attention(chip, name, gate, masked_scores, after, ahead=None):
    nc, dram, x_all, bank, ident = chip.nc, chip.dram, chip.x_all, chip.bank, chip.ident
    F, J, JP = 2, HEADS // 2, HEADS // 4
    HP = HEADS // 2
    U, TURN, MULT = UNITS, 3, 4
    scale = HD ** -0.5
    W = 2 * HD + 2
    with Phase(chip, name) as ph:
        ln = LayerNorm(ph, "ln")
        wq, wk, wv, wo = (ph.sb(n, [P, D]) for n in ("wq", "wk", "wv", "wo"))
        bk, bq, bv, bo = ph.sb("bk", [P, F]), ph.sb("bq", [P, F]), ph.sb("bv", [P, D // 2]), ph.sb("bo", [P, D])
        of_head, k_bias, q_bias = ph.sb("of_head", [P, J]), ph.sb("k_bias", [P, F, J]), ph.sb("q_bias", [P, F])
        ctx_t = ph.sb("ctx_t", [P, 2, N])
        z, z_t = ph.sb("z", [P, 2, G, D]), ph.sb("z_t", [P, N])
        q_blocks, k_heads = ph.sb("q_blocks", [P, 2, F, G, P]), ph.sb("k_heads", [P, 2, F, G, J, S])
        v_blocks = ph.sb("v_blocks", [P, 2, BG, HP, W])
        probs, top, probs_t = ph.sb("probs", [P, U, 512]), ph.sb("top", [P, U, J]), ph.sb("probs_t", [P, 2, JP, P])
        rsum, o, o_t = ph.sb("rsum", [P, 2, 2 * HP, 2]), ph.sb("o", [P, G, D]), ph.sb("o_t", [P, N])
        out = ph.sb("out", [P, G, D])

        w_in, blocks_set, qk_consts = ph.sem("w_in"), ph.sem("blocks_set"), ph.sem("qk_consts")
        ctx_in = [ph.sem("ctx_in0"), ph.sem("ctx_in1")]
        z_done, z_turned, z_t_done = ph.sem("z"), ph.sem("z_turned"), ph.sem("z_t")
        q_made, k_made, v_made = ph.sem("q_made"), ph.sem("k_made"), ph.sem("v_made")
        q_out, k_out, v_out = ph.sem("q_out"), ph.sem("k_out"), ph.sem("v_out")
        scored, capped, topped = ph.sem("scored"), ph.sem("capped"), ph.sem("topped")
        shifted, exped = ph.sem("shifted"), ph.sem("exped")
        p_turned, p_t_done, pv_done = ph.sem("p_turned"), ph.sem("p_t"), ph.sem("pv")
        rsum_done, o_done = ph.sem("rsum"), ph.sem("o")
        o_turned, o_t_done, projected = ph.sem("o_turned"), ph.sem("o_t"), ph.sem("projected")
        proj_out = ph.sem("proj_out")
        caps = masked_scores(ph, chip)
        tail = after(ph, chip, bo)
        ctx_t_dram = dram["ctx_t"].rearrange("p (g n) -> p g n", g=GROUPS)
        tanh_g = chip.tanh_g[:, gate:gate + 1]
        half_rows = lambda b: slice(b * S, (b + 1) * S)

        with nc.Block() as block:
            @block.sync
            def _(sp):
                names = ((wq, "wq"), (wk, "wk"), (wv, "wv"), (wo, "wo"), (bk, "bk"), (bv, "bv"), (bo, "bo"), (bq, "bq"))
                for dst, what in names:
                    sp.dma_start(dst[:, :], dram[f"{name}_{what}"]).then_inc(w_in, DMA)
                sp.dma_start(of_head[:, :], dram["of_head"]).then_inc(w_in, DMA)
                caps.load(sp)
                tail.load(sp)

                def step(i, h):
                    reuse(sp, v_made, i - 1)
                    sp.dma_start(ctx_t[:, h], ctx_t_dram[:, bass.ds(i, 1), :].rearrange("p a n -> p (a n)"))\
                        .then_inc(ctx_in[h], DMA)
                    if ahead and isinstance(i, int) and i == 1:
                        ahead.start(sp)
                each_group(step, sp)

            @block.gpsimd
            def _(pool):
                pool.memset(q_blocks[:, :, :, :, :], 0.0).then_inc(blocks_set, 1)
                pool.memset(v_blocks[:, :, :, :, :], 0.0).then_inc(blocks_set, 1)
                pool.wait_ge(blocks_set, 2)
                for j2 in range(2):
                    pool.memset(v_blocks[half_rows(j2), :, :, :, 2 * HD + j2], 1.0).then_inc(blocks_set, 1)

                def rstd(i, h):
                    ln.pool_rstd(pool, i)

                def shift(i, u):
                    pool.wait_ge(topped, i * U + u + 1)
                    row = probs[:, u].rearrange("p (j k) -> p j k", k=S)
                    pool.tensor_tensor(row, row, top[:, u, :].unsqueeze(2).to_broadcast([P, J, S]), ALU.subtract)\
                        .then_inc(shifted, 1)

                def front(i, h, *parts):
                    for part in parts or (rstd,):
                        part(i, h)

                def slot(i, h, s):
                    unit_ago(i, s, 0, shift)
                    if s == 6:
                        ago(i, 1, lambda g: tail.pool_rstd(pool, g))
                    if s == 7:
                        ago(i, 1, lambda g: tail.pool(pool, g))
                        unit_ago(i, s, 0, lambda g, u: tail.pool_residual(pool, g, h, z[:, h], proj_out))
                over_slots(front, slot, {0: (rstd,)}, pool)

            @block.tensor
            def _(pe):
                pe.wait_ge(w_in, 9 * DMA)

                def halves_of(dst, w, src, done):
                    moving = src.rearrange("p (t b s) -> p t b s", t=G, b=2)
                    for b in range(2):
                        for f in range(F):
                            mm = pe.matmul(dst[half_rows(b), f * N // 2:(f + 1) * N // 2],
                                           w[:, f * S:(f + 1) * S], moving[:, :, b, :], start=True, stop=True)
                    mm.then_inc(done, 1)

                def turn_z(i, h):
                    pe.wait_ge(z_done, i * G + G)
                    transposes(pe, bank[6], [z[:, h, t, :] for t in range(G)], ident).then_inc(z_turned, 1)

                def make_k(i, h):
                    pe.wait_ge(ctx_in[h], loads(i, h))
                    reuse(pe, v_out, i * 2)
                    halves_of(bank[7], wk, ctx_t[:, h], k_made)

                def make_q(i, h):
                    pe.wait_ge(z_t_done, i + 1)
                    halves_of(bank[6], wq, z_t[:, :], q_made)

                def make_v(i, h):
                    pe.wait_ge(k_out, (i + 1) * F * J)
                    for tb in range(BG):
                        for j2 in range(2):
                            mm = pe.matmul(bank[7][half_rows(j2), tb * S:(tb + 1) * S],
                                           ctx_t[:, h, tb * S:(tb + 1) * S],
                                           wv[:, :].rearrange("p (a j d) -> p j a d", j=2, d=HD)[:, j2],
                                           start=True, stop=True)
                    mm.then_inc(v_made, 1)

                def scores(i, h, u):
                    t, f = u // F, u % F
                    if u == 0:
                        pe.wait_ge(q_out, (i + 1) * 4)
                        pe.wait_ge(k_out, (i + 1) * F * J)
                    reuse(pe, capped, i * U + u - 1)
                    pe.matmul(bank[u % 2][:, :], q_blocks[:, h, f, t, :],
                              k_heads[:, h, f, t].rearrange("p j k -> p (j k)"), start=True, stop=True)\
                        .then_inc(scored, 1)

                def turn(i, u):
                    pe.wait_ge(exped, i * U + u + 1)
                    reuse(pe, p_t_done, i * U + u - 1)
                    transposes(pe, bank[2 + u % 2], [probs[:, u, a * P:(a + 1) * P] for a in range(JP)], ident)\
                        .then_inc(p_turned, 1)

                def values(i, h, u):
                    t, f = u // F, u % F
                    pe.wait_ge(p_t_done, i * U + u + 1)
                    if u == 0:
                        pe.wait_ge(v_out, i * 2 + 2)
                        reuse(pe, o_done, i * 2 - 1)
                    if u == U // 2:
                        reuse(pe, proj_out, i)
                    for a in range(JP):
                        hp = f * JP + a
                        c = ((t % 2) * HP + hp) * W
                        for b in range(2):
                            mm = pe.matmul(bank[4 + t // 2][half_rows(b), c:c + W],
                                           probs_t[:, u % 2, a, half_rows(b)], v_blocks[:, h, t * 2 + b, hp, :],
                                           start=True, stop=True)
                    mm.then_inc(pv_done, 1)

                def front(i, h, *parts):
                    for part in parts or (make_k, turn_z, make_q, make_v):
                        part(i, h)

                def turn_o(i):
                    pe.wait_ge(o_done, i * 2 + 2)
                    transposes(pe, bank[5], [o[:, t, :] for t in range(G)], ident).then_inc(o_turned, 1)

                def project(i):
                    pe.wait_ge(o_t_done, i + 1)
                    for t in range(G):
                        mm = pe.matmul(bank[5][:, t * D:(t + 1) * D], o_t[:, t * P:(t + 1) * P], wo[:, :],
                                       start=True, stop=True)
                    mm.then_inc(projected, 1)

                def slot(i, h, s):
                    unit_ago(i, s, 0, lambda g, u: scores(g, h, u))
                    unit_ago(i, s, TURN, turn)
                    unit_ago(i, s, MULT, lambda g, u: values(g, h if s >= MULT else 1 - h, u))
                    if s == 4:
                        ago(i, 1, turn_o)
                    if s == 5:
                        ago(i, 1, project)
                over_slots(front, slot, {0: (make_k,), 2: (turn_z,), 4: (make_q,), 6: (make_v,)}, pe)

            @block.scalar
            def _(act):
                act.wait_ge(w_in, 9 * DMA)
                act.wait_ge(qk_consts, 3)
                act.wait_ge(blocks_set, 4)

                def z_out(i, h):
                    act.wait_ge(z_turned, i + 1)
                    act.activation(z_t[:, :], bank[6][:, :], ACT.Identity).then_inc(z_t_done, 1)

                def q_parts(i, h):
                    act.wait_ge(q_made, i + 1)
                    reuse(act, scored, (i - 1) * U)
                    for b in range(2):
                        for f in range(F):
                            r = half_rows(b)
                            act.activation(q_blocks[r, h, f, :, b * S:(b + 1) * S],
                                           bank[6][r, f * N // 2:(f + 1) * N // 2].rearrange("p (t s) -> p t s", t=G),
                                           ACT.Identity, bias=q_bias[r, f:f + 1], scale=scale).then_inc(q_out, 1)

                def k_parts(i, h, which):
                    if which.start == 0:
                        act.wait_ge(k_made, i + 1)
                        reuse(act, scored, (i - 1) * U)
                    for j, f in (divmod(n, F) for n in which):
                        act.activation(k_heads[:, h, f, :, j, :],
                                       bank[7][:, f * N // 2:(f + 1) * N // 2].rearrange("p (t s) -> p t s", t=G),
                                       ACT.Identity, bias=k_bias[:, f, j:j + 1], scale=of_head[:, j:j + 1])\
                            .then_inc(k_out, 1)
                k_at = [(lambda i, h, a=a, b=b: k_parts(i, h, range(a, b)))
                        for a, b in ((0, 2), (2, 5), (5, 8), (8, 11), (11, 14), (14, 16))]

                def exp(i, u):
                    act.wait_ge(shifted, i * U + u + 1)
                    act.activation(probs[:, u], probs[:, u], ACT.Exp).then_inc(exped, 1)

                def turned(i, u):
                    act.wait_ge(p_turned, i * U + u + 1)
                    reuse(act, pv_done, i * U + u - 1)
                    act.activation(probs_t[:, u % 2].rearrange("p a q -> p (a q)"), bank[2 + u % 2][:, :],
                                   ACT.Identity).then_inc(p_t_done, 1)

                def front(i, h, *parts):
                    for part in parts or (*k_at, z_out, q_parts):
                        part(i, h)

                def o_out(i):
                    act.wait_ge(o_turned, i + 1)
                    act.activation(o_t[:, :], bank[5][:, :], ACT.Identity).then_inc(o_t_done, 1)

                def slot(i, h, s):
                    unit_ago(i, s, 1, exp)
                    unit_ago(i, s, TURN, turned)
                    if s == 5:
                        ago(i, 1, o_out)
                over_slots(front, slot, {0: k_at[0:1], 1: k_at[1:2], 2: k_at[2:3], 3: (k_at[3], z_out), 4: k_at[4:5],
                                         5: k_at[5:6], 6: (q_parts,)}, act)

            @block.vector
            def _(v):
                v.wait_ge(w_in, 9 * DMA)
                v.wait_ge(blocks_set, 4)
                v.tensor_scalar(q_bias[:, :], bq[:, :], scale, None, ALU.mult).then_inc(qk_consts, 1)
                for f in range(F):
                    v.tensor_scalar(k_bias[:, f, :], of_head[:, :], bk[:, f:f + 1], None, ALU.mult).then_inc(qk_consts, 1)
                caps.vector_setup(v)
                tail.vector_setup(v)

                def stats(i, h):
                    ln.vector_stats(v, i, lambda t: tile_of(x_all, i, t))

                def apply(i, h):
                    tail.z_free(v, i - 1)
                    ln.vector_apply(v, i, lambda t: tile_of(x_all, i, t), z[:, h], z_done)

                def value_rows(i, h):
                    v.wait_ge(v_made, i + 1)
                    reuse(v, pv_done, (i - 1) * U)
                    for j2 in range(2):
                        r = half_rows(j2)
                        v.tensor_tensor(v_blocks[r, h, :, :, j2 * HD:(j2 + 1) * HD],
                                        bank[7][r, :].rearrange("p (t a d) -> p t a d", t=BG, a=HP),
                                        bv[r, :].rearrange("p (a d) -> p a d", a=HP).unsqueeze(1)
                                        .to_broadcast([S, BG, HP, HD]), ALU.add).then_inc(v_out, 1)

                def cap(i, h, u):
                    n = i * U + u + 1
                    row = probs[:, u].rearrange("p (j k) -> p j k", k=S)
                    v.wait_ge(scored, n)
                    reuse(v, p_turned, (i - 1) * U + u + 1)
                    caps.vector(v, i, h, u // F, row, bank[u % 2][:, :].rearrange("p (j k) -> p j k", k=S), capped)
                    v.wait_ge(capped, n)
                    v.tensor_reduce(top[:, u, :], row, AX.X, ALU.max).then_inc(topped, 1)

                def table(i, h):
                    caps.table(v, i, h)

                def front(i, h, *parts):
                    for part in parts or (stats, apply, value_rows, table):
                        part(i, h)

                def normalize(i, pair):
                    pv = bank[4 + pair][:, 0:2 * HP * W].rearrange("p (a w) -> p a w", w=W)
                    n = i * 2 + pair + 1
                    v.wait_ge(pv_done, i * U + (pair + 1) * U // 2)
                    v.reciprocal(rsum[:, pair], pv[:, :, 2 * HD:W]).then_inc(rsum_done, 1)
                    v.wait_ge(rsum_done, n)
                    v.tensor_tensor(o[:, 2 * pair:2 * pair + 2, :].rearrange("p t (a j d) -> p (t a) j d", a=HP, j=2),
                                    pv[:, :, 0:2 * HD].rearrange("p a (j d) -> p a j d", j=2),
                                    rsum[:, pair].unsqueeze(3).to_broadcast([P, 2 * HP, 2, HD]), ALU.mult)\
                        .then_inc(o_done, 1)

                def add_output(i):
                    v.wait_ge(projected, i + 1)
                    tail.vector_output(v, i, out, bank[5][:, :].rearrange("p (t d) -> p t d", t=G), proj_out)

                def slot(i, h, s):
                    unit_ago(i, s, 0, lambda g, u: cap(g, h, u))
                    if s == 0:
                        ago(i, 1, lambda g: normalize(g, 0))
                    if s == 4:
                        ago(i, 1, lambda g: normalize(g, 1))
                    if s == 6:
                        ago(i, 1, add_output)
                    if s == 7:
                        ago(i, 1, lambda g: tail.vector(v, g, out, tanh_g))
                over_slots(front, slot, {0: (stats,), 1: (apply,), 5: (table,), 7: (value_rows,)}, v)


class QueryKeyCaps:

    def __init__(self, ph, chip):
        self.chip = chip
        self.mask, self.maskf = ph.sb("mask", [P, S], I32), ph.sb("maskf", [P, S])
        self.cap = ph.sb("cap", [P, S])
        self.mask_in, self.cap_steps = ph.sem("mask_in"), ph.sem("cap_steps")

    def load(self, sp):
        sp.dma_start(self.mask[:, :], self.chip.dram["l2_mask"]).then_inc(self.mask_in, DMA)

    def vector_setup(self, v):
        v.wait_ge(self.mask_in, DMA)
        v.tensor_copy(self.maskf[:, :], self.mask[:, :]).then_inc(self.cap_steps, 1)
        v.wait_ge(self.cap_steps, 1)
        v.tensor_scalar(self.maskf[:, :], self.maskf[:, :], 0.0, None, ALU.is_equal).then_inc(self.cap_steps, 1)
        v.wait_ge(self.cap_steps, 2)
        v.tensor_scalar(self.cap[:, :], self.maskf[:, :], -BIG, BIG, ALU.mult, ALU.add).then_inc(self.cap_steps, 1)
        v.wait_ge(self.cap_steps, 3)
        v.scalar_tensor_tensor(out=self.cap[:, :], in0=self.maskf[:, :], scalar=-1e9, in1=self.cap[:, :],
                               op0=ALU.mult, op1=ALU.add).then_inc(self.cap_steps, 1)
        v.wait_ge(self.cap_steps, 4)

    def table(self, v, i, h):
        pass

    def vector(self, v, i, h, t, out, scores, capped):
        v.tensor_tensor(out, scores, self.cap[:, :].unsqueeze(1).to_broadcast([P, 8, S]), ALU.min).then_inc(capped, 1)


class PaddingCaps:

    def __init__(self, ph, chip):
        self.chip = chip
        self.mask = ph.sb("mask", [P, TILES * S], U8)
        self.maskf, self.cap = ph.sb("maskf", [P, G * S]), ph.sb("cap", [P, 2, G * S])
        self.mask_in, self.cap_steps = ph.sem("mask_in"), ph.sem("cap_steps")

    def load(self, sp):
        sp.dma_start(self.mask[:, :], self.chip.dram["l3_mask"]).then_inc(self.mask_in, DMA)

    def vector_setup(self, v):
        v.wait_ge(self.mask_in, DMA)

    def table(self, v, i, h):
        v.tensor_scalar(self.maskf[:, :], self.mask[:, bass.ds(i * G * S, G * S)], 1.0, None, ALU.min)\
            .then_inc(self.cap_steps, 1)
        v.wait_ge(self.cap_steps, i * 4 + 1)
        v.tensor_scalar(self.cap[:, h], self.maskf[:, :], -BIG, BIG, ALU.mult, ALU.add).then_inc(self.cap_steps, 1)
        for k in range(2):
            v.wait_ge(self.cap_steps, i * 4 + 2 + k)
            v.scalar_tensor_tensor(out=self.cap[:, h], in0=self.maskf[:, :], scalar=-BIG, in1=self.cap[:, h],
                                   op0=ALU.mult, op1=ALU.add).then_inc(self.cap_steps, 1)
        v.wait_ge(self.cap_steps, i * 4 + 4)

    def vector(self, v, i, h, t, out, scores, capped):
        v.tensor_tensor(out, scores, self.cap[:, h, t * S:(t + 1) * S].unsqueeze(1).to_broadcast([P, 8, S]),
                        ALU.min).then_inc(capped, 1)


class AddToX:

    def __init__(self, ph, chip, bias):
        self.chip, self.bias, self.x_done = chip, bias, ph.sem("x")

    def load(self, sp):
        pass

    def vector_setup(self, v):
        pass

    def z_free(self, v, uses):
        pass

    def pool_residual(self, pool, i, h, z, proj_out):
        pass

    def pool_rstd(self, pool, i):
        pass

    def pool(self, pool, i):
        pass

    def vector_output(self, v, i, out, projected, proj_out):
        v.tensor_tensor(out[:, :, :], projected, self.bias[:, :].unsqueeze(1).to_broadcast([P, G, D]), ALU.add)\
            .then_inc(proj_out, 1)
        v.wait_ge(proj_out, i + 1)

    def vector(self, v, i, out, tanh_g):
        x = self.chip.x_all
        v.scalar_tensor_tensor(out=group_of(x, i), in0=out[:, :, :], scalar=tanh_g, in1=group_of(x, i),
                               op0=ALU.mult, op1=ALU.add).then_inc(self.x_done, 1)


def l2_ffn(chip, ahead):
    nc, dram, x_all, bank, ident = chip.nc, chip.dram, chip.x_all, chip.bank, chip.ident
    E, C = L2_E, L2_H // P
    with Phase(chip, "l2ffn") as ph:
        ln, ln2 = LayerNorm(ph, "ln"), LayerNorm(ph, "ln2")
        w1, w2 = ahead.tensors
        wr, gamma, beta = ph.sb("wr", [P, E]), ph.sb("gamma", [P, D]), ph.sb("beta", [P, D])
        w1_high, w1_low = ph.sb("w1_high", [P, E, L2_H], F32R), ph.sb("w1_low", [P, E, L2_H], F32R)
        n, z, z_t = ph.sb("n", [P, 2, G, D]), ph.sb("z", [P, G, D]), ph.sb("z_t", [P, N])
        z_high, z_low = ph.sb("z_high", [P, 2, N], F32R), ph.sb("z_low", [P, 2, N], F32R)
        best, rsum = ph.sb("best", [P, G]), ph.sb("rsum", [P, G])
        prob, best8 = ph.sb("prob", [P, G, E]), ph.sb("best8", [P, G, 8])
        sel, tie, tie_no, n_above = (ph.sb("sel", [P, G, E]), ph.sb("tie", [P, G, E]), ph.sb("tie_no", [P, G, E]),
                                     ph.sb("n_above", [P, G]))
        ones, w = ph.sb("ones", [P, E]), ph.sb("w", [P, 2, G, E])
        hid, acc = ph.sb("hid", [P, 2, C, N]), ph.sb("acc", [P, G, D])
        w_in, ones_set = ph.sem("w_in"), ph.sem("ones_set")
        n_done, z_norm, z_done = ph.sem("n"), ph.sem("z_norm"), ph.sem("z")
        w1_high_done, w1_low_done = ph.sem("w1_high"), ph.sem("w1_low")
        z_turned, z_t_done, gated = ph.sem("z_turned"), ph.sem("z_t"), ph.sem("gated")
        z_high_done, z_low_done = ph.sem("z_high"), ph.sem("z_low")
        route, prob_done = ph.sem("route_steps"), ph.sem("prob")
        made_h, hid_done, made_y, used, x_done = (ph.sem("made_h"), ph.sem("hid"), ph.sem("made_y"), ph.sem("used"),
                                                  ph.sem("x"))
        tanh_g = chip.tanh_g[:, 6:7]
        PARTS = (2, 5 + 2 * G, 5)
        STEPS = sum(PARTS)
        row = lambda ap: ap[:, :].unsqueeze(1).to_broadcast([P, G, D])

        with nc.Block() as block:
            @block.sync
            def _(sp):
                for dst, name in ((wr[:, :], "l2_wr"), (gamma[:, :], "l2_gamma"), (beta[:, :], "l2_beta")):
                    sp.dma_start(dst, dram[name]).then_inc(w_in, DMA)

            @block.gpsimd
            def _(pool):
                pool.memset(ones[:, :], 1.0).then_inc(ones_set, 1)

                ahead.wait(pool)

                def step(i, h):
                    ln.pool_rstd(pool, i)
                    ln2.pool_rstd(pool, i)
                    if isinstance(i, int) and i == 0:
                        for e in range(E):
                            pool.wait_ge(w1_high_done, e + 1)
                            pool.tensor_tensor(w1_low[:, e], w1[:, e], w1_high[:, e].bitcast(F32), ALU.subtract)\
                                .then_inc(w1_low_done, 1)
                each_group(step, pool)

            @block.tensor
            def _(pe):
                pe.wait_ge(w_in, 3 * DMA)
                ahead.wait(pe)

                def turn(i, h):
                    pe.wait_ge(z_done, i + 1)
                    reuse(pe, z_low_done, i)
                    transposes(pe, bank[0], [z[:, t, :] for t in range(G)], ident).then_inc(z_turned, 1)

                def router(i, h):
                    pe.wait_ge(z_t_done, i + 1)
                    reuse(pe, route, (i - 1) * STEPS + 2)
                    for t in range(G):
                        for b in range(2):
                            r = slice(b * S, (b + 1) * S)
                            mm = pe.matmul(bank[7][r, t * E:(t + 1) * E], z_t[:, t * P + b * S:t * P + (b + 1) * S],
                                           wr[:, :], start=True, stop=True)
                    mm.then_inc(gated, 1)

                def front(i, h, *parts):
                    for part in parts or (turn, router):
                        part(i, h)

                def hidden(i, h, e):
                    if e == 0:
                        pe.wait_ge(z_low_done, i + 1)
                    pe.wait_ge(w1_low_done, e + 1)
                    for c in range(C):
                        use = (i * E + e) * C + c
                        col = slice(c * P, (c + 1) * P)
                        reuse(pe, hid_done, use - 3)
                        split_product(pe, bank[1 + c][:, :], (w1_high[:, e, col], w1_low[:, e, col]),
                                      (z_high[:, h], z_low[:, h])).then_inc(made_h, 1)

                def outputs(i, h, e):
                    pe.wait_ge(hid_done, (i * E + e + 1) * C)
                    reuse(pe, used, i * E + e - 1)
                    for t in range(G):
                        for c in range(C):
                            mm = pe.matmul(bank[5 + e % 2][:, t * D:(t + 1) * D],
                                           hid[:, e % 2, c, t * P:(t + 1) * P], w2[:, e, c, :],
                                           start=(c == 0), stop=(c == C - 1))
                    mm.then_inc(made_y, 1)

                def main(i, h, nxt):
                    hidden(i, h, 0)
                    for e in range(E):
                        if e + 1 < E:
                            hidden(i, h, e + 1)
                        outputs(i, h, e)
                        for at, part in ((3, turn), (4, router)):
                            if e == at:
                                nxt(part)
                over_groups(front, main, pe)

            @block.scalar
            def _(act):
                ahead.wait(act)
                for e in range(E):
                    act.activation(w1_high[:, e], w1[:, e], ACT.Identity).then_inc(w1_high_done, 1)

                def z_out(i, h):
                    act.wait_ge(z_turned, i + 1)
                    reuse(act, gated, i)
                    act.activation(z_t[:, :], bank[0][:, :], ACT.Identity).then_inc(z_t_done, 1)
                    act.activation(z_high[:, h], bank[0][:, :], ACT.Identity).then_inc(z_high_done, 1)

                def exps(i, h):
                    act.wait_ge(route, i * STEPS + 2)
                    act.activation(prob[:, :, :], prob[:, :, :], ACT.Exp, scale=1.0 / L2_TEMP).then_inc(prob_done, 1)

                def front(i, h, *parts):
                    for part in parts or (z_out, exps):
                        part(i, h)

                def main(i, h, nxt):
                    for e in range(E):
                        for c in range(C):
                            act.wait_ge(made_h, (i * E + e) * C + c + 1)
                            if c == 0:
                                reuse(act, made_y, i * E + e - 1)
                            act.activation(hid[:, e % 2, c], bank[1 + c][:, :], ACT.Silu).then_inc(hid_done, 1)
                        for at, part in ((4, z_out), (5, exps)):
                            if e == at:
                                nxt(part)
                over_groups(front, main, act)

            @block.vector
            def _(v):
                v.wait_ge(w_in, 3 * DMA)
                v.wait_ge(ones_set, 1)
                at = steps = 0

                def step(instruction):
                    nonlocal steps
                    steps += 1
                    instruction.then_inc(route, 1)

                def settled():
                    v.wait_ge(route, at + steps)

                def norm(i, h):
                    ln.vector_stats(v, i, lambda t: tile_of(x_all, i, t))
                    ln.vector_apply(v, i, lambda t: tile_of(x_all, i, t), n[:, h], n_done)
                    wait_apart(v, n_done, i * G + G, chip.passed["v"])
                    ln2.vector_stats(v, i, lambda t: n[:, h, t, :])

                def norm_again(i, h):
                    ln2.vector_apply(v, i, lambda t: n[:, h, t, :], z, z_norm)
                    v.wait_ge(z_norm, i * (G + 1) + G)
                    v.tensor_tensor(z[:, :, :], z[:, :, :], row(gamma), ALU.mult).then_inc(z_norm, 1)
                    v.wait_ge(z_norm, (i + 1) * (G + 1))
                    v.tensor_tensor(z[:, :, :], z[:, :, :], row(beta), ALU.add).then_inc(z_done, 1)

                def z_rest(i, h):
                    v.wait_ge(z_high_done, i + 1)
                    reuse(v, made_h, (i - 1) * E * C)
                    v.tensor_tensor(z_low[:, h], bank[0][:, :], z_high[:, h].bitcast(F32), ALU.subtract)\
                        .then_inc(z_low_done, 1)

                def shift(i, h):
                    nonlocal at, steps
                    at, steps = i * STEPS, 0
                    logits = bank[7][:, 0:G * E].rearrange("p (t e) -> p t e", t=G)
                    v.wait_ge(gated, i + 1)
                    step(v.tensor_reduce(best[:, :], logits, AX.X, ALU.max))
                    settled()
                    step(v.tensor_tensor(prob[:, :, :], logits, best[:, :].unsqueeze(2).to_broadcast([P, G, E]),
                                         ALU.subtract))

                def choose(i, h):
                    nonlocal at, steps
                    at, steps = i * STEPS, PARTS[0]
                    wait_apart(v, prob_done, i + 1, chip.passed["v"])
                    for t in range(G):
                        step(v.max(best8[:, t, :], prob[:, t, :]))
                    settled()
                    second = best8[:, :, 1].unsqueeze(2).to_broadcast([P, G, E])
                    step(v.tensor_tensor(sel[:, :, :], prob[:, :, :], second, ALU.is_gt))
                    step(v.tensor_tensor(tie[:, :, :], prob[:, :, :], second, ALU.is_equal))
                    settled()
                    step(v.tensor_reduce(n_above[:, :], sel[:, :, :], AX.X, ALU.add))
                    step(v.tensor_reduce(rsum[:, :], prob[:, :, :], AX.X, ALU.add))
                    for t in range(G):
                        step(v.tensor_tensor_scan(tie_no[:, t, :], ones[:, :], tie[:, t, :], 0.0, ALU.mult, ALU.add))
                    settled()
                    step(v.reciprocal(rsum[:, :], rsum[:, :]))

                def weigh(i, h):
                    nonlocal at, steps
                    at, steps = i * STEPS, PARTS[0] + PARTS[1]
                    step(v.tensor_tensor(tie_no[:, :, :], tie_no[:, :, :], n_above[:, :].unsqueeze(2)
                                         .to_broadcast([P, G, E]), ALU.add))
                    settled()
                    step(v.scalar_tensor_tensor(out=tie[:, :, :], in0=tie_no[:, :, :], scalar=2.0,
                                                in1=tie[:, :, :], op0=ALU.is_le, op1=ALU.mult))
                    settled()
                    step(v.tensor_tensor(sel[:, :, :], sel[:, :, :], tie[:, :, :], ALU.add))
                    settled()
                    step(v.tensor_tensor(sel[:, :, :], sel[:, :, :], prob[:, :, :], ALU.mult))
                    settled()
                    step(v.tensor_tensor(w[:, h], sel[:, :, :], rsum[:, :].unsqueeze(2).to_broadcast([P, G, E]),
                                         ALU.mult))
                    assert steps == STEPS

                def front(i, h, *parts):
                    for part in parts or (norm, norm_again, z_rest, shift, choose, weigh):
                        part(i, h)

                def main(i, h, nxt):
                    for e in range(E):
                        v.wait_ge(made_y, i * E + e + 1)
                        if e == 0:
                            v.wait_ge(route, (i + 1) * STEPS)
                            reuse(v, x_done, i)
                        else:
                            v.wait_ge(used, i * E + e)
                        for t in range(G):
                            mm = v.scalar_tensor_tensor(
                                out=acc[:, t, :], in0=bank[5 + e % 2][:, t * D:(t + 1) * D], scalar=w[:, h, t, e:e + 1],
                                in1=acc[:, t, :] if e else n[:, h, t, :], op0=ALU.mult, op1=ALU.add)
                        mm.then_inc(used, 1)
                        for at_e, part in ((0, norm), (1, norm_again), (4, z_rest), (4, shift), (5, choose), (6, weigh)):
                            if e == at_e:
                                nxt(part)
                    v.wait_ge(used, (i + 1) * E)
                    v.scalar_tensor_tensor(out=group_of(x_all, i), in0=acc[:, :, :], scalar=tanh_g,
                                           in1=group_of(x_all, i), op0=ALU.mult, op1=ALU.add).then_inc(x_done, 1)
                over_groups(front, main, v)


class NormToY:

    def __init__(self, ph, chip, out_bias, y_all):
        self.chip, self.out_bias, self.y_all = chip, out_bias, y_all
        self.ln = LayerNorm(ph, "ln1")
        self.gain, self.bias = ph.sb("ln1_g", [P, D]), ph.sb("ln1_b", [P, D])
        self.residual, self.normed = ph.sb("residual", [P, G, D]), ph.sb("normed", [P, G, D])
        self.gain_in, self.res_done, self.normed_done = ph.sem("gain_in"), ph.sem("res"), ph.sem("normed")
        self.gained, self.y_done = ph.sem("gained"), ph.sem("y")

    def load(self, sp):
        sp.dma_start(self.gain[:, :], self.chip.dram["l3_ln1_g"]).then_inc(self.gain_in, DMA)
        sp.dma_start(self.bias[:, :], self.chip.dram["l3_ln1_b"]).then_inc(self.gain_in, DMA)

    def vector_setup(self, v):
        v.wait_ge(self.gain_in, 2 * DMA)

    def z_free(self, v, uses):
        reuse(v, self.res_done, uses)

    def pool_residual(self, pool, i, h, z, proj_out):
        reuse(pool, proj_out, i)
        pool.tensor_tensor(self.residual[:, :, :], z, self.row(self.out_bias), ALU.add).then_inc(self.res_done, 1)

    def row(self, ap):
        return ap[:, :].unsqueeze(1).to_broadcast([P, G, D])

    def pool_rstd(self, pool, i):
        self.ln.pool_rstd(pool, i)

    def pool(self, pool, i):
        pool.wait_ge(self.normed_done, i * G + G)
        pool.tensor_tensor(self.normed[:, :, :], self.normed[:, :, :], self.row(self.gain), ALU.mult)\
            .then_inc(self.gained, 1)
        pool.wait_ge(self.gained, i + 1)
        pool.tensor_tensor(group_of(self.y_all, i), self.normed[:, :, :], self.row(self.bias), ALU.add)\
            .then_inc(self.y_done, 1)

    def vector_output(self, v, i, out, projected, proj_out):
        v.wait_ge(self.res_done, i + 1)
        v.tensor_tensor(out[:, :, :], projected, self.residual[:, :, :], ALU.add).then_inc(proj_out, 1)
        wait_apart(v, proj_out, i + 1, self.chip.passed["v"])
        self.ln.vector_stats(v, i, lambda t: out[:, t, :])

    def vector(self, v, i, out, tanh_g):
        reuse(v, self.y_done, i)
        self.ln.vector_apply(v, i, lambda t: out[:, t, :], self.normed, self.normed_done)


def l3_mlp(chip, y_all):
    nc, dram, x_all, bank, ident = chip.nc, chip.dram, chip.x_all, chip.bank, chip.ident
    C = FFN // P
    with Phase(chip, "l3mlp") as ph:
        ln = LayerNorm(ph, "ln")
        w1, w2, b1 = ph.sb("w1", [P, FFN]), ph.sb("w2", [P, C, D]), ph.sb("b1", [P, C])
        w1_high, w1_low = ph.sb("w1_high", [P, FFN], F32R), ph.sb("w1_low", [P, FFN], F32R)
        b2, ln_g, ln_b = ph.sb("b2", [P, D]), ph.sb("ln_g", [P, D]), ph.sb("ln_b", [P, D])
        y, hid = ph.sb("y", [P, 2, G, D]), ph.sb("hid", [P, 2, C, N])
        y_high, y_low = ph.sb("y_high", [P, 2, N], F32R), ph.sb("y_low", [P, 2, N], F32R)
        y_b2, res, normed = ph.sb("y_b2", [P, 2, G, D]), ph.sb("res", [P, G, D]), ph.sb("normed", [P, 2, G, D])
        w_in, affine, w_high_done, w_low_done = ph.sem("w_in"), ph.sem("affine"), ph.sem("w_high"), ph.sem("w_low")
        y_done, y_turned, y_high_done, y_low_done = ph.sem("y"), ph.sem("y_turned"), ph.sem("y_high"), ph.sem("y_low")
        made_h, hid_done, made_o, res_done = ph.sem("made_h"), ph.sem("hid"), ph.sem("made_o"), ph.sem("res")
        y_b2_done, normed_done = ph.sem("y_b2"), ph.sem("normed")
        gained, moved, x_done = ph.sem("gained"), ph.sem("moved"), ph.sem("x")
        tanh_g = chip.tanh_g[:, 3:4]
        row = lambda ap: ap[:, :].unsqueeze(1).to_broadcast([P, G, D])

        with nc.Block() as block:
            @block.sync
            def _(sp):
                for dst, name in ((w1[:, :], "l3_w1"), (w2[:, :, :], "l3_w2"), (b1[:, :], "l3_b1"),
                                  (b2[:, :], "l3_b2"), (ln_g[:, :], "l3_ln2_g"), (ln_b[:, :], "l3_ln2_b")):
                    sp.dma_start(dst, dram[name]).then_inc(w_in, DMA)

            @block.gpsimd
            def _(pool):
                pool.wait_ge(w_in, 6 * DMA)
                pool.wait_ge(affine, 2)

                def add_b2(i, h):
                    reuse(pool, res_done, i - 1)
                    pool.tensor_tensor(y_b2[:, h], group_of(y_all, i), row(b2), ALU.add).then_inc(y_b2_done, 1)

                def affine_part(i, h):
                    pool.wait_ge(normed_done, i * G + G)
                    pool.tensor_tensor(normed[:, h], normed[:, h], row(ln_g), ALU.mult).then_inc(gained, 1)
                    pool.wait_ge(gained, i + 1)
                    pool.tensor_tensor(normed[:, h], normed[:, h], row(ln_b), ALU.add).then_inc(moved, 1)

                def main(i, h, nxt):
                    ago(i, 1, lambda g: add_b2(g, 1 - h))
                    ago(i, 2, lambda g: ln.pool_rstd(pool, g))
                    ago(i, 2, lambda g: affine_part(g, h))
                over_lagging(lambda i, h: None, main, pool, 3)

            @block.tensor
            def _(pe):
                pe.wait_ge(w_in, 6 * DMA)
                pe.wait_ge(w_low_done, 1)

                def turn_y(i, h):
                    pe.wait_ge(y_done, i + 1)
                    reuse(pe, y_low_done, i)
                    transposes(pe, bank[0], [y[:, h, t, :] for t in range(G)], ident).then_inc(y_turned, 1)

                def hidden(i, h):
                    pe.wait_ge(y_low_done, i + 1)
                    for c in range(C):
                        col = slice(c * P, (c + 1) * P)
                        reuse(pe, hid_done, (i - 1) * C + c + 1)
                        split_product(pe, bank[2 + c][:, :], (w1_high[:, col], w1_low[:, col]),
                                      (y_high[:, h], y_low[:, h])).then_inc(made_h, 1)

                def outputs(i, h):
                    pe.wait_ge(hid_done, i * C + C)
                    reuse(pe, res_done, i - 1)
                    for t in range(G):
                        for c in range(C):
                            mm = pe.matmul(bank[6 + h][:, t * D:(t + 1) * D], hid[:, h, c, t * P:(t + 1) * P],
                                           w2[:, c, :], start=(c == 0), stop=(c == C - 1))
                    mm.then_inc(made_o, 1)

                def main(i, h, nxt):
                    ago(i, 0, lambda g: hidden(g, h))
                    ago(i, -1, lambda g: turn_y(g, 1 - h))
                    ago(i, 1, lambda g: outputs(g, 1 - h))
                over_lagging(turn_y, main, pe, 3)

            @block.scalar
            def _(act):
                act.wait_ge(w_in, 6 * DMA)
                act.activation(w1_high[:, :], w1[:, :], ACT.Identity).then_inc(w_high_done, 1)

                def fetch(i, h):
                    reuse(act, y_turned, i - 1)
                    act.activation(y[:, h], group_of(y_all, i), ACT.Identity).then_inc(y_done, 1)

                def y_out(i, h):
                    act.wait_ge(y_turned, i + 1)
                    reuse(act, made_h, (i - 1) * C)
                    act.activation(y_high[:, h], bank[0][:, :], ACT.Identity).then_inc(y_high_done, 1)

                def gelus(i, h):
                    reuse(act, made_o, i - 1)
                    for c in range(C):
                        act.wait_ge(made_h, i * C + c + 1)
                        act.activation(hid[:, h, c], bank[2 + c][:, :], ACT.Gelu, bias=b1[:, c:c + 1])\
                            .then_inc(hid_done, 1)

                def front(i, h):
                    fetch(0, 0)
                    fetch(1, 1)
                    y_out(i, h)

                def main(i, h, nxt):
                    ago(i, 0, lambda g: gelus(g, h))
                    ago(i, -2, lambda g: fetch(g, h))
                    ago(i, -1, lambda g: y_out(g, 1 - h))
                over_lagging(front, main, act, 3)

            @block.vector
            def _(v):
                v.wait_ge(w_in, 6 * DMA)
                v.tensor_scalar(ln_g[:, :], ln_g[:, :], tanh_g, None, ALU.mult).then_inc(affine, 1)
                v.tensor_scalar(ln_b[:, :], ln_b[:, :], tanh_g, None, ALU.mult).then_inc(affine, 1)
                v.wait_ge(w_high_done, 1)
                v.tensor_tensor(w1_low[:, :], w1[:, :], w1_high[:, :].bitcast(F32), ALU.subtract).then_inc(w_low_done, 1)

                def y_rest(i, h):
                    v.wait_ge(y_high_done, i + 1)
                    reuse(v, made_h, (i - 1) * C)
                    v.tensor_tensor(y_low[:, h], bank[0][:, :], y_high[:, h].bitcast(F32), ALU.subtract)\
                        .then_inc(y_low_done, 1)

                def residual(i, h):
                    v.wait_ge(made_o, i + 1)
                    v.wait_ge(y_b2_done, i + 1)
                    reuse(v, normed_done, i * G)
                    v.tensor_tensor(res[:, :, :], bank[6 + h][:, :].rearrange("p (t d) -> p t d", t=G), y_b2[:, h],
                                    ALU.add).then_inc(res_done, 1)
                    wait_apart(v, res_done, i + 1, chip.passed["v"])
                    ln.vector_stats(v, i, lambda t: res[:, t, :])

                def norm(i, h):
                    reuse(v, x_done, i - 1)
                    ln.vector_apply(v, i, lambda t: res[:, t, :], normed[:, h], normed_done)

                def add_to_x(i, h):
                    v.wait_ge(moved, i + 1)
                    v.tensor_tensor(group_of(x_all, i), normed[:, h], group_of(x_all, i), ALU.add).then_inc(x_done, 1)

                def main(i, h, nxt):
                    ago(i, 2, lambda g: residual(g, h))
                    ago(i, -1, lambda g: y_rest(g, 1 - h))
                    ago(i, 2, lambda g: norm(g, h))
                    ago(i, 3, lambda g: add_to_x(g, 1 - h))
                over_lagging(y_rest, main, v, 3)


def l3_tree(chip):
    nc, dram, x_all, bank, ident = chip.nc, chip.dram, chip.x_all, chip.bank, chip.ident
    NODES, C = LEAVES - 1, LEAVES // P
    with Phase(chip, "l3tree") as ph:
        ln = LayerNorm(ph, "ln")
        wq, rt, vt, wo = ph.sb("wq", [P, D]), ph.sb("rt", [P, NODES]), ph.sb("vt", [P, LEAVES]), ph.sb("wo", [P, D])
        wr, vo, bo = ph.sb("wr", [P, LEAVES]), ph.sb("vo", [P, C, D]), ph.sb("bo", [P, D])
        z, z_t = ph.sb("z", [P, 2, G, D]), ph.sb("z_t", [P, 2, N])
        gate, lp = ph.sb("gate", [P, 2, G, LEAVES]), ph.sb("lp", [P, 2, 2, G, LEAVES])
        lp_t, out, x_out = ph.sb("lp_t", [P, C, N]), ph.sb("out", [P, G, D]), ph.sb("x_out", [P, 2, G, D])
        w_in, merged, merged_out = ph.sem("w_in"), ph.sem("merged"), ph.sem("merged_out")
        z_done, z_turned, z_t_done = ph.sem("z"), ph.sem("z_turned"), ph.sem("z_t")
        gated, gate_done, levels = ph.sem("gated"), ph.sem("gate"), ph.sem("levels")
        lp_turned, lp_t_done, summed, biased, x_done = (ph.sem("lp_turned"), ph.sem("lp_t"), ph.sem("summed"),
                                                        ph.sem("biased"), ph.sem("x"))
        stored = [ph.sem("stored0"), ph.sem("stored1")]
        out_dram = dram["out"].rearrange("(n p) d -> p n d", p=P)
        tanh_g = chip.tanh_g[:, 7:8]
        DEPTH = LEAVES.bit_length() - 1
        STEPS = 2 * DEPTH

        with nc.Block() as block:
            @block.sync
            def _(sp):
                for dst, name in ((wq, "l3_tq"), (rt, "l3_rt"), (vt, "l3_vt"), (wo, "l3_two"), (bo, "l3_tbo")):
                    sp.dma_start(dst[:, :], dram[name]).then_inc(w_in, DMA)

                def step(i, h):
                    sp.wait_ge(x_done, i + 1)
                    sp.dma_start(group_of(out_dram, i), x_out[:, h]).then_inc(stored[h], DMA)
                each_group(step, sp)
                for h in range(2):
                    sp.wait_ge(stored[h], loads(GROUPS - 2 + h, h))

            @block.gpsimd
            def _(pool):
                def front(i, h):
                    ln.pool_rstd(pool, 0)
                    ln.pool_rstd(pool, 1)
                over_lagging(front, lambda i, h, nxt: ago(i, -2, lambda g: ln.pool_rstd(pool, g)), pool, 1)

            @block.tensor
            def _(pe):
                pe.wait_ge(w_in, 5 * DMA)
                pe.matmul(bank[0][:, 0:NODES], wq[:, :], rt[:, :], start=True, stop=True).then_inc(merged, 1)
                for c in range(C):
                    mm = pe.matmul(bank[1][:, c * D:(c + 1) * D], vt[:, c * P:(c + 1) * P], wo[:, :],
                                   start=True, stop=True)
                mm.then_inc(merged, 1)
                pe.wait_ge(merged_out, 2)

                def turn_z(i, h):
                    pe.wait_ge(z_done, i * G + G)
                    reuse(pe, z_t_done, i)
                    transposes(pe, bank[0], [z[:, h, t, :] for t in range(G)], ident).then_inc(z_turned, 1)

                def node_scores(i, h):
                    pe.wait_ge(z_t_done, i + 1)
                    reuse(pe, gate_done, i * 2)
                    for t in range(G):
                        c = (t % 2) * LEAVES
                        mm = pe.matmul(bank[1 + t // 2][:, c:c + NODES], z_t[:, h, t * P:(t + 1) * P],
                                       wr[:, 0:NODES], start=True, stop=True)
                        if t % 2:
                            mm.then_inc(gated, 1)

                def turn_leaves(i, h):
                    pe.wait_ge(levels, (i + 1) * STEPS)
                    reuse(pe, lp_t_done, i * C)
                    for c in range(C):
                        transposes(pe, bank[3 + c], [lp[:, h, 1, t, c * P:(c + 1) * P] for t in range(G)], ident)\
                            .then_inc(lp_turned, 1)

                def outputs(i):
                    pe.wait_ge(lp_t_done, i * C + C)
                    reuse(pe, biased, i)
                    for t in range(G):
                        for c in range(C):
                            mm = pe.matmul(bank[5][:, t * D:(t + 1) * D], lp_t[:, c, t * P:(t + 1) * P], vo[:, c, :],
                                           start=(c == 0), stop=(c == C - 1))
                    mm.then_inc(summed, 1)

                def front(i, h):
                    turn_z(i, h)
                    node_scores(i, h)

                def main(i, h, nxt):
                    ago(i, 1, lambda g: turn_leaves(g, 1 - h))
                    ago(i, -1, lambda g: turn_z(g, 1 - h))
                    ago(i, 1, outputs)
                    ago(i, -1, lambda g: node_scores(g, 1 - h))
                over_lagging(front, main, pe, 1)

            @block.scalar
            def _(act):
                def z_out(i, h):
                    act.wait_ge(z_turned, i + 1)
                    reuse(act, gated, (i - 1) * 2)
                    act.activation(z_t[:, h], bank[0][:, :], ACT.Identity).then_inc(z_t_done, 1)

                def gates(i, h):
                    reuse(act, levels, (i - 1) * STEPS)
                    for b in range(2):
                        act.wait_ge(gated, i * 2 + b + 1)
                        act.activation(gate[:, h, 2 * b:2 * b + 2, 0:NODES],
                                       bank[1 + b][:, :].rearrange("p (t m) -> p t m", t=2)[:, :, 0:NODES],
                                       ACT.Sigmoid).then_inc(gate_done, 1)

                def leaves_out(i):
                    reuse(act, summed, i)
                    for c in range(C):
                        act.wait_ge(lp_turned, i * C + c + 1)
                        act.activation(lp_t[:, c], bank[3 + c][:, :], ACT.Identity).then_inc(lp_t_done, 1)

                def front(i, h):
                    z_out(i, h)
                    gates(i, h)

                def main(i, h, nxt):
                    ago(i, 1, leaves_out)
                    ago(i, -1, lambda g: z_out(g, 1 - h))
                    ago(i, -1, lambda g: gates(g, 1 - h))
                over_lagging(front, main, act, 1)

            @block.vector
            def _(v):
                v.wait_ge(merged, 2)
                v.tensor_copy(wr[:, 0:NODES], bank[0][:, 0:NODES]).then_inc(merged_out, 1)
                v.tensor_copy(vo[:, :, :].rearrange("p c d -> p (c d)"), bank[1][:, 0:C * D]).then_inc(merged_out, 1)

                def stats(i):
                    ln.vector_stats(v, i, lambda t: tile_of(x_all, i, t))

                def apply(i, h):
                    ln.vector_apply(v, i, lambda t: tile_of(x_all, i, t), z[:, h], z_done)

                def front(i, h):
                    for g in range(2):
                        stats(g)
                        apply(g, g)

                def tree(i, h, steps):
                    for level in steps:
                        n = 1 << level
                        src, dst = lp[:, h, (level + DEPTH + 1) % 2], lp[:, h, (level + DEPTH) % 2]
                        kids = dst[:, :, 0:2 * n].rearrange("p t (a k) -> p t a k", k=2)
                        g = gate[:, h, :, n - 1:2 * n - 1]
                        if level == 0:
                            v.tensor_scalar(kids[:, :, :, 1], g, 1.0, None, ALU.mult).then_inc(levels, 1)
                            v.tensor_scalar(kids[:, :, :, 0], g, -1.0, 1.0, ALU.mult, ALU.add).then_inc(levels, 1)
                            continue
                        v.wait_ge(levels, i * STEPS + 2 * level)
                        v.tensor_tensor(kids[:, :, :, 1], src[:, :, 0:n], g, ALU.mult).then_inc(levels, 1)
                        v.wait_ge(levels, i * STEPS + 2 * level + 1)
                        v.tensor_tensor(kids[:, :, :, 0], src[:, :, 0:n], kids[:, :, :, 1], ALU.subtract)\
                            .then_inc(levels, 1)

                def output(i, h):
                    v.wait_ge(summed, i + 1)
                    reuse(v, x_done, i)
                    v.tensor_tensor(out[:, :, :], bank[5][:, :].rearrange("p (t d) -> p t d", t=G),
                                    bo[:, :].unsqueeze(1).to_broadcast([P, G, D]), ALU.add).then_inc(biased, 1)
                    reuse(v, stored[h], loads(i - 2, h))
                    v.wait_ge(biased, i + 1)
                    v.scalar_tensor_tensor(out=x_out[:, h], in0=out[:, :, :], scalar=tanh_g,
                                           in1=group_of(x_all, i), op0=ALU.mult, op1=ALU.add).then_inc(x_done, 1)

                def main(i, h, nxt):
                    def first_levels(g):
                        v.wait_ge(gate_done, g * 2 + 2)
                        reuse(v, lp_turned, (g - 1) * C)
                        tree(g, h, range(DEPTH - 2))
                    ago(i, 0, first_levels)
                    ago(i, -2, stats)
                    ago(i, 0, lambda g: tree(g, h, range(DEPTH - 2, DEPTH)))
                    ago(i, -2, lambda g: apply(g, h))
                    ago(i, 1, lambda g: output(g, 1 - h))
                over_lagging(front, main, v, 1)


def build(nc, dram):
    with ExitStack() as ctx:
        chip = Chip(nc, ctx, dram)
        constants(chip)
        l0_mix(chip)
        with ExitStack() as l0:
            y1_all = l0.enter_context(nc.sbuf_tensor("y1_all", [P, TILES, D], F32))
            logits = l0.enter_context(nc.sbuf_tensor("l0_logits", [P, TILES, L0_E], F32))
            weight = l0.enter_context(nc.sbuf_tensor("l0_weight", [P, TILES, L0_E], F32))
            ahead = Ahead(chip, l0, "l0", w1_t=[P, L0_E, L0_FF // P, D], w2=[P, L0_E, L0_FF // P, D])
            l0_attention(chip, y1_all, logits, ahead)
            w12 = l0.enter_context(nc.sbuf_tensor("l0_w12", [P, L0_E, D], F32))
            b12 = l0.enter_context(nc.sbuf_tensor("l0_b12", [L0_E, D], F32))
            l0_route(chip, logits, weight, ahead, w12, b12)
            l0_experts(chip, y1_all, weight, w12, b12)
        with ExitStack() as l1:
            ahead = Ahead(chip, l1, "l1", w1=[P, L1_E, P], w3=[P, L1_E, P], w2=[P, L1_E, D])
            l1_mix(chip, ahead)
            l1_ffn(chip, ahead)
        with ExitStack() as l2:
            ahead = Ahead(chip, l2, "l2", w1=[P, L2_E, L2_H], w2=[P, L2_E, L2_H // P, D])
            cross_attention(chip, "l2", 2, QueryKeyCaps, AddToX, ahead)
            l2_ffn(chip, ahead)
        with nc.sbuf_tensor("y_all", [P, TILES, D], F32) as y_all:
            cross_attention(chip, "l3", 3, PaddingCaps, lambda ph, c, bias: NormToY(ph, c, bias, y_all))
            l3_mlp(chip, y_all)
        l3_tree(chip)


def layouts(i):
    rows = lambda a: np.broadcast_to(np.asarray(a).reshape(1, -1), (P, np.asarray(a).size))
    cols = lambda a: np.asarray(a).reshape(-1, P).T
    halves = lambda a: np.concatenate([np.asarray(a).reshape(2, S).T] * 2)
    by_parity = lambda a: np.repeat(np.asarray(a).reshape(HEADS // 2, 2, HD).transpose(1, 0, 2).reshape(2, -1), S, axis=0)
    s = np.arange(P)
    age = s[None, :] - s[:, None]
    same = (s[None, :] // S) == (s[:, None] // S)
    out = {
        "x": i["x"].reshape(TOKENS, D),
        "ctx": i["ctx_1024"].reshape(TOKENS, D),
        "ctx_t": i["ctx_1024"].reshape(TOKENS, D).T,
        "g_xattn": rows(i["g_xattn"]),
        "g_ffn": rows(i["g_ffn"]),
        "ident": np.eye(P, dtype=np.float32),
        "later": (s[:, None] < s[None, :]).astype(np.float32),
        "l0_of_head": (s[:, None] // L0_HD == np.arange(L0_HEADS)[None, :]).astype(np.float32),
        "l0_first": rows(np.arange(L0_E, 0, -1, dtype=np.float32)),
        "l0_wqkv": i["L0_ffn_in_proj_w"].T,
        "l0_b_cols": cols(i["L0_ffn_in_proj_b"]),
        "l0_bv": rows(i["L0_ffn_in_proj_b"][2 * D:]),
        "l0_wo": i["L0_ffn_out_proj_w"].T,
        "l0_bo": rows(i["L0_ffn_out_proj_b"]),
        "l0_ln1_g": rows(i["L0_ffn_ln1_g"]),
        "l0_ln1_b": rows(i["L0_ffn_ln1_b"]),
        "l0_ln2_g": rows(i["L0_ffn_ln2_g"]),
        "l0_ln2_b": rows(i["L0_ffn_ln2_b"]),
        "l0_wg": i["L0_ffn_wg"],
        "l0_w1_t": i["L0_ffn_w1"].reshape(L0_E, D, L0_FF // P, P).transpose(3, 0, 2, 1),
        "l0_w2": i["L0_ffn_w2"].reshape(L0_E, L0_FF // P, P, D).transpose(2, 0, 1, 3),
        "l0_b1": i["L0_ffn_b1"].reshape(L0_E, L0_FF // P, P).transpose(2, 0, 1),
        "l0_b2": i["L0_ffn_b2"],
        "block_of": (s[:, None] // S == np.arange(2)[None, :]).astype(np.float32),
        "l1_w_sim": cols(i["L1_xattn_w_sim"]),
        "l1_b_sim": rows(i["L1_xattn_b_sim"]),
        "l1_wqv": i["L1_xattn_W_qv"].reshape(4, D, D).transpose(1, 0, 2),
        "l1_bqv": rows(i["L1_xattn_b_qv"]),
        "l1_wg": i["L1_ffn_Wg"].T,
        "l1_w1": i["L1_ffn_W1"].transpose(2, 0, 1),
        "l1_w3": i["L1_ffn_W3"].transpose(2, 0, 1),
        "l1_w2": i["L1_ffn_W2"].transpose(2, 0, 1),
        "l1_b1": i["L1_ffn_b1"].T,
        "l1_b3": i["L1_ffn_b3"].T,
        "l1_b2": i["L1_ffn_b2"],
        "earlier4": np.broadcast_to(np.tri(L1_GROUPS, k=-1, dtype=np.float32), (P, L1_GROUPS, L1_GROUPS)),
        "of_head": (s[:, None] % S // HD == np.arange(HEADS // 2)[None, :]).astype(np.float32),
        "l2_mask": np.concatenate([i["mask_1x1xSxS2_ik0"][0, 0]] * 2),
        "l2_wq": i["L2_xattn_w_q"].T,
        "l2_wk": i["L2_xattn_w_k"].T,
        "l2_wv": i["L2_xattn_w_v"].T,
        "l2_wo": i["L2_xattn_w_o"].T,
        "l2_bq": halves(i["L2_xattn_b_q"]),
        "l2_bk": halves(i["L2_xattn_b_k"]),
        "l2_bv": by_parity(i["L2_xattn_b_v"]),
        "l2_bo": rows(i["L2_xattn_b_o"]),
        "l2_wr": i["L2_ffn_router_w"].T,
        "l2_gamma": rows(i["L2_ffn_gamma"]),
        "l2_beta": rows(i["L2_ffn_beta"]),
        "l2_w1": i["L2_ffn_W1"].transpose(1, 0, 2),
        "l2_w2": i["L2_ffn_W2"].reshape(L2_E, L2_H // P, P, D).transpose(2, 0, 1, 3),
        "l3_mask": np.repeat(i["mask_BxS2_bf0"].reshape(TILES, 2, S).transpose(1, 0, 2), S, axis=0).reshape(P, -1),
        "l3_wq": i["L3_xattn_Wq"],
        "l3_wk": i["L3_xattn_Wk"],
        "l3_wv": i["L3_xattn_Wv"],
        "l3_wo": i["L3_xattn_Wo"],
        "l3_bq": halves(i["L3_xattn_bq"]),
        "l3_bk": halves(i["L3_xattn_bk"]),
        "l3_bv": by_parity(i["L3_xattn_bv"]),
        "l3_bo": rows(i["L3_xattn_bo"]),
        "l3_ln1_g": rows(i["L3_xattn_ln1_g"]),
        "l3_ln1_b": rows(i["L3_xattn_ln1_b"]),
        "l3_w1": i["L3_xattn_W1"],
        "l3_b1": cols(i["L3_xattn_b1"]),
        "l3_w2": i["L3_xattn_W2"].reshape(FFN // P, P, D).transpose(1, 0, 2),
        "l3_b2": rows(i["L3_xattn_b2"]),
        "l3_ln2_g": rows(i["L3_xattn_ln2_g"]),
        "l3_ln2_b": rows(i["L3_xattn_ln2_b"]),
        "l3_tq": i["L3_ffn_Wq"],
        "l3_rt": i["L3_ffn_routers"].T,
        "l3_vt": i["L3_ffn_leaf_values"].T,
        "l3_two": i["L3_ffn_Wout_w"].T,
        "l3_tbo": rows(i["L3_ffn_Wout_b"]),
        "powers": np.where((age >= 0) & same, DECAY ** np.maximum(age, 0).astype(np.float64), 0.0).astype(np.float32),
    }
    return {k: np.ascontiguousarray(v) for k, v in out.items()}


def kernel(**inputs):
    import concourse.bacc as bacc
    from concourse.bass_utils import run_bass_kernel_spmd

    arrays = {f"in_{k}": v for k, v in layouts({k: np.asarray(v) for k, v in inputs.items()}).items()}
    nc = bacc.Bacc("TRN2", target_bir_lowering=False, num_devices=1)
    dram = {k[3:]: nc.dram_tensor(k, a.shape, mybir.dt.from_np(a.dtype), kind="ExternalInput").ap()
            for k, a in arrays.items()}
    for name, shape in (("x1", (TOKENS, D)), ("y1_t", (P, TOKENS)), ("x2", (TOKENS, D))):
        dram[name] = nc.dram_tensor(f"scratch_{name}", shape, F32, kind="Internal").ap()
    dram["out"] = nc.dram_tensor("out", (TOKENS, D), F32, kind="ExternalOutput").ap()
    build(nc, dram)
    r = run_bass_kernel_spmd(nc, [arrays], core_ids=[0])
    return r.results[0]["out"].reshape(B, S, D)
```
